# Optimizing a Trainium2 kernel written in Bass

```python
import numpy as np
import jax
import jax.numpy as jnp

def _softmax(x, axis=-1):
    return jax.nn.softmax(x, axis=axis)

def _gelu(x):
    return jax.nn.gelu(x, approximate=True)

def _silu(x):
    return jax.nn.silu(x)

def _sigmoid(x):
    return jax.nn.sigmoid(x)

def _layernorm(x, axis=-1, eps=1e-05):
    m = jnp.mean(x, axis=axis, keepdims=True)
    v = jnp.var(x, axis=axis, keepdims=True)
    return (x - m) / jnp.sqrt(v + eps)

def _scatter_add(tgt, idx, src, axis=0):
    return tgt.at[idx].add(src)

def _segment_sum(src, seg, n):
    return jax.ops.segment_sum(src, seg, n)
kernel_name = 'mk_adj_ffn_d2_adj_r2_e84602'

def setup_inputs(seed: int=0):
    np.random.seed(seed)
    _w = jnp.asarray

    def _rec_inputs():
        import jax
        import jax.numpy as jnp
        _gk = jax.random.key(seed)
        x = -0.0002928 + 1 * jax.random.normal(jax.random.fold_in(_gk, 1), (32, 256, 128), jnp.float32)
        _w = (1.0 + jnp.arange(256, dtype=jnp.float32)) ** (-0.5)
        _w = _w / _w.mean()
        _pij = jnp.clip(0.03125 * _w[:, None] * _w[None, :], 0.0, 1.0)
        _a = jax.random.uniform(jax.random.fold_in(_gk, 2), (32, 256, 256)) < _pij
        _a = jnp.logical_or(_a, jnp.swapaxes(_a, -1, -2))
        _a = jnp.logical_or(_a, jnp.eye(256, dtype=bool))
        _af = _a.astype(jnp.float32)
        _af = _af * jax.random.uniform(jax.random.fold_in(_gk, 3), (32, 256, 256), jnp.float32, 0.05, 1)
        adj = _af
        return (x, adj)
    x, adj = _rec_inputs()

    def _L0_gnn_setup():
        import jax, jax.numpy as jnp
        import numpy as np
        B, N, D, H = (8, 1024, 128, 512)
        RMS_EPS = 1e-06

        def _rmsnorm(h, w, eps=RMS_EPS):
            var = jnp.mean(jnp.square(h), axis=-1, keepdims=True)
            return h * jax.lax.rsqrt(var + eps) * w
        key = jax.random.key(seed)
        ks = jax.random.split(key, 5)
        x = jax.random.normal(ks[0], (B, N, D), dtype=jnp.float32)
        adjacency = jax.random.uniform(ks[1], (B, N, N), dtype=jnp.float32)
        epsilon = jnp.zeros((), dtype=jnp.float32)
        W1 = jax.random.normal(ks[2], (D, H), dtype=jnp.float32) * (1.0 / np.sqrt(D))
        b1 = jnp.zeros((H,), dtype=jnp.float32)
        rms_weight = jnp.ones((H,), dtype=jnp.float32)
        W2 = jax.random.normal(ks[3], (H, D), dtype=jnp.float32) * (1.0 / np.sqrt(H))
        b2 = jnp.zeros((D,), dtype=jnp.float32)
        return {'x': x, 'adjacency': adjacency, 'epsilon': epsilon, 'W1': W1, 'b1': b1, 'rms_weight': rms_weight, 'W2': W2, 'b2': b2}
    _L0_gnn_all = _L0_gnn_setup()
    _L0_gnn_in = {k: v for k, v in _L0_gnn_all.items() if k in ('epsilon', 'W1', 'b1', 'rms_weight', 'W2', 'b2')}
    del _L0_gnn_all

    def _L0_ffn_setup():
        import jax, jax.numpy as jnp
        import numpy as np
        TOP_K = 2
        key = jax.random.key(seed)
        ks = jax.random.split(key, 4)
        B, L, D, H, E = (8, 2048, 128, 512, 8)
        s = 0.02
        return {'x': jax.random.normal(ks[0], (B, L, D), jnp.float32), 'Wg': jax.random.normal(ks[1], (D, E), jnp.float32) * s, 'bg': jnp.zeros((E,), jnp.float32), 'W1': jax.random.normal(ks[2], (E, D, H), jnp.float32) * s, 'b1': jnp.zeros((E, H), jnp.float32), 'W2': jax.random.normal(ks[3], (E, H, D), jnp.float32) * s, 'b2': jnp.zeros((E, D), jnp.float32)}
    _L0_ffn_all = _L0_ffn_setup()
    _L0_ffn_in = {k: v for k, v in _L0_ffn_all.items() if k in ('Wg', 'bg', 'W1', 'b1', 'W2', 'b2')}
    del _L0_ffn_all

    def _L1_gnn_setup():
        import jax, jax.numpy as jnp
        import numpy as np
        NEG_SLOPE = -0.2
        MASK_VAL = -9000000000000000.0
        key = jax.random.key(seed)
        k1, k2, k3, k4 = jax.random.split(key, 4)
        B, N, F, O = (8, 1024, 128, 128)
        x = jax.random.normal(k1, (B, N, F), dtype=jnp.float32)
        adj = jax.random.normal(k2, (B, N, N), dtype=jnp.float32)
        bw = 1.414 * np.sqrt(6.0 / (F + O))
        W_a = jax.random.uniform(k3, (F, O), minval=-bw, maxval=bw, dtype=jnp.float32)
        bb = 1.414 * np.sqrt(6.0 / (1 + O))
        bias = jax.random.uniform(k4, (1, O), minval=-bb, maxval=bb, dtype=jnp.float32)
        return {'x': x, 'adj': adj, 'W_a': W_a, 'bias': bias}
    _L1_gnn_all = _L1_gnn_setup()
    _L1_gnn_in = {k: v for k, v in _L1_gnn_all.items() if k in ('W_a', 'bias')}
    del _L1_gnn_all

    def _L1_ffn_setup():
        import jax, jax.numpy as jnp
        import numpy as np
        B, S, H, F, E, K = (8, 2048, 128, 256, 16, 2)
        EPS = 1e-05
        key = jax.random.key(seed)
        ks = jax.random.split(key, 9)
        sc = 0.02
        return {'x': jax.random.normal(ks[0], (B, S, H), dtype=jnp.float32), 'gate_w': jax.random.normal(ks[1], (H, E), dtype=jnp.float32) * sc, 'gate_b': jnp.zeros((E,), dtype=jnp.float32), 'w1': jax.random.normal(ks[2], (E, H, F), dtype=jnp.float32) * sc, 'b1': jnp.zeros((E, F), dtype=jnp.float32), 'w2': jax.random.normal(ks[3], (E, F, H), dtype=jnp.float32) * sc, 'b2': jnp.zeros((E, H), dtype=jnp.float32), 'gamma': jnp.ones((H,), dtype=jnp.float32), 'beta': jnp.zeros((H,), dtype=jnp.float32)}
    _L1_ffn_all = _L1_ffn_setup()
    _L1_ffn_in = {k: v for k, v in _L1_ffn_all.items() if k in ('gate_w', 'gate_b', 'w1', 'b1', 'w2', 'b2', 'gamma', 'beta')}
    del _L1_ffn_all
    return {'x': x, 'adj': adj, 'L0_gnn_epsilon': _L0_gnn_in['epsilon'], 'L0_gnn_W1': _L0_gnn_in['W1'], 'L0_gnn_b1': _L0_gnn_in['b1'], 'L0_gnn_rms_weight': _L0_gnn_in['rms_weight'], 'L0_gnn_W2': _L0_gnn_in['W2'], 'L0_gnn_b2': _L0_gnn_in['b2'], 'L0_ffn_Wg': _L0_ffn_in['Wg'], 'L0_ffn_bg': _L0_ffn_in['bg'], 'L0_ffn_W1': _L0_ffn_in['W1'], 'L0_ffn_b1': _L0_ffn_in['b1'], 'L0_ffn_W2': _L0_ffn_in['W2'], 'L0_ffn_b2': _L0_ffn_in['b2'], 'L1_gnn_W_a': _L1_gnn_in['W_a'], 'L1_gnn_bias': _L1_gnn_in['bias'], 'L1_ffn_gate_w': _L1_ffn_in['gate_w'], 'L1_ffn_gate_b': _L1_ffn_in['gate_b'], 'L1_ffn_w1': _L1_ffn_in['w1'], 'L1_ffn_b1': _L1_ffn_in['b1'], 'L1_ffn_w2': _L1_ffn_in['w2'], 'L1_ffn_b2': _L1_ffn_in['b2'], 'L1_ffn_gamma': _L1_ffn_in['gamma'], 'L1_ffn_beta': _L1_ffn_in['beta']}

def reference(x, adj, L0_gnn_epsilon, L0_gnn_W1, L0_gnn_b1, L0_gnn_rms_weight, L0_gnn_W2, L0_gnn_b2, L0_ffn_Wg, L0_ffn_bg, L0_ffn_W1, L0_ffn_b1, L0_ffn_W2, L0_ffn_b2, L1_gnn_W_a, L1_gnn_bias, L1_ffn_gate_w, L1_ffn_gate_b, L1_ffn_w1, L1_ffn_b1, L1_ffn_w2, L1_ffn_b2, L1_ffn_gamma, L1_ffn_beta):
    import jax
    import jax.numpy as jnp

    def _L0_gnn_ref(x, adjacency, epsilon, W1, b1, rms_weight, W2, b2):
        import jax, jax.numpy as jnp
        import numpy as np
        B, N, D, H = (8, 1024, 128, 512)
        RMS_EPS = 1e-06

        def _rmsnorm(h, w, eps=RMS_EPS):
            var = jnp.mean(jnp.square(h), axis=-1, keepdims=True)
            return h * jax.lax.rsqrt(var + eps) * w
        neighbor_sum = jnp.einsum('bnm,bmd->bnd', adjacency, x)
        agg = epsilon * x + neighbor_sum
        h = jnp.einsum('bnd,dh->bnh', agg, W1) + b1
        h = jax.nn.silu(_rmsnorm(h, rms_weight))
        out = jnp.einsum('bnh,hd->bnd', h, W2) + b2
        return out

    def _L0_ffn_ref(x, Wg, bg, W1, b1, W2, b2):
        import jax, jax.numpy as jnp
        import numpy as np
        TOP_K = 2
        B, L, D = x.shape
        E = W1.shape[0]
        xf = x.reshape(-1, D)
        gate_logits = xf @ Wg + bg
        top_w, top_i = jax.lax.top_k(gate_logits, TOP_K)
        top_w = jax.nn.softmax(top_w, axis=-1)
        w_dense = jnp.sum(jax.nn.one_hot(top_i, E, dtype=xf.dtype) * top_w[..., None], axis=1)
        out = jnp.zeros_like(xf)
        for e in range(E):
            h = jax.nn.gelu(xf @ W1[e] + b1[e], approximate=False)
            out = out + w_dense[:, e:e + 1] * (h @ W2[e] + b2[e])
        return out.reshape(B, L, D)

    def _L1_gnn_ref(x, adj, W_a, bias):
        import jax, jax.numpy as jnp
        import numpy as np
        NEG_SLOPE = -0.2
        MASK_VAL = -9000000000000000.0
        Xp = jnp.einsum('bnf,fo->bno', x, W_a)
        A = jnp.einsum('bno,bmo->bnm', Xp, Xp)
        mag = jnp.linalg.norm(A, axis=2, keepdims=True)
        A = A / (mag * jnp.swapaxes(mag, 1, 2))
        e = jnp.where(A >= 0, A, NEG_SLOPE * A)
        att = jnp.where(adj > 0, e, MASK_VAL)
        att = jax.nn.softmax(att, axis=2)
        h = jnp.einsum('bnm,bmf->bnf', att, x) + bias
        return jax.nn.elu(h)

    def _L1_ffn_ref(x, gate_w, gate_b, w1, b1, w2, b2, gamma, beta):
        import jax, jax.numpy as jnp
        import numpy as np
        B, S, H, F, E, K = (8, 2048, 128, 256, 16, 2)
        EPS = 1e-05
        gate_logits = x @ gate_w + gate_b
        topk_vals, topk_idx = jax.lax.top_k(gate_logits, K)
        topk_w = jax.nn.softmax(topk_vals, axis=-1)
        h = jax.nn.relu(jnp.einsum('bsh,ehf->bsef', x, w1) + b1)
        expert_out = jnp.einsum('bsef,efh->bseh', h, w2) + b2
        sel = jnp.take_along_axis(expert_out, topk_idx[:, :, :, None], axis=2)
        moe = jnp.sum(topk_w[..., None] * sel, axis=2)
        y = x + moe
        mu = jnp.mean(y, axis=-1, keepdims=True)
        var = jnp.var(y, axis=-1, keepdims=True)
        return (y - mu) / jnp.sqrt(var + EPS) * gamma + beta
    x = x + _L0_gnn_ref(_layernorm(x, axis=-1), adj, L0_gnn_epsilon, L0_gnn_W1, L0_gnn_b1, L0_gnn_rms_weight, L0_gnn_W2, L0_gnn_b2)
    x = x + _L0_ffn_ref(_layernorm(x, axis=-1), L0_ffn_Wg, L0_ffn_bg, L0_ffn_W1, L0_ffn_b1, L0_ffn_W2, L0_ffn_b2)
    x = x + _L1_gnn_ref(_layernorm(x, axis=-1), adj, L1_gnn_W_a, L1_gnn_bias)
    x = x + _L1_ffn_ref(_layernorm(x, axis=-1), L1_ffn_gate_w, L1_ffn_gate_b, L1_ffn_w1, L1_ffn_b1, L1_ffn_w2, L1_ffn_b2, L1_ffn_gamma, L1_ffn_beta)
    return x

_drawn_inputs = setup_inputs


def setup_inputs(seed=0):
    import zlib

    import numpy as np

    out = dict(_drawn_inputs(seed))
    spreads = {'L0_gnn_b1': (0.0, 0.1),
     'L0_gnn_rms_weight': (1.0, 0.2),
     'L0_gnn_b2': (0.0, 0.1),
     'L0_ffn_bg': (0.0, 0.1),
     'L0_ffn_b1': (0.0, 0.486),
     'L0_ffn_b2': (0.0, 0.1),
     'L1_ffn_gate_b': (0.0, 0.321),
     'L1_ffn_b1': (0.0, 0.8),
     'L1_ffn_b2': (0.0, 0.303),
     'L1_ffn_gamma': (1.0, 0.2),
     'L1_ffn_beta': (0.0, 0.1)}
    factors = {'L1_gnn_W_a': 200.0, 'L1_ffn_w1': 4.381, 'L1_ffn_w2': 3.436}
    for name, (base, spread) in spreads.items():
        noise = np.random.default_rng([zlib.crc32(name.encode()), seed]).standard_normal(out[name].shape)
        drawn = base * np.exp(spread * noise) if base else spread * noise
        out[name] = jnp.asarray(drawn.astype(out[name].dtype))
    for name, factor in factors.items():
        out[name] = (out[name] * factor).astype(out[name].dtype)
    return out
```

```python
from contextlib import ExitStack, contextmanager

import concourse.bass as bass
from concourse import mybir
from concourse.alu_op_type import AluOpType as ALU

ACT = mybir.ActivationFunctionType
F32 = mybir.dt.float32
BF16 = mybir.dt.bfloat16
I32 = mybir.dt.int32
AX_X = mybir.AxisListType.X

P = 128
D = 128
LN_EPS = 1e-5
RMS_EPS = 1e-6
MASKED = -9000000000000000.0
BIG = 3.0e38


def steps(eng, count, depth, unroll, step):
    head = -(-(depth + unroll) // unroll) * unroll
    full = count // unroll * unroll
    assert head < full
    for s in range(head):
        step(s // unroll, s % unroll)
    with eng.Fori(head // unroll, full // unroll) as i:
        for u in range(unroll):
            step(i, u)
    for s in range(full, count + depth):
        step(s // unroll, s % unroll)


class Item:

    def __init__(self, i, u, lag, unroll, count):
        self.n = i * unroll + (u - lag)
        self.round = i + (u - lag) // unroll
        self.slot = (u - lag) % unroll
        self.pair = self.slot % 2
        self.known = isinstance(i, int)
        self.alive = not self.known or 0 <= self.n < count

    def after(self, k):
        return not self.known or self.n >= k


def rows(dram, n, k):
    v = dram.rearrange("(n k p) d -> n p k d", p=P, k=k)
    return v[bass.ds(n, 1)].rearrange("a p k d -> (a p) k d")


def tiles(buf, n, k):
    return buf[:, bass.ds(n * k, k), :]


def constants(nc, sem, keep, sb, psum, c, w):
    H = 512
    HC = H // P
    c.ident = keep("ident", [P, P])
    c.ones = keep("ones", [P, P])
    c.neg_half = keep("neg_half", [P, 256])
    c.ln_eps = keep("ln_eps", [P, 2])
    c.zero_col = keep("zero_col", [P, 1])
    c.zero_i = keep("zero_i", [P, 1], I32)
    c.iota_row = keep("iota_row", [P, 256])
    c.iota_row_bf = keep("iota_row_bf", [P, 256], BF16)
    c.part_no = keep("part_no", [P, 1])
    c.before = keep("before", [P, P], BF16)
    c.ones_bf = keep("ones_bf", [P, P], BF16)
    c.a_W1w = keep("a_W1w", [P, H])
    c.a_W2 = keep("a_W2", [P, HC, D])
    c.a_b1w = keep("a_b1w", [P, HC])
    c.a_gram = keep("a_gram", [P, P])
    c.a_cross = keep("a_cross", [P, 1])
    c.a_b1sq = keep("a_b1sq", [P, 1])
    c.a_eps_ident = keep("a_eps_ident", [P, 512])
    c.a_b2 = keep("a_b2", [P, 2, D])
    W1 = sb("s_W1", [P, H])
    W1T = sb("s_W1T", [P, H])
    w_bc = sb("s_w_bc", [P, H])
    b1_bc = sb("s_b1_bc", [P, H])
    b1_col = sb("s_b1_col", [P, HC])
    w_col = sb("s_w_col", [P, HC])
    eps_bc = sb("s_eps_bc", [P, 1])
    junk = sb("s_junk", [P, H])
    cross = sb("s_cross", [P, 2])
    iota_i = sb("s_iota_i", [P, 256], I32)
    part_i = sb("s_part_i", [P, 1], I32)
    turn_ps = psum("s_turn_ps")
    gram_ps = psum("s_gram_ps")

    loaded = [sem(f"s_loaded{n}") for n in range(9)]
    pool_filled = sem("s_pool_filled")
    pool_made = sem("s_pool_made")
    turned = sem("s_turned")
    w1T_done = sem("s_w1T_done")
    gram_summed = sem("s_gram_summed")
    made = sem("s_made")

    loads = [
        (W1[:], w["L0_gnn_W1"]),
        (w_bc[:], w["L0_gnn_rms_weight"].partition_broadcast(P)),
        (b1_bc[:], w["L0_gnn_b1"].partition_broadcast(P)),
        (b1_col[:], w["L0_gnn_b1"].rearrange("(c p) -> p c", p=P)),
        (w_col[:], w["L0_gnn_rms_weight"].rearrange("(c p) -> p c", p=P)),
        (c.a_W2[:], w["L0_gnn_W2"].rearrange("(c p) d -> p c d", p=P)),
        (c.a_b2[:, 0], w["L0_gnn_b2"].partition_broadcast(P)),
        (c.a_b2[:, 1], w["L0_gnn_b2"].partition_broadcast(P)),
        (eps_bc[:], w["L0_gnn_epsilon"].partition_broadcast(P)),
    ]

    with nc.Block() as block:

        @block.sync
        def _(sp):
            for n, (dst, src) in enumerate(loads):
                sp.dma_start(dst, src, allow_slow_non_contiguous=True).then_inc(loaded[n], 16)
            for n in range(len(loads)):
                sp.wait_ge(loaded[n], 16)

        @block.gpsimd
        def _(pool):
            pool.memset(c.ident[:], 0.0)
            pool.memset(c.before[:], 1.0)
            pool.memset(c.ones[:], 1.0)
            pool.memset(c.ones_bf[:], 1.0)
            pool.memset(c.neg_half[:], -0.5)
            pool.memset(c.ln_eps[:], LN_EPS)
            pool.memset(c.zero_col[:], 0.0)
            pool.memset(c.zero_i[:], 0)
            pool.memset(c.a_eps_ident[:], 0.0)
            pool.iota(iota_i[:], [[1, 256]], base=0, channel_multiplier=0)
            pool.iota(part_i[:], [[0, 1]], base=0, channel_multiplier=1).then_inc(pool_filled, 1)
            pool.wait_ge(pool_filled, 1)
            pool.affine_select(out=c.ident[:], in_=c.ident[:], compare_op=ALU.not_equal, fill=1.0, base=0,
                               pattern=[[-1, P]], channel_multiplier=1)
            pool.affine_select(out=c.before[:], in_=c.before[:], compare_op=ALU.is_gt, fill=0.0, base=0,
                               pattern=[[1, P]], channel_multiplier=-1)
            pool.tensor_copy(c.iota_row[:], iota_i[:])
            pool.tensor_copy(c.iota_row_bf[:], iota_i[:])
            pool.tensor_copy(c.part_no[:], part_i[:]).then_inc(pool_made, 1)

        @block.tensor
        def _(pe):
            pe.wait_ge(pool_made, 1)
            pe.wait_ge(loaded[0], 16)
            for j in range(HC):
                mm = pe.transpose(turn_ps[:, P * j:P * j + P], W1[:, P * j:P * j + P], c.ident[:])
            mm.then_inc(turned, 1)
            pe.wait_ge(w1T_done, 1)
            for j in range(HC):
                mm = pe.matmul(gram_ps[:, 0:P], W1T[:, P * j:P * j + P], W1T[:, P * j:P * j + P],
                               start=(j == 0), stop=(j == HC - 1))
            mm.then_inc(gram_summed, 1)

        @block.vector
        def _(dve):
            for n in range(len(loads)):
                dve.wait_ge(loaded[n], 16)
            dve.wait_ge(pool_made, 1)
            dve.tensor_tensor(c.a_W1w[:], W1[:], w_bc[:], ALU.mult)
            dve.tensor_tensor(c.a_b1w[:], b1_col[:], w_col[:], ALU.mult)
            dve.tensor_tensor_reduce(out=junk[:], in0=W1[:], in1=b1_bc[:], scale=1.0, scalar=0.0, op0=ALU.mult,
                                     op1=ALU.add, accum_out=cross[:, 0:1]).then_inc(made, 1)
            dve.wait_ge(made, 1)
            dve.tensor_scalar(c.a_cross[:], cross[:, 0:1], 2.0, None, ALU.mult)
            dve.tensor_tensor_reduce(out=junk[:], in0=b1_bc[:], in1=b1_bc[:], scale=1.0, scalar=0.0, op0=ALU.mult,
                                     op1=ALU.add, accum_out=cross[:, 1:2]).then_inc(made, 1)
            dve.wait_ge(made, 2)
            dve.tensor_scalar(c.a_b1sq[:], cross[:, 1:2], H * RMS_EPS, None, ALU.add)
            for m in range(2):
                dve.tensor_scalar(c.a_eps_ident[:, 384 * m:384 * m + P], c.ident[:], eps_bc[:, 0:1], None, ALU.mult)
            dve.wait_ge(turned, 1)
            dve.tensor_copy(W1T[:], turn_ps[:]).then_inc(w1T_done, 1)
            dve.wait_ge(gram_summed, 1)
            dve.tensor_copy(c.a_gram[:], gram_ps[:, 0:P]).then_inc(made, 1)
            dve.wait_ge(made, 3)


def gnn_mlp_layer(nc, sem, sb, psum, c, x_dram, adj_dram, xs, B):
    H = 512
    HC = H // P
    U = 2

    adj = sb("a_adj", [P, U, 2, 256])
    stats = sb("a_stats", [P, U, 2, 6])
    meanvar = sb("a_meanvar", [P, U, 2, 2])
    var_eps = sb("a_var_eps", [P, U, 2])
    rstd = sb("a_rstd", [P, U, 2])
    xln = sb("a_xln", [P, U, 2, D])
    adjT = sb("a_adjT", [P, U, 512])
    aggT = sb("a_aggT", [P, U, 256])
    prod = sb("a_prod", [P, U, 256])
    sumsq = sb("a_sumsq", [P, U, 2])
    rms_col = sb("a_rms_col", [P, U, 2])
    rms_diag = sb("a_rms_diag", [P, U, 256])
    rms = sb("a_rms", [P, U, 256])
    hid = sb("a_hid", [P, U, HC * 256])
    act_hid = sb("a_act_hid", [P, U, HC * 256])
    x_b2 = sb("a_x_b2", [P, U, 2, D])

    adjT_ps = psum("a_adjT_ps")
    agg_ps = psum("a_agg_ps")
    ss_ps = psum("a_ss_ps")
    rms_ps = psum("a_rms_ps")
    out_ps = psum("a_out_ps")
    hid_ps = [psum(f"a_hid_ps{j}") for j in range(2)]

    x_in = [sem(f"a_x_in{i}") for i in range(U)]
    adj_in = [sem(f"a_adj_in{i}") for i in range(U)]
    stats_done = sem("a_stats_done")
    meanvar_done = sem("a_meanvar_done")
    var_eps_done = sem("a_var_eps_done")
    rstd_done = sem("a_rstd_done")
    xln_done = sem("a_xln_done")
    adj_turned = sem("a_adj_turned")
    adjT_done = sem("a_adjT_done")
    agg_summed = sem("a_agg_summed")
    aggT_done = sem("a_aggT_done")
    quad_summed = sem("a_quad_summed")
    prod_done = sem("a_prod_done")
    ss_summed = sem("a_ss_summed")
    sumsq_done = sem("a_sumsq_done")
    rms_col_done = sem("a_rms_col_done")
    rms_diag_done = sem("a_rms_diag_done")
    rms_spread = sem("a_rms_spread")
    rms_done = sem("a_rms_done")
    hid_summed = sem("a_hid_summed")
    hid_done = sem("a_hid_done")
    silu_done = sem("a_silu_done")
    out_summed = sem("a_out_summed")
    x_b2_done = sem("a_x_b2_done")
    x_done = sem("a_x_done")

    adj_rows = adj_dram.rearrange("b (h p) m -> b p h m", p=P)

    with nc.Block() as block:

        @block.sync
        def _(sp):
            def step(i, u):
                b = Item(i, u, 0, U, B)
                if not b.alive:
                    return
                if b.after(2):
                    sp.wait_ge(adj_turned, b.n - 1)
                    sp.wait_ge(xln_done, b.n - 1)
                sp.dma_start(tiles(xs, b.n, 2), rows(x_dram, b.n, 2)).then_inc(x_in[b.pair], 16)
                sp.dma_start(adj[:, b.pair], adj_rows[bass.ds(b.n, 1)].rearrange("a p h m -> (a p) h m")
                             ).then_inc(adj_in[b.pair], 16)
            steps(sp, B, 0, U, step)

        @block.gpsimd
        def _(pool):
            def step(i, u):
                b = Item(i, u, 0, U, B)
                if b.alive:
                    pool.wait_ge(meanvar_done, b.n + 1)
                    pool.tensor_tensor(var_eps[:, b.pair], meanvar[:, b.pair, :, 1], c.ln_eps[:], ALU.add
                                       ).then_inc(var_eps_done, 1)
                    if b.after(2):
                        pool.wait_ge(xln_done, b.n - 1)
                    pool.wait_ge(var_eps_done, b.n + 1)
                    pool.tensor_tensor(rstd[:, b.pair], var_eps[:, b.pair], c.neg_half[:, 0:2], ALU.pow
                                       ).then_inc(rstd_done, 1)
                a = Item(i, u, 2, U, B)
                if a.alive:
                    pool.wait_ge(sumsq_done, a.n + 1)
                    pool.tensor_tensor(rms_col[:, a.pair], sumsq[:, a.pair], c.neg_half[:, 0:2], ALU.pow
                                       ).then_inc(rms_col_done, 1)
                    pool.wait_ge(rms_col_done, a.n + 1)
                    if a.after(2):
                        pool.wait_ge(rms_spread, a.n - 1)
                    for h in range(2):
                        op = pool.tensor_tensor(rms_diag[:, a.pair, P * h:P * h + P], c.ident[:],
                                                rms_col[:, a.pair, h:h + 1].to_broadcast([P, P]), ALU.mult)
                    op.then_inc(rms_diag_done, 1)
                    if a.after(2):
                        pool.wait_ge(x_done, a.n - 1)
                    pool.tensor_tensor(x_b2[:, a.pair], tiles(xs, a.n, 2), c.a_b2[:], ALU.add
                                       ).then_inc(x_b2_done, 1)
            steps(pool, B, 2, U, step)

        @block.tensor
        def _(pe):
            def step(i, u):
                y = Item(i, u, 3, U, B)
                if y.alive:
                    pe.wait_ge(rms_diag_done, y.n + 1)
                    if y.after(1):
                        pe.wait_ge(rms_done, y.n)
                    pe.matmul(rms_ps[:, 0:256], c.ones[:], rms_diag[:, y.pair], start=True, stop=True
                              ).then_inc(rms_spread, 1)
                a = Item(i, u, 2, U, B)
                if a.alive:
                    pe.wait_ge(adjT_done, a.n + 1)
                    pe.wait_ge(xln_done, a.n + 1)
                    if a.after(1):
                        pe.wait_ge(prod_done, a.n)
                    for m in range(2):
                        mm = pe.matmul(agg_ps[:, 0:256], xln[:, a.pair, m], adjT[:, a.pair, 256 * m:256 * m + 256],
                                       start=(m == 0), stop=(m == 1))
                    mm.then_inc(agg_summed, 1)
                if y.alive:
                    for k in range(2):
                        if y.after(1):
                            pe.wait_ge(hid_done, 2 * y.n - 1 + k)
                        for j in range(2 * k, 2 * k + 2):
                            mm = pe.matmul(hid_ps[k][:, 256 * (j % 2):256 * (j % 2) + 256],
                                           c.a_W1w[:, P * j:P * j + P], aggT[:, y.pair], start=True, stop=True)
                        mm.then_inc(hid_summed, 1)
                b = Item(i, u, 1, U, B)
                if b.alive:
                    pe.wait_ge(adj_in[b.pair], (b.round + 1) * 16)
                    if b.after(1):
                        pe.wait_ge(adjT_done, b.n)
                    for m in range(2):
                        for h in range(2):
                            mm = pe.transpose(adjT_ps[:, 256 * m + P * h:256 * m + P * h + P],
                                              adj[:, b.pair, h, P * m:P * m + P], c.ident[:])
                    mm.then_inc(adj_turned, 1)
                if a.alive:
                    pe.wait_ge(aggT_done, a.n + 1)
                    pe.matmul(agg_ps[:, 256:512], c.a_gram[:], aggT[:, a.pair], start=True, stop=True
                              ).then_inc(quad_summed, 1)
                z = Item(i, u, 4, U, B)
                if z.alive:
                    pe.wait_ge(silu_done, 2 * z.n + 2)
                    if z.after(1):
                        pe.wait_ge(x_done, z.n)
                    for h in range(2):
                        for j in range(HC):
                            mm = pe.matmul(out_ps[:, P * h:P * h + P],
                                           act_hid[:, z.pair, 256 * j + P * h:256 * j + P * h + P],
                                           c.a_W2[:, j], start=(j == 0), stop=(j == HC - 1))
                    mm.then_inc(out_summed, 1)
                if a.alive:
                    pe.wait_ge(prod_done, a.n + 1)
                    if a.after(1):
                        pe.wait_ge(sumsq_done, a.n)
                    for h in range(2):
                        mm = pe.matmul(ss_ps[:, h:h + 1], prod[:, a.pair, P * h:P * h + P], c.ones[:, 0:1],
                                       start=True, stop=True)
                    mm.then_inc(ss_summed, 1)
            steps(pe, B, 4, U, step)

        @block.scalar
        def _(act):
            def step(i, u):
                y = Item(i, u, 3, U, B)
                if y.alive:
                    act.wait_ge(rms_spread, y.n + 1)
                    if y.after(2):
                        act.wait_ge(hid_done, 2 * y.n - 2)
                    act.copy(rms[:, y.pair], rms_ps[:, 0:256]).then_inc(rms_done, 1)
                a = Item(i, u, 2, U, B)
                if a.alive:
                    act.wait_ge(agg_summed, a.n + 1)
                    if a.after(2):
                        act.wait_ge(hid_summed, 2 * a.n - 2)
                        act.wait_ge(prod_done, a.n - 1)
                    act.copy(aggT[:, a.pair], agg_ps[:, 0:256]).then_inc(aggT_done, 1)
                if y.alive:
                    for k in range(2):
                        act.wait_ge(hid_done, 2 * y.n + 1 + k)
                        if y.after(2):
                            act.wait_ge(out_summed, y.n - 1)
                        act.activation(act_hid[:, y.pair, 512 * k:512 * k + 512], hid[:, y.pair, 512 * k:512 * k + 512],
                                       ACT.Silu).then_inc(silu_done, 1)
            steps(act, B, 4, U, step)

        @block.vector
        def _(dve):
            def step(i, u):
                a = Item(i, u, 2, U, B)
                y = Item(i, u, 3, U, B)
                z = Item(i, u, 4, U, B)
                if y.alive:
                    dve.wait_ge(rms_done, y.n + 1)
                    for k in range(2):
                        dve.wait_ge(hid_summed, 2 * y.n + 1 + k)
                        if y.after(2):
                            dve.wait_ge(silu_done, 2 * y.n - 3 + k)
                        for j in range(2 * k, 2 * k + 2):
                            op = dve.scalar_tensor_tensor(hid[:, y.pair, 256 * j:256 * j + 256],
                                                          hid_ps[k][:, 256 * (j % 2):256 * (j % 2) + 256],
                                                          c.a_b1w[:, j:j + 1], rms[:, y.pair], ALU.add, ALU.mult)
                        op.then_inc(hid_done, 1)
                if a.alive:
                    dve.wait_ge(quad_summed, a.n + 1)
                    if a.after(2):
                        dve.wait_ge(ss_summed, a.n - 1)
                    dve.scalar_tensor_tensor(prod[:, a.pair], agg_ps[:, 256:512], c.a_cross[:, 0:1], aggT[:, a.pair],
                                             ALU.add, ALU.mult).then_inc(prod_done, 1)
                b = Item(i, u, 1, U, B)
                if b.alive:
                    if b.after(2):
                        dve.wait_ge(agg_summed, b.n - 1)
                    dve.wait_ge(rstd_done, b.n + 1)
                    for h in range(2):
                        op = dve.tensor_scalar(xln[:, b.pair, h], tiles(xs, b.n, 2)[:, h], meanvar[:, b.pair, h, 0:1],
                                               rstd[:, b.pair, h:h + 1], ALU.subtract, ALU.mult)
                    op.then_inc(xln_done, 1)
                    dve.wait_ge(adj_turned, b.n + 1)
                    dve.tensor_tensor(adjT[:, b.pair], adjT_ps[:], c.a_eps_ident[:], ALU.add
                                      ).then_inc(adjT_done, 1)
                f = Item(i, u, 0, U, B)
                if f.alive:
                    dve.wait_ge(x_in[f.pair], (f.round + 1) * 16)
                    for h in range(2):
                        op = dve.bn_stats(stats[:, f.pair, h], tiles(xs, f.n, 2)[:, h])
                    op.then_inc(stats_done, 1)
                    dve.wait_ge(stats_done, f.n + 1)
                if a.alive:
                    dve.wait_ge(ss_summed, a.n + 1)
                    if a.after(2):
                        dve.wait_ge(rms_col_done, a.n - 1)
                    dve.tensor_scalar(sumsq[:, a.pair], ss_ps[:, 0:2], c.a_b1sq[:, 0:1], 1.0 / H, ALU.add, ALU.mult
                                      ).then_inc(sumsq_done, 1)
                if f.alive:
                    for h in range(2):
                        op = dve.bn_aggr(meanvar[:, f.pair, h], stats[:, f.pair, h])
                    op.then_inc(meanvar_done, 1)
                if z.alive:
                    dve.wait_ge(out_summed, z.n + 1)
                    dve.wait_ge(x_b2_done, z.n + 1)
                    dve.tensor_tensor(tiles(xs, z.n, 2), out_ps[:, 0:256].rearrange("p (h d) -> p h d", h=2),
                                      x_b2[:, z.pair], ALU.add).then_inc(x_done, 1)
            steps(dve, B, 4, U, step)


def expert_tiles(T, E):
    return -(-(2 * T + E) // 4) * 4


def load_experts(eng, loaded, c, w, names, E, F):
    W1, b1, W2, b2 = (w[name] for name in names)
    eng.dma_start(c.W1[:].rearrange("p (e f) -> p e f", e=E), W1.rearrange("e d f -> d e f")).then_inc(loaded[0], 16)
    eng.dma_start(c.W2[:].rearrange("p (n d) -> p n d", d=D), W2.rearrange("e (k p) d -> p (e k) d", p=P)
                  ).then_inc(loaded[1], 16)
    eng.dma_start(c.b1[:], b1.rearrange("e f -> (e f)").partition_broadcast(P)).then_inc(loaded[2], 16)
    eng.dma_start(c.b2[:, 0:E * D], b2.rearrange("e d -> (e d)").partition_broadcast(P)).then_inc(loaded[3], 16)


def gate_scores(nc, sem, sb, psum, c, w, pre, xs, xln_dram, logits, gate_w, gate_b, expert_names, B, E, F):
    U = 2
    stats = sb(pre + "stats", [P, U, 2, 6])
    meanvar = sb(pre + "meanvar", [P, U, 2, 2])
    var_eps = sb(pre + "var_eps", [P, U, 2])
    rstd = sb(pre + "rstd", [P, U, 2])
    xln = sb(pre + "xln", [P, U, 2, D])
    xT = sb(pre + "xT", [P, U, 256])
    Wg = sb(pre + "Wg", [P, E])
    bg = sb(pre + "bg", [P, 2, E])
    xT_ps = [psum(f"{pre}xT_ps{i}") for i in range(U)]
    gate_ps = [psum(f"{pre}gate_ps{i}") for i in range(U)]
    experts_in = [sem(f"{pre}experts_in{i}") for i in range(4)]
    gate_in = [sem(f"{pre}gate_in{i}") for i in range(3)]
    xln_out = [sem(f"{pre}xln_out{i}") for i in range(U)]
    stats_done = sem(pre + "stats_done")
    meanvar_done = sem(pre + "meanvar_done")
    var_eps_done = sem(pre + "var_eps_done")
    rstd_done = sem(pre + "rstd_done")
    xln_done = sem(pre + "xln_done")
    x_turned = sem(pre + "x_turned")
    xT_done = sem(pre + "xT_done")
    gate_summed = sem(pre + "gate_summed")
    gate_done = sem(pre + "gate_done")

    with nc.Block() as block:

        @block.sync
        def _(sp):
            sp.dma_start(Wg[:], gate_w).then_inc(gate_in[0], 16)
            for k in range(2):
                sp.dma_start(bg[:, k], gate_b.partition_broadcast(P)).then_inc(gate_in[1 + k], 16)
            load_experts(sp, experts_in, c, w, expert_names, E, F)

            def step(i, u):
                b = Item(i, u, 1, U, B)
                if b.alive:
                    sp.wait_ge(xln_done, b.n + 1)
                    sp.dma_start(rows(xln_dram, b.n, 2), xln[:, b.pair]).then_inc(xln_out[b.pair], 16)
            steps(sp, B, 1, U, step)
            for k in range(U):
                sp.wait_ge(xln_out[k], B // U * 16)
            for k in range(4):
                sp.wait_ge(experts_in[k], 16)

        @block.gpsimd
        def _(pool):
            def step(i, u):
                f = Item(i, u, 0, U, B)
                if f.alive:
                    pool.wait_ge(meanvar_done, f.n + 1)
                    pool.tensor_tensor(var_eps[:, f.pair], meanvar[:, f.pair, :, 1], c.ln_eps[:], ALU.add
                                       ).then_inc(var_eps_done, 1)
                    if f.after(2):
                        pool.wait_ge(xln_done, f.n - 1)
                    pool.wait_ge(var_eps_done, f.n + 1)
                    pool.tensor_tensor(rstd[:, f.pair], var_eps[:, f.pair], c.neg_half[:, 0:2], ALU.pow
                                       ).then_inc(rstd_done, 1)
            steps(pool, B, 0, U, step)

        @block.tensor
        def _(pe):
            pe.wait_ge(gate_in[0], 16)

            def step(i, u):
                a = Item(i, u, 2, U, B)
                if a.alive:
                    pe.wait_ge(xT_done, a.n + 1)
                    if a.after(2):
                        pe.wait_ge(gate_done, a.n - 1)
                    for k in range(2):
                        mm = pe.matmul(gate_ps[a.pair][:, E * k:E * k + E], xT[:, a.pair, P * k:P * k + P], Wg[:],
                                       start=True, stop=True)
                    mm.then_inc(gate_summed, 1)
                b = Item(i, u, 1, U, B)
                if b.alive:
                    pe.wait_ge(xln_done, b.n + 1)
                    if b.after(2):
                        pe.wait_ge(xT_done, b.n - 1)
                    for k in range(2):
                        mm = pe.transpose(xT_ps[b.pair][:, P * k:P * k + P], xln[:, b.pair, k], c.ident[:])
                    mm.then_inc(x_turned, 1)
            steps(pe, B, 2, U, step)

        @block.scalar
        def _(act):
            def step(i, u):
                b = Item(i, u, 1, U, B)
                if b.alive:
                    act.wait_ge(x_turned, b.n + 1)
                    if b.after(2):
                        act.wait_ge(gate_summed, b.n - 1)
                    act.copy(xT[:, b.pair], xT_ps[b.pair][:, 0:256]).then_inc(xT_done, 1)
            steps(act, B, 1, U, step)

        @block.vector
        def _(dve):
            for k in range(2):
                dve.wait_ge(gate_in[1 + k], 16)

            def step(i, u):
                f = Item(i, u, 0, U, B)
                if f.alive:
                    for k in range(2):
                        op = dve.bn_stats(stats[:, f.pair, k], tiles(xs, f.n, 2)[:, k])
                    op.then_inc(stats_done, 1)
                    dve.wait_ge(stats_done, f.n + 1)
                a = Item(i, u, 2, U, B)
                if a.alive:
                    dve.wait_ge(gate_summed, a.n + 1)
                    dve.tensor_tensor(tiles(logits, a.n, 2), gate_ps[a.pair][:, 0:2 * E].rearrange("p (k e) -> p k e", k=2),
                                      bg[:], ALU.add).then_inc(gate_done, 1)
                if f.alive:
                    for k in range(2):
                        op = dve.bn_aggr(meanvar[:, f.pair, k], stats[:, f.pair, k])
                    op.then_inc(meanvar_done, 1)
                b = Item(i, u, 1, U, B)
                if b.alive:
                    dve.wait_ge(rstd_done, b.n + 1)
                    if b.after(2):
                        dve.wait_ge(x_turned, b.n - 1)
                        dve.wait_ge(xln_out[b.pair], b.round * 16)
                    for k in range(2):
                        op = dve.tensor_scalar(xln[:, b.pair, k], tiles(xs, b.n, 2)[:, k], meanvar[:, b.pair, k, 0:1],
                                               rstd[:, b.pair, k:k + 1], ALU.subtract, ALU.mult)
                    op.then_inc(xln_done, 1)
            steps(dve, B, 2, U, step)
            dve.wait_ge(gate_done, B)


def route(nc, sem, sb, psum, c, pre, logits, r, T, E):
    NT = expert_tiles(T, E)
    TE = T * E
    NB = -(-TE // 512)
    TB = T // NB

    def work(name, shape, dt=F32):
        return sb(pre + name, shape, dt)

    best = work("best", [P, 2, T])
    hit = work("hit", [P, T, E])
    rank = work("rank", [P, T, E])
    top_rank = work("top_rank", [P, T])
    chosen = [work(f"chosen{k}", [P, T, E]) for k in range(2)]
    rest = work("rest", [P, T, E])
    order = work("order", [P, E])
    gap = work("gap", [P, T])
    gap_exp = work("gap_exp", [P, T])
    denom = work("denom", [P, T])
    taken = work("taken", [P, TE], BF16)
    count = work("count", [P, E, T])
    zeros = work("zeros", [P, TE])
    running = work("running", [P, E, T])
    start = work("start", [P, E + 1])
    total = work("total", [P, E])
    tiles_i = work("tiles_i", [P, 2, E], I32)
    n_tiles = work("n_tiles", [P, E])
    tile_end = work("tile_end", [P, E])
    shift = work("shift", [P, E])
    offset = work("offset", [P, E, T])
    place = work("place", [P, T, E])
    slot_f = work("slot_f", [P, T, 2])
    row_i = work("row_i", [P, T, 2], I32)
    tile_i = work("tile_i", [P, T, 2], I32)
    row_f = work("row_f", [P, 2 * T])
    tile_f = work("tile_f", [P, 2 * T])
    token_tile = work("token_tile", [P, T, 2])
    ended = work("ended", [P, NT, E])
    expert_f = work("expert_f", [P, NT])
    is_row = work("is_row", [P, 2, P], BF16)
    is_tile = work("is_tile", [P, 2, 2, NT], BF16)
    token_hi = work("token_hi", [P, NT])
    token_f = work("token_f", [P, NT])

    before_ps = [psum(f"{pre}before_ps{k}") for k in range(NB)]
    count_ps = [psum(f"{pre}count_ps{k}") for k in range(NB)]
    token_ps = psum(pre + "token_ps")

    chain = sem(pre + "chain")
    gap_done = sem(pre + "gap_done")
    exp_done = sem(pre + "exp_done")
    taken_done = sem(pre + "taken_done")
    counted = sem(pre + "counted")
    hot_done = sem(pre + "hot_done")
    hot_used = sem(pre + "hot_used")

    with nc.Block() as block:

        @block.scalar
        def _(act):
            act.wait_ge(gap_done, 1)
            act.activation(gap_exp[:], gap[:], ACT.Exp).then_inc(exp_done, 1)

        @block.tensor
        def _(pe):
            pe.wait_ge(taken_done, 1)
            for k in range(NB):
                pe.matmul(before_ps[k][:, 0:TB * E], c.before[:], taken[:, TB * E * k:TB * E * (k + 1)],
                          start=True, stop=True)
                mm = pe.matmul(count_ps[k][:, 0:TB * E], c.ones_bf[:], taken[:, TB * E * k:TB * E * (k + 1)],
                               start=True, stop=True)
            mm.then_inc(counted, 1)

            def step(i, u):
                a = Item(i, u, 1, 2, 2 * T)
                if a.alive:
                    pe.wait_ge(hot_done, a.n + 1)
                    pe.matmul(token_ps[:, 0:2 * NT], is_row[:, a.pair], is_tile[:, a.pair].rearrange("p a j -> p (a j)"),
                              start=a.known and a.n == 0, stop=a.known and a.n == 2 * T - 1).then_inc(hot_used, 1)
            steps(pe, 2 * T, 1, 2, step)

        @block.vector
        def _(dve):
            made = [0]

            def link(op):
                made[0] += 1
                op.then_inc(chain, 1)
                dve.wait_ge(chain, made[0])

            def over_e(v):
                return v.unsqueeze(2).to_broadcast([P, v.shape[1], E])

            def over_t(v, n):
                return v.unsqueeze(1).to_broadcast([P, n, v.shape[1]])

            dve.memset(zeros[:], 0.0)
            dve.memset(start[:, 0:1], 0.0)
            link(dve.tensor_scalar(order[:], c.iota_row[:, 0:E], -1.0, float(E), ALU.mult, ALU.add))
            left = logits
            for k in range(2):
                link(dve.tensor_reduce(best[:, k], left[:], AX_X, ALU.max))
                link(dve.tensor_tensor(hit[:], left[:], over_e(best[:, k]), ALU.is_equal))
                link(dve.tensor_tensor(rank[:], hit[:], over_t(order[:], T), ALU.mult))
                link(dve.tensor_reduce(top_rank[:], rank[:], AX_X, ALU.max))
                link(dve.tensor_tensor(chosen[k][:], rank[:], over_e(top_rank[:]), ALU.is_equal))
                if k == 0:
                    link(dve.scalar_tensor_tensor(rest[:], chosen[0][:], -BIG, logits[:], ALU.mult, ALU.add))
                    left = rest
            dve.tensor_tensor(gap[:], best[:, 1], best[:, 0], ALU.subtract).then_inc(gap_done, 1)
            dve.tensor_tensor(taken[:].rearrange("p (t e) -> p t e", e=E), chosen[0][:], chosen[1][:], ALU.add
                              ).then_inc(taken_done, 1)
            dve.wait_ge(exp_done, 1)
            link(dve.tensor_scalar(denom[:], gap_exp[:], 1.0, None, ALU.add))
            link(dve.reciprocal(r.weight[:, :, 0], denom[:]))
            dve.tensor_tensor(r.weight[:, :, 1], gap_exp[:], r.weight[:, :, 0], ALU.mult)
            dve.wait_ge(counted, 1)
            for k in range(NB):
                op = dve.tensor_copy(count[:, :, TB * k:TB * k + TB],
                                     count_ps[k][:, 0:TB * E].rearrange("p (t e) -> p e t", e=E))
            link(op)
            link(dve.tensor_tensor_scan(running[:].rearrange("p e t -> p (e t)"),
                                        count[:].rearrange("p e t -> p (e t)"), zeros[:], 0.0, ALU.add, ALU.add))
            link(dve.tensor_copy(start[:, 1:E + 1], running[:, :, T - 1]))
            link(dve.tensor_tensor(total[:], start[:, 1:E + 1], start[:, 0:E], ALU.subtract))
            link(dve.tensor_scalar(tiles_i[:, 0], total[:], float(P - 1), None, ALU.add))
            link(dve.tensor_scalar(tiles_i[:, 1], tiles_i[:, 0], 7, None, ALU.arith_shift_right))
            link(dve.tensor_copy(n_tiles[:], tiles_i[:, 1]))
            link(dve.tensor_tensor_scan(tile_end[:], n_tiles[:], zeros[:, 0:E], 0.0, ALU.add, ALU.add))
            link(dve.tensor_tensor(total[:], tile_end[:], n_tiles[:], ALU.subtract))
            link(dve.scalar_tensor_tensor(shift[:], total[:], float(P), start[:, 0:E], ALU.mult, ALU.subtract))
            link(dve.tensor_tensor(offset[:], running[:], count[:], ALU.subtract))
            link(dve.tensor_tensor(offset[:], offset[:], shift[:].unsqueeze(2).to_broadcast([P, E, T]), ALU.add))
            for k in range(NB):
                op = dve.tensor_tensor(place[:, TB * k:TB * k + TB],
                                       before_ps[k][:, 0:TB * E].rearrange("p (t e) -> p t e", e=E),
                                       offset[:, :, TB * k:TB * k + TB].rearrange("p e t -> p t e"), ALU.add)
            link(op)
            for k in range(2):
                link(dve.tensor_tensor(rank[:], place[:], chosen[k][:], ALU.mult))
                link(dve.tensor_reduce(slot_f[:, :, k], rank[:], AX_X, ALU.add))
            link(dve.tensor_copy(r.slot[:, 0:T], slot_f[:]))
            dve.tensor_scalar(row_i[:], r.slot[:, 0:T], P - 1, None, ALU.bitwise_and)
            link(dve.tensor_scalar(tile_i[:], r.slot[:, 0:T], 7, None, ALU.arith_shift_right))
            dve.tensor_copy(row_f[:], row_i[:].rearrange("p t k -> p (t k)"))
            dve.tensor_copy(tile_f[:], tile_i[:].rearrange("p t k -> p (t k)"))
            dve.memset(r.slot[:, T:T + 2], 0)
            dve.memset(r.token[:, NT:NT + 1], 0)
            dve.tensor_copy(token_tile[:], over_k(c.iota_row[:, 0:T]))
            link(dve.tensor_tensor(ended[:], over_t(tile_end[:], NT), over_e(c.iota_row[:, 0:NT]), ALU.is_le))
            link(dve.tensor_reduce(expert_f[:], ended[:], AX_X, ALU.add))
            link(dve.tensor_scalar(r.expert[:], expert_f[:], float(E - 1), None, ALU.min))

            tile_col = token_tile[:].rearrange("p t k -> p (t k)")

            def step(i, u):
                a = Item(i, u, 0, 2, 2 * T)
                if not a.alive:
                    return
                if a.after(2):
                    dve.wait_ge(hot_used, a.n - 1)
                dve.tensor_scalar(is_row[:, a.pair], c.iota_row_bf[:, 0:P], row_f[:, bass.ds(a.n, 1)], None,
                                  ALU.is_equal)
                dve.tensor_scalar(is_tile[:, a.pair, 0], c.iota_row_bf[:, 0:NT], tile_f[:, bass.ds(a.n, 1)],
                                  tile_col[:, bass.ds(a.n, 1)], ALU.is_equal, ALU.mult)
                dve.tensor_scalar(is_tile[:, a.pair, 1], c.iota_row_bf[:, 0:NT], tile_f[:, bass.ds(a.n, 1)],
                                  c.part_no[:, 0:1], ALU.is_equal, ALU.mult).then_inc(hot_done, 1)
            steps(dve, 2 * T, 0, 2, step)
            dve.wait_ge(hot_used, 2 * T)
            link(dve.tensor_copy(token_hi[:], token_ps[:, 0:NT]))
            link(dve.scalar_tensor_tensor(token_f[:], token_hi[:], float(P), token_ps[:, NT:2 * NT], ALU.mult, ALU.add))
            link(dve.tensor_copy(r.token[:, 0:NT], token_f[:]))


def over_k(v):
    return v.unsqueeze(2).to_broadcast([P, v.shape[1], 2])


def run_experts(nc, sem, sb, psum, c, pre, xln_dram, y_dram, r, T, E, F, gelu):
    U = 4
    NT = expert_tiles(T, E)
    K = F // P
    index = sb(pre + "index", [P, U], I32)
    x = sb(pre + "x", [P, U, D])
    xT = sb(pre + "xT", [P, 2, P])
    hid = sb(pre + "hid", [P, 2, F])
    act_hid = sb(pre + "act_hid", [P, 2, F]) if gelu else hid
    hidT = sb(pre + "hidT", [P, 2, F])
    y = sb(pre + "y", [P, 2, D])
    xT_ps = [psum(f"{pre}xT_ps{i}") for i in range(2)]
    hid_ps = [psum(f"{pre}hid_ps{i}") for i in range(2)]
    hidT_ps = [psum(f"{pre}hidT_ps{i}") for i in range(2)]
    y_ps = [psum(f"{pre}y_ps{i}") for i in range(2)]
    x_in = [sem(f"{pre}x_in{i}") for i in range(U)]
    y_out = [sem(f"{pre}y_out{i}") for i in range(2)]
    index_done = sem(pre + "index_done")
    x_turned = sem(pre + "x_turned")
    xT_done = sem(pre + "xT_done")
    hid_summed = sem(pre + "hid_summed")
    hid_done = sem(pre + "hid_done")
    act_done = sem(pre + "act_done") if gelu else hid_done
    hid_turned = sem(pre + "hid_turned")
    hidT_done = sem(pre + "hidT_done")
    y_summed = sem(pre + "y_summed")
    y_done = sem(pre + "y_done")

    with nc.Block() as block:

        @block.gpsimd
        def _(pool):
            pool.tensor_tensor(index[:, 0:1], r.token[:, 0:1], c.zero_i[:], ALU.add).then_inc(index_done, 1)

            def step(i, u):
                j = Item(i, u, 0, U, NT)
                if not j.alive:
                    return
                if j.after(3):
                    pool.wait_ge(x_turned, j.n - 2)
                pool.wait_ge(index_done, j.n + 1)
                nxt = (u + 1) % U
                pool.tensor_tensor(index[:, nxt:nxt + 1], r.token[:, bass.ds(j.n + 1, 1)], c.zero_i[:], ALU.add
                                   ).then_inc(index_done, 1)
                pool.indirect_dma_start(x[:, j.slot], None, xln_dram,
                                        bass.IndirectOffsetOnAxis(ap=index[:, u:u + 1], axis=0)
                                        ).then_inc(x_in[j.slot], 16)
            steps(pool, NT, 0, U, step)

        @block.tensor
        def _(pe):
            def step(i, u):
                h = Item(i, u, 2, U, NT)
                if h.alive:
                    e = pe.value_load(r.expert[0:1, bass.ds(h.n, 1)], min_val=0, max_val=E - 1)
                    pe.wait_ge(xT_done, h.n + 1)
                    if h.after(2):
                        pe.wait_ge(hid_done, h.n - 1)
                    pe.matmul(hid_ps[h.pair][:, 0:F], xT[:, h.pair], c.W1[:, bass.ds(e * F, F)], start=True, stop=True
                              ).then_inc(hid_summed, 1)
                g = Item(i, u, 3, U, NT)
                if g.alive:
                    pe.wait_ge(act_done, g.n + 1)
                    if g.after(2):
                        pe.wait_ge(hidT_done, g.n - 1)
                    for k in range(K):
                        mm = pe.transpose(hidT_ps[g.pair][:, P * k:P * k + P], act_hid[:, g.pair, P * k:P * k + P],
                                          c.ident[:])
                    mm.then_inc(hid_turned, 1)
                o = Item(i, u, 4, U, NT)
                if o.alive:
                    e = pe.value_load(r.expert[0:1, bass.ds(o.n, 1)], min_val=0, max_val=E - 1)
                    pe.wait_ge(hidT_done, o.n + 1)
                    if o.after(2):
                        pe.wait_ge(y_done, o.n - 1)
                    for k in range(K):
                        mm = pe.matmul(y_ps[o.pair][:, 0:D], hidT[:, o.pair, P * k:P * k + P],
                                       c.W2[:, bass.ds(e * (K * D) + k * D, D)], start=(k == 0), stop=(k == K - 1))
                    mm.then_inc(y_summed, 1)
                x1 = Item(i, u, 1, U, NT)
                if x1.alive:
                    pe.wait_ge(x_in[x1.slot], (x1.round + 1) * 16)
                    if x1.after(2):
                        pe.wait_ge(xT_done, x1.n - 1)
                    pe.transpose(xT_ps[x1.pair][:, 0:P], x[:, x1.slot], c.ident[:]).then_inc(x_turned, 1)
            steps(pe, NT, 4, U, step)

        @block.scalar
        def _(act):
            def step(i, u):
                g = Item(i, u, 3, U, NT)
                if g.alive:
                    act.wait_ge(hid_turned, g.n + 1)
                    if g.after(2):
                        act.wait_ge(y_summed, g.n - 1)
                    act.activation(hidT[:, g.pair], hidT_ps[g.pair][:, 0:F], ACT.Copy if gelu else ACT.Relu
                                   ).then_inc(hidT_done, 1)
                h = Item(i, u, 2, U, NT)
                if gelu and h.alive:
                    act.wait_ge(hid_done, h.n + 1)
                    if h.after(2):
                        act.wait_ge(hid_turned, h.n - 1)
                    act.activation(act_hid[:, h.pair], hid[:, h.pair], ACT.Gelu).then_inc(act_done, 1)
            steps(act, NT, 3, U, step)

        @block.vector
        def _(dve):
            def step(i, u):
                x1 = Item(i, u, 1, U, NT)
                if x1.alive:
                    dve.wait_ge(x_turned, x1.n + 1)
                    if x1.after(2):
                        dve.wait_ge(hid_summed, x1.n - 1)
                    dve.tensor_copy(xT[:, x1.pair], xT_ps[x1.pair][:, 0:P]).then_inc(xT_done, 1)
                h = Item(i, u, 2, U, NT)
                if h.alive:
                    e = dve.value_load(r.expert[0:1, bass.ds(h.n, 1)], min_val=0, max_val=E - 1)
                    dve.wait_ge(hid_summed, h.n + 1)
                    if h.after(2):
                        dve.wait_ge(act_done if gelu else hid_turned, h.n - 1)
                    dve.tensor_tensor(hid[:, h.pair], hid_ps[h.pair][:, 0:F], c.b1[:, bass.ds(e * F, F)], ALU.add
                                      ).then_inc(hid_done, 1)
                o = Item(i, u, 4, U, NT)
                if o.alive:
                    e = dve.value_load(r.expert[0:1, bass.ds(o.n, 1)], min_val=0, max_val=E - 1)
                    dve.wait_ge(y_summed, o.n + 1)
                    if o.after(2):
                        dve.wait_ge(y_out[o.pair], (i * (U // 2) + (u - 4) // 2) * 16)
                    dve.tensor_tensor(y[:, o.pair], y_ps[o.pair][:, 0:D], c.b2[:, bass.ds(e * D, D)], ALU.add
                                      ).then_inc(y_done, 1)
            steps(dve, NT, 4, U, step)

        @block.sync
        def _(sp):
            def step(i, u):
                o = Item(i, u, 4, U, NT)
                if o.alive:
                    sp.wait_ge(y_done, o.n + 1)
                    sp.dma_start(rows(y_dram, o.n, 1), y[:, o.pair].unsqueeze(1)).then_inc(y_out[o.pair], 16)
            steps(sp, NT, 4, U, step)
            for k in range(2):
                sp.wait_ge(y_out[k], NT // 2 * 16)


class Combine:

    def __init__(self, sem, sb, c, pre, r, y_dram, B):
        self.c, self.r, self.y_dram, self.B = c, r, y_dram, B
        self.index = sb(pre + "index", [P, 2, 4], I32)
        self.y = sb(pre + "y", [P, 2, 4, D])
        self.y_in = [sem(f"{pre}y_in{i}") for i in range(2)]
        self.index_done = sem(pre + "index_done")
        self.first_done = sem(pre + "first_done")
        self.x_done = sem(pre + "x_done")

    def pool_begin(self, pool):
        pool.tensor_tensor(self.index[:, 0], self.r.slot[:, 0:2].rearrange("p t k -> p (t k)"),
                           self.c.zero_i[:].to_broadcast([P, 4]), ALU.add).then_inc(self.index_done, 1)

    def pool(self, pool, i, u):
        g = Item(i, u, 0, 2, self.B)
        if not g.alive:
            return
        if g.after(2):
            pool.wait_ge(self.x_done, g.n - 1)
        if g.after(1):
            pool.wait_ge(self.y_in[1 - g.pair], (i + (u - 1) // 2 + 1) * 64)
        pool.wait_ge(self.index_done, g.n + 1)
        pool.tensor_tensor(self.index[:, 1 - g.pair].rearrange("p (t k) -> p t k", k=2), tiles(self.r.slot, g.n + 1, 2),
                           self.c.zero_i[:].unsqueeze(2).to_broadcast([P, 2, 2]), ALU.add
                           ).then_inc(self.index_done, 1)
        for n in range(4):
            pool.indirect_dma_start(self.y[:, g.pair, n], None, self.y_dram,
                                    bass.IndirectOffsetOnAxis(ap=self.index[:, g.pair, n:n + 1], axis=0)
                                    ).then_inc(self.y_in[g.pair], 16)

    def vector(self, dve, a, base, dst):
        weight = tiles(self.r.weight, a.n, 2)
        dve.wait_ge(self.y_in[a.pair], (a.round + 1) * 64)
        for t in range(2):
            op = dve.scalar_tensor_tensor(dst[:, t], self.y[:, a.pair, 2 * t], weight[:, t, 0:1], base[:, t],
                                          ALU.mult, ALU.add)
        op.then_inc(self.first_done, 1)
        dve.wait_ge(self.first_done, a.n + 1)
        for t in range(2):
            op = dve.scalar_tensor_tensor(dst[:, t], self.y[:, a.pair, 2 * t + 1], weight[:, t, 1:2], dst[:, t],
                                          ALU.mult, ALU.add)
        op.then_inc(self.x_done, 1)


def graph_attention_layer(nc, sem, sb, psum, c, w, adj_dram, xs, B, combine):
    U = 2
    NEG_SLOPE = -0.2

    adj = sb("c_adj", [P, U, 512])
    penalty = sb("c_penalty", [P, U, 512])
    stats = sb("c_stats", [P, U, 2, 6])
    meanvar = sb("c_meanvar", [P, U, 2, 2])
    var_eps = sb("c_var_eps", [P, U, 2])
    rstd = sb("c_rstd", [P, U, 2])
    xln = sb("c_xln", [P, U, 2, D])
    xln_all = sb("c_xln_all", [P, 2 * B, D])
    xT = sb("c_xT", [P, U, 256])
    xpT = sb("c_xpT", [P, U, 256])
    squares = sb("c_squares", [P, U, 512])
    sumsq = sb("c_sumsq", [P, U, 2])
    inv_mag = sb("c_inv_mag", [P, U, 2])
    mag_diag = sb("c_mag_diag", [P, U, 256])
    mag_row = sb("c_mag_row", [P, U, 256])
    score = sb("c_score", [P, U, 512])
    leaky = sb("c_leaky", [P, U, 512])
    masked = sb("c_masked", [P, U, 512])
    rowmax = sb("c_rowmax", [P, U, 2])
    neg_max = sb("c_neg_max", [P, U, 2])
    e = sb("c_e", [P, U, 512])
    eT = sb("c_eT", [P, U, 512])
    e_sum = sb("c_e_sum", [P, U, 2])
    inv_sum = sb("c_inv_sum", [P, U, 2])
    h = sb("c_h", [P, U, 256])
    h_neg = sb("c_h_neg", [P, U, 256])
    h_exp = sb("c_h_exp", [P, U, 256])
    h_elu1 = sb("c_h_elu1", [P, U, 256])
    W_a = sb("c_W_a", [P, P])
    bias = sb("c_bias", [P, D])

    xT_ps = psum("c_xT_ps")
    xpT_ps = psum("c_xpT_ps")
    A_ps = [psum(f"c_A_ps{i}") for i in range(U)]
    mag_ps = psum("c_mag_ps")
    eT_ps = psum("c_eT_ps")
    out_ps = psum("c_out_ps")

    adj_in = [sem(f"c_adj_in{i}") for i in range(U)]
    w_in = [sem(f"c_w_in{i}") for i in range(2)]
    names = ("stats_done meanvar_done var_eps_done rstd_done xln_done xln_kept x_turned xT_done xp_summed "
             "xpT_done A_summed sumsq_done inv_mag_done mag_diag_done mag_spread mag_row_done score_done leaky_done "
             "penalty_done masked_done neg_max_done exp_done e_turned eT_done inv_sum_done "
             "out_summed h_done h_neg_done h_exp_done elu1_done x_done").split()
    s = Shared()
    (s.stats_done, s.meanvar_done, s.var_eps_done, s.rstd_done, s.xln_done, s.xln_kept, s.x_turned,
     s.xT_done, s.xp_summed, s.xpT_done, s.A_summed, s.sumsq_done, s.inv_mag_done, s.mag_diag_done, s.mag_spread,
     s.mag_row_done, s.score_done, s.leaky_done, s.penalty_done, s.masked_done, s.neg_max_done,
     s.exp_done, s.e_turned, s.eT_done, s.inv_sum_done, s.out_summed, s.h_done, s.h_neg_done, s.h_exp_done,
     s.elu1_done, s.x_done) = [sem("c_" + name) for name in names]

    adj_rows = adj_dram.rearrange("b (h p) m -> b p h m", p=P)

    with nc.Block() as block:

        @block.sync
        def _(sp):
            sp.dma_start(W_a[:], w["L1_gnn_W_a"]).then_inc(w_in[0], 16)
            sp.dma_start(bias[:], w["L1_gnn_bias"].partition_broadcast(P)
                         .rearrange("p a d -> p (a d)")).then_inc(w_in[1], 16)

            def step(i, u):
                a = Item(i, u, 3, U, B)
                if a.alive:
                    if a.after(2):
                        sp.wait_ge(s.penalty_done, a.n - 1)
                    sp.dma_start(adj[:, a.pair].rearrange("p (h m) -> p h m", h=2),
                                 adj_rows[bass.ds(a.n, 1)].rearrange("a p h m -> (a p) h m")
                                 ).then_inc(adj_in[a.pair], 16)
            steps(sp, B, 3, U, step)

        @block.gpsimd
        def _(pool):
            combine.pool_begin(pool)

            def step(i, u):
                combine.pool(pool, i, u)
                b = Item(i, u, 2, U, B)
                if b.alive:
                    pool.wait_ge(s.meanvar_done, b.n + 1)
                    pool.tensor_tensor(var_eps[:, b.pair], meanvar[:, b.pair, :, 1], c.ln_eps[:], ALU.add
                                       ).then_inc(s.var_eps_done, 1)
                    if b.after(2):
                        pool.wait_ge(s.xln_done, b.n - 1)
                    pool.wait_ge(s.var_eps_done, b.n + 1)
                    pool.tensor_tensor(rstd[:, b.pair], var_eps[:, b.pair], c.neg_half[:, 0:2], ALU.pow
                                       ).then_inc(s.rstd_done, 1)
                a = Item(i, u, 3, U, B)
                if a.alive:
                    if a.after(2):
                        pool.wait_ge(s.score_done, a.n - 1)
                    pool.wait_ge(s.sumsq_done, a.n + 1)
                    pool.tensor_tensor(inv_mag[:, a.pair], sumsq[:, a.pair], c.neg_half[:, 0:2], ALU.pow
                                       ).then_inc(s.inv_mag_done, 1)
                    if a.after(2):
                        pool.wait_ge(s.mag_spread, a.n - 1)
                    pool.wait_ge(s.inv_mag_done, a.n + 1)
                    for k in range(2):
                        op = pool.tensor_tensor(mag_diag[:, a.pair, P * k:P * k + P], c.ident[:],
                                                inv_mag[:, a.pair, k:k + 1].to_broadcast([P, P]), ALU.mult)
                    op.then_inc(s.mag_diag_done, 1)
                    pool.wait_ge(s.xln_done, a.n + 1)
                    pool.tensor_copy(tiles(xln_all, a.n, 2), xln[:, a.pair]).then_inc(s.xln_kept, 1)
            steps(pool, B, 3, U, step)

        @block.tensor
        def _(pe):
            pe.wait_ge(w_in[0], 16)

            def step(i, u):
                y = Item(i, u, 4, U, B)
                if y.alive:
                    pe.wait_ge(s.mag_diag_done, y.n + 1)
                    if y.after(1):
                        pe.wait_ge(s.mag_row_done, y.n)
                    pe.matmul(mag_ps[:, 0:256], c.ones[:], mag_diag[:, y.pair], start=True, stop=True
                              ).then_inc(s.mag_spread, 1)
                a = Item(i, u, 3, U, B)
                if a.alive:
                    pe.wait_ge(s.xT_done, a.n + 1)
                    if a.after(1):
                        pe.wait_ge(s.xpT_done, a.n)
                    pe.matmul(xpT_ps[:, 0:256], W_a[:], xT[:, a.pair], start=True, stop=True).then_inc(s.xp_summed, 1)
                z = Item(i, u, 5, U, B)
                if z.alive:
                    pe.wait_ge(s.exp_done, 2 * z.n + 2)
                    if z.after(1):
                        pe.wait_ge(s.eT_done, z.n)
                    for m in range(2):
                        for k in range(2):
                            mm = pe.transpose(eT_ps[:, 256 * m + P * k:256 * m + P * k + P],
                                              e[:, z.pair, 256 * k + P * m:256 * k + P * m + P], c.ident[:])
                    mm.then_inc(s.e_turned, 1)
                if a.alive:
                    pe.wait_ge(s.xpT_done, a.n + 1)
                    if a.after(2):
                        pe.wait_ge(s.score_done, a.n - 1)
                    for k in range(2):
                        mm = pe.matmul(A_ps[a.pair][:, 256 * k:256 * k + 256], xpT[:, a.pair, P * k:P * k + P],
                                       xpT[:, a.pair], start=True, stop=True)
                    mm.then_inc(s.A_summed, 1)
                b = Item(i, u, 2, U, B)
                if b.alive:
                    pe.wait_ge(s.xln_done, b.n + 1)
                    if b.after(1):
                        pe.wait_ge(s.xT_done, b.n)
                    for k in range(2):
                        mm = pe.transpose(xT_ps[:, P * k:P * k + P], xln[:, b.pair, k], c.ident[:])
                    mm.then_inc(s.x_turned, 1)
                if z.alive:
                    pe.wait_ge(s.eT_done, z.n + 1)
                    pe.wait_ge(s.xln_kept, z.n + 1)
                    if z.after(1):
                        pe.wait_ge(s.h_done, z.n)
                    for k in range(2):
                        for m in range(2):
                            mm = pe.matmul(out_ps[:, P * k:P * k + P], eT[:, z.pair, 256 * m + P * k:256 * m + P * k + P],
                                           tiles(xln_all, z.n, 2)[:, m], start=(m == 0), stop=(m == 1))
                    mm.then_inc(s.out_summed, 1)
            steps(pe, B, 5, U, step)

        @block.scalar
        def _(act):
            def step(i, u):
                y = Item(i, u, 4, U, B)
                if y.alive:
                    act.wait_ge(s.mag_spread, y.n + 1)
                    if y.after(2):
                        act.wait_ge(s.score_done, y.n - 1)
                    act.copy(mag_row[:, y.pair], mag_ps[:, 0:256]).then_inc(s.mag_row_done, 1)
                a = Item(i, u, 3, U, B)
                if a.alive:
                    act.wait_ge(s.xp_summed, a.n + 1)
                    if a.after(2):
                        act.wait_ge(s.A_summed, a.n - 1)
                    act.copy(xpT[:, a.pair], xpT_ps[:, 0:256]).then_inc(s.xpT_done, 1)
                v = Item(i, u, 6, U, B)
                if v.alive:
                    act.wait_ge(s.h_neg_done, v.n + 1)
                    if v.after(2):
                        act.wait_ge(s.elu1_done, v.n - 1)
                    act.activation(h_exp[:, v.pair], h_neg[:, v.pair], ACT.Exp).then_inc(s.h_exp_done, 1)
                if a.alive:
                    act.wait_ge(s.A_summed, a.n + 1)
                    if a.after(2):
                        act.wait_ge(s.inv_mag_done, a.n - 1)
                    for k in range(2):
                        op = act.activation(squares[:, a.pair, 256 * k:256 * k + 256], A_ps[a.pair][:, 256 * k:256 * k + 256], ACT.Square,
                                            accum_out=sumsq[:, a.pair, k:k + 1])
                    op.then_inc(s.sumsq_done, 1)
                b = Item(i, u, 2, U, B)
                if b.alive:
                    act.wait_ge(s.x_turned, b.n + 1)
                    if b.after(2):
                        act.wait_ge(s.xp_summed, b.n - 1)
                    act.copy(xT[:, b.pair], xT_ps[:, 0:256]).then_inc(s.xT_done, 1)
                if y.alive:
                    act.wait_ge(s.neg_max_done, y.n + 1)
                    if y.after(2):
                        act.wait_ge(s.e_turned, y.n - 1)
                        act.wait_ge(s.inv_sum_done, y.n - 1)
                    for k in range(2):
                        act.activation(e[:, y.pair, 256 * k:256 * k + 256], masked[:, y.pair, 256 * k:256 * k + 256],
                                       ACT.Exp, bias=neg_max[:, y.pair, k:k + 1],
                                       accum_out=e_sum[:, y.pair, k:k + 1]).then_inc(s.exp_done, 1)
            steps(act, B, 6, U, step)

        @block.vector
        def _(dve):
            dve.wait_ge(w_in[1], 16)

            def step(i, u):
                v = Item(i, u, 6, U, B)
                z = Item(i, u, 5, U, B)
                y = Item(i, u, 4, U, B)
                q = Item(i, u, 7, U, B)
                b = Item(i, u, 2, U, B)
                f = Item(i, u, 1, U, B)
                if y.alive:
                    dve.wait_ge(s.mag_row_done, y.n + 1)
                    if y.after(2):
                        dve.wait_ge(s.leaky_done, y.n - 1)
                    for k in range(2):
                        op = dve.scalar_tensor_tensor(score[:, y.pair, 256 * k:256 * k + 256],
                                                      A_ps[y.pair][:, 256 * k:256 * k + 256],
                                                      inv_mag[:, y.pair, k:k + 1], mag_row[:, y.pair],
                                                      ALU.mult, ALU.mult)
                    op.then_inc(s.score_done, 1)
                if z.alive:
                    dve.wait_ge(s.e_turned, z.n + 1)
                    if z.after(2):
                        dve.wait_ge(s.out_summed, z.n - 1)
                    dve.tensor_copy(eT[:, z.pair], eT_ps[:]).then_inc(s.eT_done, 1)
                if y.alive:
                    dve.wait_ge(s.score_done, y.n + 1)
                    dve.scalar_tensor_tensor(leaky[:, y.pair], score[:, y.pair], NEG_SLOPE, score[:, y.pair],
                                             ALU.mult, ALU.max).then_inc(s.leaky_done, 1)
                if v.alive:
                    dve.wait_ge(s.out_summed, v.n + 1)
                    if v.after(2):
                        dve.wait_ge(s.elu1_done, v.n - 1)
                    for k in range(2):
                        op = dve.scalar_tensor_tensor(h[:, v.pair, P * k:P * k + P], out_ps[:, P * k:P * k + P],
                                                      inv_sum[:, v.pair, k:k + 1], bias[:], ALU.mult, ALU.add)
                    op.then_inc(s.h_done, 1)
                if y.alive:
                    dve.wait_ge(s.leaky_done, y.n + 1)
                    dve.wait_ge(s.penalty_done, y.n + 1)
                    if y.after(2):
                        dve.wait_ge(s.exp_done, 2 * y.n - 2)
                if v.alive:
                    dve.wait_ge(s.h_done, v.n + 1)
                    if v.after(2):
                        dve.wait_ge(s.h_exp_done, v.n - 1)
                    dve.tensor_scalar(h_neg[:, v.pair], h[:, v.pair], 0.0, None, ALU.min).then_inc(s.h_neg_done, 1)
                if y.alive:
                    for k in range(2):
                        op = dve.tensor_tensor_reduce(out=masked[:, y.pair, 256 * k:256 * k + 256],
                                                      in0=leaky[:, y.pair, 256 * k:256 * k + 256],
                                                      in1=penalty[:, y.pair, 256 * k:256 * k + 256], scale=1.0,
                                                      scalar=-BIG, op0=ALU.add, op1=ALU.max,
                                                      accum_out=rowmax[:, y.pair, k:k + 1])
                    op.then_inc(s.masked_done, 1)
                if y.alive:
                    dve.wait_ge(s.masked_done, y.n + 1)
                    dve.tensor_scalar(neg_max[:, y.pair], rowmax[:, y.pair], -1.0, None, ALU.mult
                                      ).then_inc(s.neg_max_done, 1)
                a = Item(i, u, 3, U, B)
                if a.alive:
                    dve.wait_ge(adj_in[a.pair], (a.round + 1) * 16)
                    dve.tensor_scalar(penalty[:, a.pair], adj[:, a.pair], 0.0, MASKED, ALU.is_le, ALU.mult
                                      ).then_inc(s.penalty_done, 1)
                if b.alive:
                    dve.wait_ge(s.rstd_done, b.n + 1)
                    if b.after(2):
                        dve.wait_ge(s.x_turned, b.n - 1)
                        dve.wait_ge(s.xln_kept, b.n - 1)
                    for k in range(2):
                        op = dve.tensor_scalar(xln[:, b.pair, k], tiles(xs, b.n, 2)[:, k], meanvar[:, b.pair, k, 0:1],
                                               rstd[:, b.pair, k:k + 1], ALU.subtract, ALU.mult)
                    op.then_inc(s.xln_done, 1)
                if f.alive:
                    combine.vector(dve, f, tiles(xs, f.n, 2), tiles(xs, f.n, 2))
                    dve.wait_ge(combine.x_done, f.n + 1)
                if v.alive:
                    dve.wait_ge(s.h_exp_done, v.n + 1)
                    dve.scalar_tensor_tensor(h_elu1[:, v.pair], h[:, v.pair], 0.0, h_exp[:, v.pair], ALU.max, ALU.add
                                             ).then_inc(s.elu1_done, 1)
                if f.alive:
                    for k in range(2):
                        op = dve.bn_stats(stats[:, f.pair, k], tiles(xs, f.n, 2)[:, k])
                    op.then_inc(s.stats_done, 1)
                    dve.wait_ge(s.stats_done, f.n + 1)
                if y.alive:
                    dve.wait_ge(s.exp_done, 2 * y.n + 2)
                    dve.reciprocal(inv_sum[:, y.pair], e_sum[:, y.pair]).then_inc(s.inv_sum_done, 1)
                if f.alive:
                    for k in range(2):
                        op = dve.bn_aggr(meanvar[:, f.pair, k], stats[:, f.pair, k])
                    op.then_inc(s.meanvar_done, 1)
                if v.alive:
                    dve.wait_ge(s.elu1_done, v.n + 1)
                    dve.scalar_tensor_tensor(tiles(xs, v.n, 2), h_elu1[:, v.pair].rearrange("p (k d) -> p k d", k=2),
                                             -1.0, tiles(xs, v.n, 2), ALU.add, ALU.add).then_inc(s.x_done, 1)
            steps(dve, B, 7, U, step)
            dve.wait_ge(s.x_done, B)


def last_norm(nc, sem, sb, c, w, xs, xln_dram, combine, out_dram, B):
    U = 2
    xln = sb("l_xln", [P, U, 2, D])
    moe = sb("l_moe", [P, U, 2, D])
    stats = sb("l_stats", [P, U, 2, 6])
    meanvar = sb("l_meanvar", [P, U, 2, 2])
    var_eps = sb("l_var_eps", [P, U, 2])
    rstd = sb("l_rstd", [P, U, 2])
    normed = sb("l_normed", [P, U, 2, D])
    scaled = sb("l_scaled", [P, U, 2, D])
    x_beta = sb("l_x_beta", [P, U, 2, D])
    result = sb("l_result", [P, U, 2, D])
    gamma = sb("l_gamma", [P, 2, D])
    beta = sb("l_beta", [P, 2, D])
    w_in = [sem(f"l_w_in{k}") for k in range(4)]
    xln_in = [sem(f"l_xln_in{k}") for k in range(U)]
    out_stored = [sem(f"l_out_stored{k}") for k in range(U)]
    stats_done = sem("l_stats_done")
    meanvar_done = sem("l_meanvar_done")
    var_eps_done = sem("l_var_eps_done")
    rstd_done = sem("l_rstd_done")
    normed_done = sem("l_normed_done")
    scaled_done = sem("l_scaled_done")
    x_beta_done = sem("l_x_beta_done")
    result_done = sem("l_result_done")

    with nc.Block() as block:

        @block.sync
        def _(sp):
            for k in range(2):
                sp.dma_start(gamma[:, k], w["L1_ffn_gamma"].partition_broadcast(P)).then_inc(w_in[k], 16)
                sp.dma_start(beta[:, k], w["L1_ffn_beta"].partition_broadcast(P)).then_inc(w_in[2 + k], 16)

            def step(i, u):
                g = Item(i, u, 0, U, B)
                if g.alive:
                    if g.after(2):
                        sp.wait_ge(combine.x_done, g.n - 1)
                    sp.dma_start(xln[:, g.pair], rows(xln_dram, g.n, 2)).then_inc(xln_in[g.pair], 16)
                o = Item(i, u, 4, U, B)
                if o.alive:
                    sp.wait_ge(result_done, o.n + 1)
                    sp.dma_start(rows(out_dram, o.n, 2), result[:, o.pair]).then_inc(out_stored[o.pair], 16)
            steps(sp, B, 4, U, step)
            for k in range(U):
                sp.wait_ge(out_stored[k], B // U * 16)

        @block.gpsimd
        def _(pool):
            combine.pool_begin(pool)
            for k in range(4):
                pool.wait_ge(w_in[k], 16)

            def step(i, u):
                combine.pool(pool, i, u)
                f = Item(i, u, 1, U, B)
                if f.alive:
                    pool.wait_ge(meanvar_done, f.n + 1)
                    pool.tensor_tensor(var_eps[:, f.pair], meanvar[:, f.pair, :, 1], c.ln_eps[:], ALU.add
                                       ).then_inc(var_eps_done, 1)
                    if f.after(2):
                        pool.wait_ge(normed_done, f.n - 1)
                    pool.wait_ge(var_eps_done, f.n + 1)
                    pool.tensor_tensor(rstd[:, f.pair], var_eps[:, f.pair], c.neg_half[:, 0:2], ALU.pow
                                       ).then_inc(rstd_done, 1)
                a = Item(i, u, 3, U, B)
                if a.alive:
                    pool.wait_ge(normed_done, a.n + 1)
                    if a.after(2):
                        pool.wait_ge(result_done, a.n - 1)
                    pool.tensor_tensor(scaled[:, a.pair], normed[:, a.pair], gamma[:], ALU.mult).then_inc(scaled_done, 1)
                    pool.tensor_tensor(x_beta[:, a.pair], tiles(xs, a.n, 2), beta[:], ALU.add).then_inc(x_beta_done, 1)
            steps(pool, B, 3, U, step)

        @block.vector
        def _(dve):
            def step(i, u):
                f = Item(i, u, 1, U, B)
                if f.alive:
                    dve.wait_ge(xln_in[f.pair], (f.round + 1) * 16)
                    if f.after(2):
                        dve.wait_ge(normed_done, f.n - 1)
                    combine.vector(dve, f, xln[:, f.pair], moe[:, f.pair])
                    dve.wait_ge(combine.x_done, f.n + 1)
                    for k in range(2):
                        op = dve.bn_stats(stats[:, f.pair, k], moe[:, f.pair, k])
                    op.then_inc(stats_done, 1)
                    dve.wait_ge(stats_done, f.n + 1)
                o = Item(i, u, 4, U, B)
                if o.alive:
                    dve.wait_ge(scaled_done, o.n + 1)
                    dve.wait_ge(x_beta_done, o.n + 1)
                    if o.after(2):
                        dve.wait_ge(out_stored[o.pair], o.round * 16)
                    dve.tensor_tensor(result[:, o.pair], scaled[:, o.pair], x_beta[:, o.pair], ALU.add
                                      ).then_inc(result_done, 1)
                if f.alive:
                    for k in range(2):
                        op = dve.bn_aggr(meanvar[:, f.pair, k], stats[:, f.pair, k])
                    op.then_inc(meanvar_done, 1)
                b = Item(i, u, 2, U, B)
                if b.alive:
                    dve.wait_ge(rstd_done, b.n + 1)
                    if b.after(2):
                        dve.wait_ge(scaled_done, b.n - 1)
                    for k in range(2):
                        op = dve.tensor_scalar(normed[:, b.pair, k], moe[:, b.pair, k], meanvar[:, b.pair, k, 0:1],
                                               rstd[:, b.pair, k:k + 1], ALU.subtract, ALU.mult)
                    op.then_inc(normed_done, 1)
            steps(dve, B, 4, U, step)


@contextmanager
def phase(nc):
    with ExitStack() as own:
        sems = []

        def sem(name):
            sems.append(nc.alloc_semaphore(name=name))
            return sems[-1]

        def sb(name, shape, dt=F32):
            return own.enter_context(nc.sbuf_tensor(name, shape, dt))

        def psum(name):
            return own.enter_context(nc.psum_tensor(name, [P, 512], F32))

        yield sem, sb, psum
    nc.clear_and_free_semaphores(sems)
    nc.all_engine_barrier()


class Shared:
    pass


def program(nc, w, out, scratch):
    B, N, _ = w["x"].shape
    x_dram = w["x"].rearrange("b n d -> (b n) d")
    out_dram = out.rearrange("b n d -> (b n) d")
    T = B * N // P
    c = Shared()
    with ExitStack() as ctx:
        def keep(name, shape, dt=F32):
            return ctx.enter_context(nc.sbuf_tensor(name, shape, dt))

        xs = keep("xs", [P, T, D])
        c.W1 = keep("experts_W1", [P, 4096])
        c.W2 = keep("experts_W2", [P, 4096])
        c.b1 = keep("experts_b1", [P, 4096])
        c.b2 = keep("experts_b2", [P, 2048])
        with phase(nc) as (sem, sb, psum):
            constants(nc, sem, keep, sb, psum, c, w)
        with phase(nc) as (sem, sb, psum):
            gnn_mlp_layer(nc, sem, sb, psum, c, x_dram, w["adj"], xs, B)

        def experts(pre, names, gelu):
            gate_w, gate_b, *expert_names = names
            E = w[gate_w].shape[1]
            F = w[expert_names[0]].shape[2]
            NT = expert_tiles(T, E)
            r = Shared()
            r.weight = keep(pre + "weight", [P, T, 2])
            r.slot = keep(pre + "slot", [P, T + 2, 2], I32)
            r.expert = keep(pre + "expert", [P, NT], I32)
            r.token = keep(pre + "token", [P, NT + 1], I32)
            with ExitStack() as own:
                logits = own.enter_context(nc.sbuf_tensor(pre + "logits", [P, T, E], F32))
                with phase(nc) as (sem, sb, psum):
                    gate_scores(nc, sem, sb, psum, c, w, pre + "g_", xs, scratch["xln"], logits, w[gate_w], w[gate_b],
                                expert_names, B, E, F)
                with phase(nc) as (sem, sb, psum):
                    route(nc, sem, sb, psum, c, pre + "r_", logits, r, T, E)
            with phase(nc) as (sem, sb, psum):
                run_experts(nc, sem, sb, psum, c, pre + "e_", scratch["xln"], scratch[pre + "y"], r, T, E, F,
                            gelu)
            return r

        r = experts("b_", ["L0_ffn_Wg", "L0_ffn_bg", "L0_ffn_W1", "L0_ffn_b1", "L0_ffn_W2", "L0_ffn_b2"], True)
        with phase(nc) as (sem, sb, psum):
            combine = Combine(sem, sb, c, "cc_", r, scratch["b_y"], B)
            graph_attention_layer(nc, sem, sb, psum, c, w, w["adj"], xs, B, combine)
        r = experts("d_", ["L1_ffn_gate_w", "L1_ffn_gate_b", "L1_ffn_w1", "L1_ffn_b1", "L1_ffn_w2", "L1_ffn_b2"], False)
        with phase(nc) as (sem, sb, psum):
            combine = Combine(sem, sb, c, "lc_", r, scratch["d_y"], B)
            last_norm(nc, sem, sb, c, w, xs, scratch["xln"], combine, out_dram, B)


_INS = ["x", "adj", "L0_gnn_epsilon", "L0_gnn_W1", "L0_gnn_b1", "L0_gnn_rms_weight", "L0_gnn_W2", "L0_gnn_b2",
        "L0_ffn_Wg", "L0_ffn_bg", "L0_ffn_W1", "L0_ffn_b1", "L0_ffn_W2", "L0_ffn_b2", "L1_gnn_W_a", "L1_gnn_bias",
        "L1_ffn_gate_w", "L1_ffn_gate_b", "L1_ffn_w1", "L1_ffn_b1", "L1_ffn_w2", "L1_ffn_b2", "L1_ffn_gamma",
        "L1_ffn_beta"]


def kernel(**inputs):
    import numpy as _np
    import concourse.bacc as _bacc
    from concourse.bass_utils import run_bass_kernel_spmd as _run

    nc = _bacc.Bacc("TRN2", target_bir_lowering=False, num_devices=1)
    arrays, args = {}, {}
    for name in _INS:
        a = _np.ascontiguousarray(inputs[name])
        if name == "L0_gnn_epsilon":
            a = a.reshape(1)
        arrays[f"in_{name}"] = a
        args[name] = nc.dram_tensor(f"in_{name}", a.shape, mybir.dt.from_np(a.dtype), kind="ExternalInput").ap()
    out = nc.dram_tensor("out_x", inputs["x"].shape, F32, kind="ExternalOutput").ap()
    tokens = inputs["x"].shape[0] * inputs["x"].shape[1]
    scratch = {"xln": nc.dram_tensor("xln_rows", [tokens, D], F32).ap()}
    for layer, gate in (("b_", "L0_ffn_Wg"), ("d_", "L1_ffn_gate_w")):
        slots = expert_tiles(tokens // P, inputs[gate].shape[1]) * P
        scratch[layer + "y"] = nc.dram_tensor(layer + "y_rows", [slots, D], F32).ap()
    program(nc, args, out, scratch)
    r = _run(nc, [arrays], core_ids=[0])
    return r.results[0]["out_x"]
```

```python
from contextlib import ExitStack, contextmanager

import concourse.bass as bass
from concourse import mybir
from concourse.alu_op_type import AluOpType as ALU

ACT = mybir.ActivationFunctionType
F32 = mybir.dt.float32
BF16 = mybir.dt.bfloat16
I32 = mybir.dt.int32
AX_X = mybir.AxisListType.X

P = 128
D = 128
LN_EPS = 1e-5
RMS_EPS = 1e-6
MASKED = -9000000000000000.0
BIG = 3.0e38


def steps(eng, count, depth, unroll, step):
    head = -(-(depth + unroll) // unroll) * unroll
    full = count // unroll * unroll
    assert head < full
    for s in range(head):
        step(s // unroll, s % unroll)
    with eng.Fori(head // unroll, full // unroll) as i:
        for u in range(unroll):
            step(i, u)
    for s in range(full, count + depth):
        step(s // unroll, s % unroll)


class Item:

    def __init__(self, i, u, lag, unroll, count):
        self.n = i * unroll + (u - lag)
        self.round = i + (u - lag) // unroll
        self.slot = (u - lag) % unroll
        self.pair = self.slot % 2
        self.known = isinstance(i, int)
        self.alive = not self.known or 0 <= self.n < count

    def after(self, k):
        return not self.known or self.n >= k


def rows(dram, n, k):
    v = dram.rearrange("(n k p) d -> n p k d", p=P, k=k)
    return v[bass.ds(n, 1)].rearrange("a p k d -> (a p) k d")


def tiles(buf, n, k):
    return buf[:, bass.ds(n * k, k), :]


def constants(nc, sem, keep, sb, psum, c, w):
    H = 512
    HC = H // P
    c.ident = keep("ident", [P, P])
    c.ones = keep("ones", [P, P])
    c.neg_half = keep("neg_half", [P, 256])
    c.ln_eps = keep("ln_eps", [P, 2])
    c.zero_col = keep("zero_col", [P, 1])
    c.zero_i = keep("zero_i", [P, 1], I32)
    c.iota_row = keep("iota_row", [P, 256])
    c.iota_row_bf = keep("iota_row_bf", [P, 256], BF16)
    c.part_no = keep("part_no", [P, 1])
    c.before = keep("before", [P, P], BF16)
    c.ones_bf = keep("ones_bf", [P, P], BF16)
    c.a_W1w = keep("a_W1w", [P, H])
    c.a_W2 = keep("a_W2", [P, HC, D])
    c.a_b1w = keep("a_b1w", [P, HC])
    c.a_gram = keep("a_gram", [P, P])
    c.a_cross = keep("a_cross", [P, 1])
    c.a_b1sq = keep("a_b1sq", [P, 1])
    c.a_eps_ident = keep("a_eps_ident", [P, 512])
    c.a_b2 = keep("a_b2", [P, 2, D])
    W1 = sb("s_W1", [P, H])
    W1T = sb("s_W1T", [P, H])
    w_bc = sb("s_w_bc", [P, H])
    b1_bc = sb("s_b1_bc", [P, H])
    b1_col = sb("s_b1_col", [P, HC])
    w_col = sb("s_w_col", [P, HC])
    eps_bc = sb("s_eps_bc", [P, 1])
    junk = sb("s_junk", [P, H])
    cross = sb("s_cross", [P, 2])
    iota_i = sb("s_iota_i", [P, 256], I32)
    part_i = sb("s_part_i", [P, 1], I32)
    turn_ps = psum("s_turn_ps")
    gram_ps = psum("s_gram_ps")

    loaded = [sem(f"s_loaded{n}") for n in range(9)]
    pool_filled = sem("s_pool_filled")
    pool_made = sem("s_pool_made")
    turned = sem("s_turned")
    w1T_done = sem("s_w1T_done")
    gram_summed = sem("s_gram_summed")
    made = sem("s_made")

    loads = [
        (W1[:], w["L0_gnn_W1"]),
        (w_bc[:], w["L0_gnn_rms_weight"].partition_broadcast(P)),
        (b1_bc[:], w["L0_gnn_b1"].partition_broadcast(P)),
        (b1_col[:], w["L0_gnn_b1"].rearrange("(c p) -> p c", p=P)),
        (w_col[:], w["L0_gnn_rms_weight"].rearrange("(c p) -> p c", p=P)),
        (c.a_W2[:], w["L0_gnn_W2"].rearrange("(c p) d -> p c d", p=P)),
        (c.a_b2[:, 0], w["L0_gnn_b2"].partition_broadcast(P)),
        (c.a_b2[:, 1], w["L0_gnn_b2"].partition_broadcast(P)),
        (eps_bc[:], w["L0_gnn_epsilon"].partition_broadcast(P)),
    ]

    with nc.Block() as block:

        @block.sync
        def _(sp):
            for n, (dst, src) in enumerate(loads):
                sp.dma_start(dst, src, allow_slow_non_contiguous=True).then_inc(loaded[n], 16)
            for n in range(len(loads)):
                sp.wait_ge(loaded[n], 16)

        @block.gpsimd
        def _(pool):
            pool.memset(c.ident[:], 0.0)
            pool.memset(c.before[:], 1.0)
            pool.memset(c.ones[:], 1.0)
            pool.memset(c.ones_bf[:], 1.0)
            pool.memset(c.neg_half[:], -0.5)
            pool.memset(c.ln_eps[:], LN_EPS)
            pool.memset(c.zero_col[:], 0.0)
            pool.memset(c.zero_i[:], 0)
            pool.memset(c.a_eps_ident[:], 0.0)
            pool.iota(iota_i[:], [[1, 256]], base=0, channel_multiplier=0)
            pool.iota(part_i[:], [[0, 1]], base=0, channel_multiplier=1).then_inc(pool_filled, 1)
            pool.wait_ge(pool_filled, 1)
            pool.affine_select(out=c.ident[:], in_=c.ident[:], compare_op=ALU.not_equal, fill=1.0, base=0,
                               pattern=[[-1, P]], channel_multiplier=1)
            pool.affine_select(out=c.before[:], in_=c.before[:], compare_op=ALU.is_gt, fill=0.0, base=0,
                               pattern=[[1, P]], channel_multiplier=-1)
            pool.tensor_copy(c.iota_row[:], iota_i[:])
            pool.tensor_copy(c.iota_row_bf[:], iota_i[:])
            pool.tensor_copy(c.part_no[:], part_i[:]).then_inc(pool_made, 1)

        @block.tensor
        def _(pe):
            pe.wait_ge(pool_made, 1)
            pe.wait_ge(loaded[0], 16)
            for j in range(HC):
                mm = pe.transpose(turn_ps[:, P * j:P * j + P], W1[:, P * j:P * j + P], c.ident[:])
            mm.then_inc(turned, 1)
            pe.wait_ge(w1T_done, 1)
            for j in range(HC):
                mm = pe.matmul(gram_ps[:, 0:P], W1T[:, P * j:P * j + P], W1T[:, P * j:P * j + P],
                               start=(j == 0), stop=(j == HC - 1))
            mm.then_inc(gram_summed, 1)

        @block.vector
        def _(dve):
            for n in range(len(loads)):
                dve.wait_ge(loaded[n], 16)
            dve.wait_ge(pool_made, 1)
            dve.tensor_tensor(c.a_W1w[:], W1[:], w_bc[:], ALU.mult)
            dve.tensor_tensor(c.a_b1w[:], b1_col[:], w_col[:], ALU.mult)
            dve.tensor_tensor_reduce(out=junk[:], in0=W1[:], in1=b1_bc[:], scale=1.0, scalar=0.0, op0=ALU.mult,
                                     op1=ALU.add, accum_out=cross[:, 0:1]).then_inc(made, 1)
            dve.wait_ge(made, 1)
            dve.tensor_scalar(c.a_cross[:], cross[:, 0:1], 2.0, None, ALU.mult)
            dve.tensor_tensor_reduce(out=junk[:], in0=b1_bc[:], in1=b1_bc[:], scale=1.0, scalar=0.0, op0=ALU.mult,
                                     op1=ALU.add, accum_out=cross[:, 1:2]).then_inc(made, 1)
            dve.wait_ge(made, 2)
            dve.tensor_scalar(c.a_b1sq[:], cross[:, 1:2], H * RMS_EPS, None, ALU.add)
            for m in range(2):
                dve.tensor_scalar(c.a_eps_ident[:, 384 * m:384 * m + P], c.ident[:], eps_bc[:, 0:1], None, ALU.mult)
            dve.wait_ge(turned, 1)
            dve.tensor_copy(W1T[:], turn_ps[:]).then_inc(w1T_done, 1)
            dve.wait_ge(gram_summed, 1)
            dve.tensor_copy(c.a_gram[:], gram_ps[:, 0:P]).then_inc(made, 1)
            dve.wait_ge(made, 3)


def gnn_mlp_layer(nc, sem, sb, psum, c, x_dram, adj_dram, xs, B, gate):
    H = 512
    HC = H // P
    U = 2

    adj = sb("a_adj", [P, U, 2, 256])
    stats = sb("a_stats", [P, U, 2, 6])
    meanvar = sb("a_meanvar", [P, U, 2, 2])
    var_eps = sb("a_var_eps", [P, U, 2])
    rstd = sb("a_rstd", [P, U, 2])
    xln = sb("a_xln", [P, U, 2, D])
    adjT = sb("a_adjT", [P, U, 512])
    aggT = sb("a_aggT", [P, U, 256])
    prod = sb("a_prod", [P, U, 256])
    sumsq = sb("a_sumsq", [P, U, 2])
    rms_col = sb("a_rms_col", [P, U, 2])
    rms_diag = sb("a_rms_diag", [P, U, 256])
    rms = sb("a_rms", [P, U, 256])
    hid = sb("a_hid", [P, U, HC * 256])
    act_hid = sb("a_act_hid", [P, U, HC * 256])
    x_b2 = sb("a_x_b2", [P, U, 2, D])

    adjT_ps = psum("a_adjT_ps")
    agg_ps = psum("a_agg_ps")
    ss_ps = psum("a_ss_ps")
    rms_ps = psum("a_rms_ps")
    out_ps = psum("a_out_ps")
    hid_ps = [psum(f"a_hid_ps{j}") for j in range(2)]

    x_in = [sem(f"a_x_in{i}") for i in range(U)]
    adj_in = [sem(f"a_adj_in{i}") for i in range(U)]
    stats_done = sem("a_stats_done")
    meanvar_done = sem("a_meanvar_done")
    var_eps_done = sem("a_var_eps_done")
    rstd_done = sem("a_rstd_done")
    xln_done = sem("a_xln_done")
    adj_turned = sem("a_adj_turned")
    adjT_done = sem("a_adjT_done")
    agg_summed = sem("a_agg_summed")
    aggT_done = sem("a_aggT_done")
    quad_summed = sem("a_quad_summed")
    prod_done = sem("a_prod_done")
    ss_summed = sem("a_ss_summed")
    sumsq_done = sem("a_sumsq_done")
    rms_col_done = sem("a_rms_col_done")
    rms_diag_done = sem("a_rms_diag_done")
    rms_spread = sem("a_rms_spread")
    rms_done = sem("a_rms_done")
    hid_summed = sem("a_hid_summed")
    hid_done = sem("a_hid_done")
    silu_done = sem("a_silu_done")
    out_summed = sem("a_out_summed")
    x_b2_done = sem("a_x_b2_done")
    x_done = sem("a_x_done")

    adj_rows = adj_dram.rearrange("b (h p) m -> b p h m", p=P)

    with nc.Block() as block:

        @block.sync
        def _(sp):
            def step(i, u):
                b = Item(i, u, 0, U, B)
                if b.alive:
                    if b.after(2):
                        sp.wait_ge(adj_turned, b.n - 1)
                        sp.wait_ge(xln_done, b.n - 1)
                    sp.dma_start(tiles(xs, b.n, 2), rows(x_dram, b.n, 2)).then_inc(x_in[b.pair], 16)
                    sp.dma_start(adj[:, b.pair], adj_rows[bass.ds(b.n, 1)].rearrange("a p h m -> (a p) h m")
                                 ).then_inc(adj_in[b.pair], 16)
                if b.known and b.n == 1:
                    gate.sync_begin(sp)
                gate.sync(sp, i, u)
            steps(sp, B, 6, U, step)
            gate.sync_end(sp)

        @block.gpsimd
        def _(pool):
            def step(i, u):
                b = Item(i, u, 0, U, B)
                if b.alive:
                    pool.wait_ge(meanvar_done, b.n + 1)
                    pool.tensor_tensor(var_eps[:, b.pair], meanvar[:, b.pair, :, 1], c.ln_eps[:], ALU.add
                                       ).then_inc(var_eps_done, 1)
                    if b.after(2):
                        pool.wait_ge(xln_done, b.n - 1)
                    pool.wait_ge(var_eps_done, b.n + 1)
                    pool.tensor_tensor(rstd[:, b.pair], var_eps[:, b.pair], c.neg_half[:, 0:2], ALU.pow
                                       ).then_inc(rstd_done, 1)
                a = Item(i, u, 2, U, B)
                if a.alive:
                    if a.after(2):
                        pool.wait_ge(rms_diag_done, a.n - 1)
                    pool.wait_ge(sumsq_done, a.n + 1)
                    pool.tensor_tensor(rms_col[:, a.pair], sumsq[:, a.pair], c.neg_half[:, 0:2], ALU.pow
                                       ).then_inc(rms_col_done, 1)
                if a.alive:
                    if a.after(2):
                        pool.wait_ge(x_done, a.n - 1)
                    pool.tensor_tensor(x_b2[:, a.pair], tiles(xs, a.n, 2), c.a_b2[:], ALU.add
                                       ).then_inc(x_b2_done, 1)
                gate.pool(pool, i, u)
            steps(pool, B, 5, U, step)

        @block.tensor
        def _(pe):
            gate.tensor_begin(pe)

            def step(i, u):
                y = Item(i, u, 3, U, B)
                gate.tensor_scores(pe, i, u)
                a = Item(i, u, 2, U, B)
                if a.alive:
                    pe.wait_ge(adjT_done, a.n + 1)
                    pe.wait_ge(xln_done, a.n + 1)
                    if a.after(1):
                        pe.wait_ge(prod_done, a.n)
                    for m in range(2):
                        mm = pe.matmul(agg_ps[:, 0:256], xln[:, a.pair, m], adjT[:, a.pair, 256 * m:256 * m + 256],
                                       start=(m == 0), stop=(m == 1))
                    mm.then_inc(agg_summed, 1)
                if y.alive:
                    for k in range(2):
                        if y.after(1):
                            pe.wait_ge(hid_done, 2 * y.n - 1 + k)
                        for j in range(2 * k, 2 * k + 2):
                            mm = pe.matmul(hid_ps[k][:, 256 * (j % 2):256 * (j % 2) + 256],
                                           c.a_W1w[:, P * j:P * j + P], aggT[:, y.pair], start=True, stop=True)
                        mm.then_inc(hid_summed, 1)
                b = Item(i, u, 1, U, B)
                if b.alive:
                    pe.wait_ge(adj_in[b.pair], (b.round + 1) * 16)
                    if b.after(1):
                        pe.wait_ge(adjT_done, b.n)
                    for m in range(2):
                        for h in range(2):
                            mm = pe.transpose(adjT_ps[:, 256 * m + P * h:256 * m + P * h + P],
                                              adj[:, b.pair, h, P * m:P * m + P], c.ident[:])
                    mm.then_inc(adj_turned, 1)
                if a.alive:
                    pe.wait_ge(aggT_done, a.n + 1)
                    pe.matmul(agg_ps[:, 256:512], c.a_gram[:], aggT[:, a.pair], start=True, stop=True
                              ).then_inc(quad_summed, 1)
                if y.alive:
                    pe.wait_ge(rms_diag_done, y.n + 1)
                    if y.after(1):
                        pe.wait_ge(rms_done, y.n)
                    pe.matmul(rms_ps[:, 0:256], c.ones[:], rms_diag[:, y.pair], start=True, stop=True
                              ).then_inc(rms_spread, 1)
                z = Item(i, u, 4, U, B)
                if z.alive:
                    pe.wait_ge(silu_done, 2 * z.n + 2)
                    if z.after(1):
                        pe.wait_ge(x_done, z.n)
                    for h in range(2):
                        for j in range(HC):
                            mm = pe.matmul(out_ps[:, P * h:P * h + P],
                                           act_hid[:, z.pair, 256 * j + P * h:256 * j + P * h + P],
                                           c.a_W2[:, j], start=(j == 0), stop=(j == HC - 1))
                    mm.then_inc(out_summed, 1)
                if a.alive:
                    pe.wait_ge(prod_done, a.n + 1)
                    if a.after(1):
                        pe.wait_ge(sumsq_done, a.n)
                    for h in range(2):
                        mm = pe.matmul(ss_ps[:, h:h + 1], prod[:, a.pair, P * h:P * h + P], c.ones[:, 0:1],
                                       start=True, stop=True)
                    mm.then_inc(ss_summed, 1)
                gate.tensor_turn(pe, i, u)
            steps(pe, B, 7, U, step)

        @block.scalar
        def _(act):
            def step(i, u):
                y = Item(i, u, 3, U, B)
                a = Item(i, u, 2, U, B)
                if y.alive:
                    act.wait_ge(rms_col_done, y.n + 1)
                    if y.after(2):
                        act.wait_ge(rms_spread, y.n - 1)
                    for h in range(2):
                        op = act.activation(rms_diag[:, y.pair, P * h:P * h + P], c.ident[:], ACT.Copy,
                                            scale=rms_col[:, y.pair, h:h + 1])
                    op.then_inc(rms_diag_done, 1)
                if a.alive:
                    act.wait_ge(agg_summed, a.n + 1)
                    if a.after(2):
                        act.wait_ge(hid_summed, 2 * a.n - 2)
                        act.wait_ge(prod_done, a.n - 1)
                    act.copy(aggT[:, a.pair], agg_ps[:, 0:256]).then_inc(aggT_done, 1)
                gate.scalar_norm(act, i, u)
                if y.alive:
                    act.wait_ge(rms_spread, y.n + 1)
                    if y.after(2):
                        act.wait_ge(hid_done, 2 * y.n - 2)
                    act.copy(rms[:, y.pair], rms_ps[:, 0:256]).then_inc(rms_done, 1)
                if y.alive:
                    for k in range(2):
                        act.wait_ge(hid_done, 2 * y.n + 1 + k)
                        if y.after(2):
                            act.wait_ge(out_summed, y.n - 1)
                        act.activation(act_hid[:, y.pair, 512 * k:512 * k + 512], hid[:, y.pair, 512 * k:512 * k + 512],
                                       ACT.Silu).then_inc(silu_done, 1)
                gate.scalar_copy(act, i, u)
            steps(act, B, 6, U, step)

        @block.vector
        def _(dve):
            gate.vector_begin(dve)

            def step(i, u):
                a = Item(i, u, 2, U, B)
                y = Item(i, u, 3, U, B)
                z = Item(i, u, 4, U, B)
                gate.vector_wait(dve, i, u, x_done)
                gate.vector_neg_mean(dve, i, u)
                if a.alive:
                    dve.wait_ge(quad_summed, a.n + 1)
                    if a.after(2):
                        dve.wait_ge(ss_summed, a.n - 1)
                    dve.scalar_tensor_tensor(prod[:, a.pair], agg_ps[:, 256:512], c.a_cross[:, 0:1], aggT[:, a.pair],
                                             ALU.add, ALU.mult).then_inc(prod_done, 1)
                b = Item(i, u, 1, U, B)
                if b.alive:
                    if b.after(2):
                        dve.wait_ge(agg_summed, b.n - 1)
                    dve.wait_ge(rstd_done, b.n + 1)
                    for h in range(2):
                        op = dve.tensor_scalar(xln[:, b.pair, h], tiles(xs, b.n, 2)[:, h], meanvar[:, b.pair, h, 0:1],
                                               rstd[:, b.pair, h:h + 1], ALU.subtract, ALU.mult)
                    op.then_inc(xln_done, 1)
                    dve.wait_ge(adj_turned, b.n + 1)
                    dve.tensor_tensor(adjT[:, b.pair], adjT_ps[:], c.a_eps_ident[:], ALU.add
                                      ).then_inc(adjT_done, 1)
                f = Item(i, u, 0, U, B)
                if f.alive:
                    dve.wait_ge(x_in[f.pair], (f.round + 1) * 16)
                    for h in range(2):
                        op = dve.bn_stats(stats[:, f.pair, h], tiles(xs, f.n, 2)[:, h])
                    op.then_inc(stats_done, 1)
                    dve.wait_ge(stats_done, f.n + 1)
                if y.alive:
                    dve.wait_ge(rms_done, y.n + 1)
                    for k in range(2):
                        dve.wait_ge(hid_summed, 2 * y.n + 1 + k)
                        if y.after(2):
                            dve.wait_ge(silu_done, 2 * y.n - 3 + k)
                        for j in range(2 * k, 2 * k + 2):
                            op = dve.scalar_tensor_tensor(hid[:, y.pair, 256 * j:256 * j + 256],
                                                          hid_ps[k][:, 256 * (j % 2):256 * (j % 2) + 256],
                                                          c.a_b1w[:, j:j + 1], rms[:, y.pair], ALU.add, ALU.mult)
                        op.then_inc(hid_done, 1)
                gate.vector_stats(dve, i, u)
                if a.alive:
                    dve.wait_ge(ss_summed, a.n + 1)
                    if a.after(2):
                        dve.wait_ge(rms_col_done, a.n - 1)
                    dve.tensor_scalar(sumsq[:, a.pair], ss_ps[:, 0:2], c.a_b1sq[:, 0:1], 1.0 / H, ALU.add, ALU.mult
                                      ).then_inc(sumsq_done, 1)
                if f.alive:
                    for h in range(2):
                        op = dve.bn_aggr(meanvar[:, f.pair, h], stats[:, f.pair, h])
                    op.then_inc(meanvar_done, 1)
                if z.alive:
                    dve.wait_ge(out_summed, z.n + 1)
                    dve.wait_ge(x_b2_done, z.n + 1)
                    dve.tensor_tensor(tiles(xs, z.n, 2), out_ps[:, 0:256].rearrange("p (h d) -> p h d", h=2),
                                      x_b2[:, z.pair], ALU.add).then_inc(x_done, 1)
            steps(dve, B, 7, U, step)
            gate.vector_end(dve)


def expert_tiles(T, E):
    return -(-(2 * T + E) // 8) * 8


def load_experts(eng, loaded, c, w, names, E, F):
    W1, b1, W2, b2 = (w[name] for name in names)
    eng.dma_start(c.W1[:].rearrange("p (e f) -> p e f", e=E), W1.rearrange("e d f -> d e f")).then_inc(loaded[0], 16)
    eng.dma_start(c.W2[:].rearrange("p (n d) -> p n d", d=D), W2.rearrange("e (k p) d -> p (e k) d", p=P)
                  ).then_inc(loaded[1], 16)
    eng.dma_start(c.b1[:], b1.rearrange("e f -> (e f)").partition_broadcast(P)).then_inc(loaded[2], 16)
    eng.dma_start(c.b2[:, 0:E * D], b2.rearrange("e d -> (e d)").partition_broadcast(P)).then_inc(loaded[3], 16)


class GateScores:

    def __init__(self, sem, sb, psum, c, w, pre, lag, xs, xln_dram, logits, names, B, E, F):
        self.c, self.w, self.lag, self.B, self.E, self.F = c, w, lag, B, E, F
        self.xs, self.xln_dram, self.logits, self.names = xs, xln_dram, logits, names
        self.stats = sb(pre + "stats", [P, 2, 2, 6])
        self.meanvar = sb(pre + "meanvar", [P, 2, 2, 2])
        self.var_eps = sb(pre + "var_eps", [P, 2, 2])
        self.rstd = sb(pre + "rstd", [P, 2, 2])
        self.neg_mean = sb(pre + "neg_mean", [P, 2, 2])
        self.xln = sb(pre + "xln", [P, 2, 2, D])
        self.xT = sb(pre + "xT", [P, 2, 256])
        self.Wg = sb(pre + "Wg", [P, E])
        self.bg = sb(pre + "bg", [P, 2, E])
        self.ps = psum(pre + "ps")
        self.experts_in = [sem(f"{pre}experts_in{i}") for i in range(4)]
        self.gate_in = [sem(f"{pre}gate_in{i}") for i in range(3)]
        self.xln_out = [sem(f"{pre}xln_out{i}") for i in range(2)]
        self.stats_done = sem(pre + "stats_done")
        self.meanvar_done = sem(pre + "meanvar_done")
        self.var_eps_done = sem(pre + "var_eps_done")
        self.rstd_done = sem(pre + "rstd_done")
        self.neg_mean_done = sem(pre + "neg_mean_done")
        self.xln_done = sem(pre + "xln_done")
        self.x_turned = sem(pre + "x_turned")
        self.xT_done = sem(pre + "xT_done")
        self.gate_summed = sem(pre + "gate_summed")
        self.gate_done = sem(pre + "gate_done")

    def item(self, i, u, k):
        return Item(i, u, self.lag + k, 2, self.B)

    def sync_begin(self, sp):
        gate_w, gate_b, *expert_names = self.names
        sp.dma_start(self.Wg[:], self.w[gate_w]).then_inc(self.gate_in[0], 16)
        for k in range(2):
            sp.dma_start(self.bg[:, k], self.w[gate_b].partition_broadcast(P)).then_inc(self.gate_in[1 + k], 16)
        load_experts(sp, self.experts_in, self.c, self.w, expert_names, self.E, self.F)

    def sync(self, sp, i, u):
        b = self.item(i, u, 1)
        if b.alive:
            sp.wait_ge(self.xln_done, b.n + 1)
            sp.dma_start(rows(self.xln_dram, b.n, 2), self.xln[:, b.pair]).then_inc(self.xln_out[b.pair], 16)

    def sync_end(self, sp):
        for k in range(2):
            sp.wait_ge(self.xln_out[k], self.B // 2 * 16)
        for k in range(4):
            sp.wait_ge(self.experts_in[k], 16)

    def pool(self, pool, i, u):
        f = self.item(i, u, 0)
        if f.alive:
            pool.wait_ge(self.meanvar_done, f.n + 1)
            pool.tensor_tensor(self.var_eps[:, f.pair], self.meanvar[:, f.pair, :, 1], self.c.ln_eps[:], ALU.add
                               ).then_inc(self.var_eps_done, 1)
            if f.after(2):
                pool.wait_ge(self.xln_done, f.n - 1)
            pool.wait_ge(self.var_eps_done, f.n + 1)
            pool.tensor_tensor(self.rstd[:, f.pair], self.var_eps[:, f.pair], self.c.neg_half[:, 0:2], ALU.pow
                               ).then_inc(self.rstd_done, 1)

    def tensor_begin(self, pe):
        pe.wait_ge(self.gate_in[0], 16)

    def tensor_scores(self, pe, i, u):
        a = self.item(i, u, 2)
        if a.alive:
            pe.wait_ge(self.xT_done, a.n + 1)
            for k in range(2):
                mm = pe.matmul(self.ps[:, 256 + self.E * k:256 + self.E * k + self.E],
                               self.xT[:, a.pair, P * k:P * k + P], self.Wg[:], start=True, stop=True)
            mm.then_inc(self.gate_summed, 1)

    def tensor_turn(self, pe, i, u):
        b = self.item(i, u, 1)
        if b.alive:
            pe.wait_ge(self.xln_done, b.n + 1)
            if b.after(1):
                pe.wait_ge(self.gate_done, b.n)
            for k in range(2):
                mm = pe.transpose(self.ps[:, P * k:P * k + P], self.xln[:, b.pair, k], self.c.ident[:])
            mm.then_inc(self.x_turned, 1)

    def scalar_norm(self, act, i, u):
        b = self.item(i, u, 1)
        if b.alive:
            act.wait_ge(self.neg_mean_done, b.n + 1)
            if b.after(2):
                act.wait_ge(self.x_turned, b.n - 1)
                act.wait_ge(self.xln_out[b.pair], b.round * 16)
            for k in range(2):
                op = act.activation(self.xln[:, b.pair, k], tiles(self.xs, b.n, 2)[:, k], ACT.Identity,
                                    bias=self.neg_mean[:, b.pair, k:k + 1], scale=self.rstd[:, b.pair, k:k + 1])
            op.then_inc(self.xln_done, 1)

    def scalar_copy(self, act, i, u):
        b = self.item(i, u, 1)
        if b.alive:
            act.wait_ge(self.x_turned, b.n + 1)
            if b.after(2):
                act.wait_ge(self.gate_summed, b.n - 1)
            act.copy(self.xT[:, b.pair], self.ps[:, 0:256]).then_inc(self.xT_done, 1)

    def vector_begin(self, dve):
        for k in range(2):
            dve.wait_ge(self.gate_in[1 + k], 16)

    def vector_wait(self, dve, i, u, x_done):
        f = self.item(i, u, 0)
        if f.alive:
            dve.wait_ge(x_done, f.n + 1)

    def vector_stats(self, dve, i, u):
        f = self.item(i, u, 0)
        if f.alive:
            for k in range(2):
                op = dve.bn_stats(self.stats[:, f.pair, k], tiles(self.xs, f.n, 2)[:, k])
            op.then_inc(self.stats_done, 1)
            dve.wait_ge(self.stats_done, f.n + 1)
        a = self.item(i, u, 2)
        if a.alive:
            dve.wait_ge(self.gate_summed, a.n + 1)
            dve.tensor_tensor(tiles(self.logits, a.n, 2),
                              self.ps[:, 256:256 + 2 * self.E].rearrange("p (k e) -> p k e", k=2),
                              self.bg[:], ALU.add).then_inc(self.gate_done, 1)
        if f.alive:
            for k in range(2):
                op = dve.bn_aggr(self.meanvar[:, f.pair, k], self.stats[:, f.pair, k])
            op.then_inc(self.meanvar_done, 1)

    def vector_neg_mean(self, dve, i, u):
        b = self.item(i, u, 1)
        if b.alive:
            dve.wait_ge(self.rstd_done, b.n + 1)
            if b.after(2):
                dve.wait_ge(self.xln_done, b.n - 1)
            dve.scalar_tensor_tensor(self.neg_mean[:, b.pair], self.meanvar[:, b.pair, :, 0], -1.0,
                                     self.rstd[:, b.pair], ALU.mult, ALU.mult).then_inc(self.neg_mean_done, 1)

    def vector_end(self, dve):
        dve.wait_ge(self.gate_done, self.B)


def route(nc, sem, sb, psum, c, pre, logits, r, T, E):
    NT = expert_tiles(T, E)
    TE = T * E
    NB = -(-TE // 512)
    TB = T // NB

    def work(name, shape, dt=F32):
        return sb(pre + name, shape, dt)

    best = work("best", [P, 2, T])
    hit = work("hit", [P, T, E])
    rank = work("rank", [P, T, E])
    top_rank = work("top_rank", [P, T])
    chosen = [work(f"chosen{k}", [P, T, E]) for k in range(2)]
    rest = work("rest", [P, T, E])
    order = work("order", [P, E])
    gap = work("gap", [P, T])
    gap_exp = work("gap_exp", [P, T])
    denom = work("denom", [P, T])
    taken = work("taken", [P, TE], BF16)
    count = work("count", [P, E, T])
    zeros = work("zeros", [P, TE])
    running = work("running", [P, E, T])
    start = work("start", [P, E + 1])
    total = work("total", [P, E])
    tiles_i = work("tiles_i", [P, 2, E], I32)
    n_tiles = work("n_tiles", [P, E])
    tile_end = work("tile_end", [P, E])
    shift = work("shift", [P, E])
    offset = work("offset", [P, E, T])
    place = work("place", [P, T, E])
    slot_f = work("slot_f", [P, T, 2])
    row_i = work("row_i", [P, T, 2], I32)
    tile_i = work("tile_i", [P, T, 2], I32)
    row_f = work("row_f", [P, 2 * T])
    tile_f = work("tile_f", [P, 2 * T])
    token_tile = work("token_tile", [P, T, 2])
    ended = work("ended", [P, NT, E])
    expert_f = work("expert_f", [P, NT])
    is_row = work("is_row", [P, 2, P], BF16)
    is_tile = work("is_tile", [P, 2, 2, NT], BF16)
    token_hi = work("token_hi", [P, NT])
    token_f = work("token_f", [P, NT])

    before_ps = [psum(f"{pre}before_ps{k}") for k in range(NB)]
    count_ps = [psum(f"{pre}count_ps{k}") for k in range(NB)]
    token_ps = psum(pre + "token_ps")

    chain = sem(pre + "chain")
    gap_done = sem(pre + "gap_done")
    exp_done = sem(pre + "exp_done")
    taken_done = sem(pre + "taken_done")
    counted = sem(pre + "counted")
    hot_done = sem(pre + "hot_done")
    hot_used = sem(pre + "hot_used")

    with nc.Block() as block:

        @block.scalar
        def _(act):
            act.wait_ge(gap_done, 1)
            act.activation(gap_exp[:], gap[:], ACT.Exp).then_inc(exp_done, 1)

        @block.tensor
        def _(pe):
            pe.wait_ge(taken_done, 1)
            for k in range(NB):
                pe.matmul(before_ps[k][:, 0:TB * E], c.before[:], taken[:, TB * E * k:TB * E * (k + 1)],
                          start=True, stop=True)
                mm = pe.matmul(count_ps[k][:, 0:TB * E], c.ones_bf[:], taken[:, TB * E * k:TB * E * (k + 1)],
                               start=True, stop=True)
            mm.then_inc(counted, 1)

            def step(i, u):
                a = Item(i, u, 1, 2, 2 * T)
                if a.alive:
                    pe.wait_ge(hot_done, a.n + 1)
                    pe.matmul(token_ps[:, 0:2 * NT], is_row[:, a.pair], is_tile[:, a.pair].rearrange("p a j -> p (a j)"),
                              start=a.known and a.n == 0, stop=a.known and a.n == 2 * T - 1).then_inc(hot_used, 1)
            steps(pe, 2 * T, 1, 2, step)

        @block.vector
        def _(dve):
            made = [0]

            def link(op):
                made[0] += 1
                op.then_inc(chain, 1)
                dve.wait_ge(chain, made[0])

            def over_e(v):
                return v.unsqueeze(2).to_broadcast([P, v.shape[1], E])

            def over_t(v, n):
                return v.unsqueeze(1).to_broadcast([P, n, v.shape[1]])

            dve.memset(zeros[:], 0.0)
            dve.memset(r.expert[:, 0:6], 0)
            dve.memset(r.expert[:, NT + 6:NT + 16], 0)
            dve.memset(start[:, 0:1], 0.0)
            link(dve.tensor_scalar(order[:], c.iota_row[:, 0:E], -1.0, float(E), ALU.mult, ALU.add))
            left = logits
            for k in range(2):
                link(dve.tensor_reduce(best[:, k], left[:], AX_X, ALU.max))
                link(dve.tensor_tensor(hit[:], left[:], over_e(best[:, k]), ALU.is_equal))
                link(dve.tensor_tensor(rank[:], hit[:], over_t(order[:], T), ALU.mult))
                link(dve.tensor_reduce(top_rank[:], rank[:], AX_X, ALU.max))
                link(dve.tensor_tensor(chosen[k][:], rank[:], over_e(top_rank[:]), ALU.is_equal))
                if k == 0:
                    link(dve.scalar_tensor_tensor(rest[:], chosen[0][:], -BIG, logits[:], ALU.mult, ALU.add))
                    left = rest
            dve.tensor_tensor(gap[:], best[:, 1], best[:, 0], ALU.subtract).then_inc(gap_done, 1)
            dve.tensor_tensor(taken[:].rearrange("p (t e) -> p t e", e=E), chosen[0][:], chosen[1][:], ALU.add
                              ).then_inc(taken_done, 1)
            dve.wait_ge(exp_done, 1)
            link(dve.tensor_scalar(denom[:], gap_exp[:], 1.0, None, ALU.add))
            link(dve.reciprocal(r.weight[:, :, 0], denom[:]))
            dve.tensor_tensor(r.weight[:, :, 1], gap_exp[:], r.weight[:, :, 0], ALU.mult)
            dve.wait_ge(counted, 1)
            for k in range(NB):
                op = dve.tensor_copy(count[:, :, TB * k:TB * k + TB],
                                     count_ps[k][:, 0:TB * E].rearrange("p (t e) -> p e t", e=E))
            link(op)
            link(dve.tensor_tensor_scan(running[:].rearrange("p e t -> p (e t)"),
                                        count[:].rearrange("p e t -> p (e t)"), zeros[:], 0.0, ALU.add, ALU.add))
            link(dve.tensor_copy(start[:, 1:E + 1], running[:, :, T - 1]))
            link(dve.tensor_tensor(total[:], start[:, 1:E + 1], start[:, 0:E], ALU.subtract))
            link(dve.tensor_scalar(tiles_i[:, 0], total[:], float(P - 1), None, ALU.add))
            link(dve.tensor_scalar(tiles_i[:, 1], tiles_i[:, 0], 7, None, ALU.arith_shift_right))
            link(dve.tensor_copy(n_tiles[:], tiles_i[:, 1]))
            link(dve.tensor_tensor_scan(tile_end[:], n_tiles[:], zeros[:, 0:E], 0.0, ALU.add, ALU.add))
            link(dve.tensor_tensor(total[:], tile_end[:], n_tiles[:], ALU.subtract))
            link(dve.scalar_tensor_tensor(shift[:], total[:], float(P), start[:, 0:E], ALU.mult, ALU.subtract))
            link(dve.tensor_tensor(offset[:], running[:], count[:], ALU.subtract))
            link(dve.tensor_tensor(offset[:], offset[:], shift[:].unsqueeze(2).to_broadcast([P, E, T]), ALU.add))
            for k in range(NB):
                op = dve.tensor_tensor(place[:, TB * k:TB * k + TB],
                                       before_ps[k][:, 0:TB * E].rearrange("p (t e) -> p t e", e=E),
                                       offset[:, :, TB * k:TB * k + TB].rearrange("p e t -> p t e"), ALU.add)
            link(op)
            for k in range(2):
                link(dve.tensor_tensor(rank[:], place[:], chosen[k][:], ALU.mult))
                link(dve.tensor_reduce(slot_f[:, :, k], rank[:], AX_X, ALU.add))
            link(dve.tensor_copy(r.slot[:, 0:T], slot_f[:]))
            dve.tensor_scalar(row_i[:], r.slot[:, 0:T], P - 1, None, ALU.bitwise_and)
            link(dve.tensor_scalar(tile_i[:], r.slot[:, 0:T], 7, None, ALU.arith_shift_right))
            dve.tensor_copy(row_f[:], row_i[:].rearrange("p t k -> p (t k)"))
            dve.tensor_copy(tile_f[:], tile_i[:].rearrange("p t k -> p (t k)"))
            dve.memset(r.slot[:, T:T + 2], 0)
            dve.memset(r.token[:, NT:NT + 1], 0)
            dve.tensor_copy(token_tile[:], over_k(c.iota_row[:, 0:T]))
            link(dve.tensor_tensor(ended[:], over_t(tile_end[:], NT), over_e(c.iota_row[:, 0:NT]), ALU.is_le))
            link(dve.tensor_reduce(expert_f[:], ended[:], AX_X, ALU.add))
            link(dve.tensor_scalar(r.expert[:, 6:NT + 6], expert_f[:], float(E - 1), None, ALU.min))

            tile_col = token_tile[:].rearrange("p t k -> p (t k)")

            def step(i, u):
                a = Item(i, u, 0, 2, 2 * T)
                if not a.alive:
                    return
                if a.after(2):
                    dve.wait_ge(hot_used, a.n - 1)
                dve.tensor_scalar(is_row[:, a.pair], c.iota_row_bf[:, 0:P], row_f[:, bass.ds(a.n, 1)], None,
                                  ALU.is_equal)
                dve.tensor_scalar(is_tile[:, a.pair, 0], c.iota_row_bf[:, 0:NT], tile_f[:, bass.ds(a.n, 1)],
                                  tile_col[:, bass.ds(a.n, 1)], ALU.is_equal, ALU.mult)
                dve.tensor_scalar(is_tile[:, a.pair, 1], c.iota_row_bf[:, 0:NT], tile_f[:, bass.ds(a.n, 1)],
                                  c.part_no[:, 0:1], ALU.is_equal, ALU.mult).then_inc(hot_done, 1)
            steps(dve, 2 * T, 0, 2, step)
            dve.wait_ge(hot_used, 2 * T)
            link(dve.tensor_copy(token_hi[:], token_ps[:, 0:NT]))
            link(dve.scalar_tensor_tensor(token_f[:], token_hi[:], float(P), token_ps[:, NT:2 * NT], ALU.mult, ALU.add))
            link(dve.tensor_copy(r.token[:, 0:NT], token_f[:]))


def over_k(v):
    return v.unsqueeze(2).to_broadcast([P, v.shape[1], 2])


def run_experts(nc, sem, sb, psum, c, pre, xln_dram, y_dram, r, T, E, F, gelu):
    U = 8
    NT = expert_tiles(T, E)
    K = F // P

    def load_window(engine, i):
        return nc.values_load_multi_w_load_instructions(r.expert[0:1, bass.ds(i * U, U + 3)], engines=(engine,),
                                                        min_val=0, max_val=E - 1,
                                                        skip_runtime_bounds_check_because=
                                                        "route clamps every expert to 0 .. E - 1")[1]

    index = sb(pre + "index", [P, U], I32)
    x = sb(pre + "x", [P, U, D])
    xT = sb(pre + "xT", [P, 2, P])
    hid = sb(pre + "hid", [P, 2, F])
    act_hid = sb(pre + "act_hid", [P, 2, F]) if gelu else hid
    hidT = sb(pre + "hidT", [P, 2, F])
    y = sb(pre + "y", [P, 2, D])
    xT_ps = [psum(f"{pre}xT_ps{i}") for i in range(2)]
    hid_ps = [psum(f"{pre}hid_ps{i}") for i in range(2)]
    hidT_ps = [psum(f"{pre}hidT_ps{i}") for i in range(2)]
    y_ps = [psum(f"{pre}y_ps{i}") for i in range(2)]
    x_in = [sem(f"{pre}x_in{i}") for i in range(U)]
    y_out = [sem(f"{pre}y_out{i}") for i in range(2)]
    index_done = sem(pre + "index_done")
    x_turned = sem(pre + "x_turned")
    xT_done = sem(pre + "xT_done")
    hid_summed = sem(pre + "hid_summed")
    hid_done = sem(pre + "hid_done")
    act_done = sem(pre + "act_done") if gelu else hid_done
    hid_turned = sem(pre + "hid_turned")
    hidT_done = sem(pre + "hidT_done")
    y_summed = sem(pre + "y_summed")
    y_done = sem(pre + "y_done")

    with nc.Block() as block:

        @block.gpsimd
        def _(pool):
            pool.tensor_tensor(index[:, 0:1], r.token[:, 0:1], c.zero_i[:], ALU.add).then_inc(index_done, 1)

            def step(i, u):
                j = Item(i, u, 0, U, NT)
                if not j.alive:
                    return
                if j.after(7):
                    pool.wait_ge(x_turned, j.n - 6)
                pool.wait_ge(index_done, j.n + 1)
                nxt = (u + 1) % U
                pool.tensor_tensor(index[:, nxt:nxt + 1], r.token[:, bass.ds(j.n + 1, 1)], c.zero_i[:], ALU.add
                                   ).then_inc(index_done, 1)
                pool.indirect_dma_start(x[:, j.slot], None, xln_dram,
                                        bass.IndirectOffsetOnAxis(ap=index[:, u:u + 1], axis=0)
                                        ).then_inc(x_in[j.slot], 16)
            steps(pool, NT, 0, U, step)

        @block.tensor
        def _(pe):
            window = []

            def step(i, u):
                g = Item(i, u, 5, U, NT)
                if g.alive:
                    pe.wait_ge(act_done, g.n + 1)
                    if g.after(2):
                        pe.wait_ge(hidT_done, g.n - 1)
                    for k in range(K):
                        mm = pe.transpose(hidT_ps[g.pair][:, P * k:P * k + P], act_hid[:, g.pair, P * k:P * k + P],
                                          c.ident[:])
                    mm.then_inc(hid_turned, 1)
                x1 = Item(i, u, 1, U, NT)
                if x1.alive:
                    pe.wait_ge(x_in[x1.slot], (x1.round + 1) * 16)
                    if x1.after(2):
                        pe.wait_ge(xT_done, x1.n - 1)
                    pe.transpose(xT_ps[x1.pair][:, 0:P], x[:, x1.slot], c.ident[:]).then_inc(x_turned, 1)
                if u == 0:
                    window[:] = load_window(mybir.EngineType.PE, i)
                o = Item(i, u, 6, U, NT)
                if o.alive:
                    e = window[u]
                    pe.wait_ge(hidT_done, o.n + 1)
                    if o.after(2):
                        pe.wait_ge(y_done, o.n - 1)
                    for k in range(K):
                        mm = pe.matmul(y_ps[o.pair][:, 0:D], hidT[:, o.pair, P * k:P * k + P],
                                       c.W2[:, bass.ds(e * (K * D) + k * D, D)], start=(k == 0), stop=(k == K - 1))
                    mm.then_inc(y_summed, 1)
                h = Item(i, u, 3, U, NT)
                if h.alive:
                    e = window[u + 3]
                    pe.wait_ge(xT_done, h.n + 1)
                    if h.after(2):
                        pe.wait_ge(hid_done, h.n - 1)
                    pe.matmul(hid_ps[h.pair][:, 0:F], xT[:, h.pair], c.W1[:, bass.ds(e * F, F)], start=True, stop=True
                              ).then_inc(hid_summed, 1)
            steps(pe, NT, 6, U, step)

        @block.scalar
        def _(act):
            def step(i, u):
                g = Item(i, u, 5, U, NT)
                if g.alive:
                    act.wait_ge(hid_turned, g.n + 1)
                    if g.after(2):
                        act.wait_ge(y_summed, g.n - 1)
                    act.activation(hidT[:, g.pair], hidT_ps[g.pair][:, 0:F], ACT.Copy if gelu else ACT.Relu
                                   ).then_inc(hidT_done, 1)
                h = Item(i, u, 3, U, NT)
                if gelu and h.alive:
                    act.wait_ge(hid_done, h.n + 1)
                    if h.after(2):
                        act.wait_ge(hid_turned, h.n - 1)
                    act.activation(act_hid[:, h.pair], hid[:, h.pair], ACT.Gelu).then_inc(act_done, 1)
            steps(act, NT, 5, U, step)

        @block.vector
        def _(dve):
            window = []

            def step(i, u):
                if u == 0:
                    window[:] = load_window(mybir.EngineType.DVE, i)
                o = Item(i, u, 6, U, NT)
                if o.alive:
                    e = window[u]
                    dve.wait_ge(y_summed, o.n + 1)
                    if o.after(2):
                        dve.wait_ge(y_out[o.pair], (i * (U // 2) + (u - 6) // 2) * 16)
                    dve.tensor_tensor(y[:, o.pair], y_ps[o.pair][:, 0:D], c.b2[:, bass.ds(e * D, D)], ALU.add
                                      ).then_inc(y_done, 1)
                h = Item(i, u, 3, U, NT)
                if h.alive:
                    e = window[u + 3]
                    dve.wait_ge(hid_summed, h.n + 1)
                    if h.after(2):
                        dve.wait_ge(act_done if gelu else hid_turned, h.n - 1)
                    dve.tensor_tensor(hid[:, h.pair], hid_ps[h.pair][:, 0:F], c.b1[:, bass.ds(e * F, F)], ALU.add
                                      ).then_inc(hid_done, 1)
                x1 = Item(i, u, 1, U, NT)
                if x1.alive:
                    dve.wait_ge(x_turned, x1.n + 1)
                    if x1.after(2):
                        dve.wait_ge(hid_summed, x1.n - 1)
                    dve.tensor_copy(xT[:, x1.pair], xT_ps[x1.pair][:, 0:P]).then_inc(xT_done, 1)
            steps(dve, NT, 6, U, step)

        @block.sync
        def _(sp):
            def step(i, u):
                o = Item(i, u, 6, U, NT)
                if o.alive:
                    sp.wait_ge(y_done, o.n + 1)
                    sp.dma_start(rows(y_dram, o.n, 1), y[:, o.pair].unsqueeze(1)).then_inc(y_out[o.pair], 16)
            steps(sp, NT, 6, U, step)
            for k in range(2):
                sp.wait_ge(y_out[k], NT // 2 * 16)


class Combine:

    def __init__(self, sem, sb, c, pre, r, y_dram, B):
        self.c, self.r, self.y_dram, self.B = c, r, y_dram, B
        self.index = sb(pre + "index", [P, 2, 4], I32)
        self.y = sb(pre + "y", [P, 2, 4, D])
        self.y_in = [sem(f"{pre}y_in{i}") for i in range(2)]
        self.index_done = sem(pre + "index_done")
        self.first_done = sem(pre + "first_done")
        self.x_done = sem(pre + "x_done")

    def pool_begin(self, pool):
        pool.tensor_tensor(self.index[:, 0], self.r.slot[:, 0:2].rearrange("p t k -> p (t k)"),
                           self.c.zero_i[:].to_broadcast([P, 4]), ALU.add).then_inc(self.index_done, 1)

    def pool(self, pool, i, u):
        g = Item(i, u, 0, 2, self.B)
        if not g.alive:
            return
        if g.after(2):
            pool.wait_ge(self.x_done, g.n - 1)
        if g.after(1):
            pool.wait_ge(self.y_in[1 - g.pair], (i + (u - 1) // 2 + 1) * 64)
        pool.wait_ge(self.index_done, g.n + 1)
        pool.tensor_tensor(self.index[:, 1 - g.pair].rearrange("p (t k) -> p t k", k=2), tiles(self.r.slot, g.n + 1, 2),
                           self.c.zero_i[:].unsqueeze(2).to_broadcast([P, 2, 2]), ALU.add
                           ).then_inc(self.index_done, 1)
        for n in range(4):
            pool.indirect_dma_start(self.y[:, g.pair, n], None, self.y_dram,
                                    bass.IndirectOffsetOnAxis(ap=self.index[:, g.pair, n:n + 1], axis=0)
                                    ).then_inc(self.y_in[g.pair], 16)

    def vector(self, dve, a, base, dst):
        weight = tiles(self.r.weight, a.n, 2)
        dve.wait_ge(self.y_in[a.pair], (a.round + 1) * 64)
        for t in range(2):
            op = dve.scalar_tensor_tensor(dst[:, t], self.y[:, a.pair, 2 * t], weight[:, t, 0:1], base[:, t],
                                          ALU.mult, ALU.add)
        op.then_inc(self.first_done, 1)
        dve.wait_ge(self.first_done, a.n + 1)
        for t in range(2):
            op = dve.scalar_tensor_tensor(dst[:, t], self.y[:, a.pair, 2 * t + 1], weight[:, t, 1:2], dst[:, t],
                                          ALU.mult, ALU.add)
        op.then_inc(self.x_done, 1)


def graph_attention_layer(nc, sem, sb, psum, c, w, adj_dram, xs, B, combine, gate):
    U = 2
    NEG_SLOPE = -0.2

    adj = sb("c_adj", [P, U, 512])
    penalty = sb("c_penalty", [P, U, 512])
    stats = sb("c_stats", [P, U, 2, 6])
    meanvar = sb("c_meanvar", [P, U, 2, 2])
    var_eps = sb("c_var_eps", [P, U, 2])
    rstd = sb("c_rstd", [P, U, 2])
    xln = sb("c_xln", [P, U, 2, D])
    xln_all = sb("c_xln_all", [P, 2 * B, D])
    xT = sb("c_xT", [P, U, 256])
    xpT = sb("c_xpT", [P, U, 256])
    squares = sb("c_squares", [P, U, 512])
    sumsq = sb("c_sumsq", [P, U, 2])
    inv_mag = sb("c_inv_mag", [P, U, 2])
    mag_diag = sb("c_mag_diag", [P, U, 256])
    mag_row = sb("c_mag_row", [P, U, 256])
    score = sb("c_score", [P, U, 512])
    leaky = sb("c_leaky", [P, U, 512])
    masked = sb("c_masked", [P, U, 512])
    rowmax = sb("c_rowmax", [P, U, 2])
    neg_max = sb("c_neg_max", [P, U, 2])
    e = sb("c_e", [P, U, 512])
    eT = sb("c_eT", [P, U, 512])
    e_sum = sb("c_e_sum", [P, U, 2])
    inv_sum = sb("c_inv_sum", [P, U, 2])
    h = sb("c_h", [P, U, 256])
    h_neg = sb("c_h_neg", [P, U, 256])
    h_exp = sb("c_h_exp", [P, U, 256])
    h_elu1 = sb("c_h_elu1", [P, U, 256])
    W_a = sb("c_W_a", [P, P])
    bias = sb("c_bias", [P, D])

    xT_ps = psum("c_xT_ps")
    xpT_ps = psum("c_xpT_ps")
    A_ps = [psum(f"c_A_ps{i}") for i in range(U)]
    mag_ps = psum("c_mag_ps")
    eT_ps = psum("c_eT_ps")
    out_ps = psum("c_out_ps")

    adj_in = [sem(f"c_adj_in{i}") for i in range(U)]
    w_in = [sem(f"c_w_in{i}") for i in range(2)]
    names = ("stats_done meanvar_done var_eps_done rstd_done xln_done xln_kept x_turned xT_done xp_summed "
             "xpT_done A_summed sumsq_done inv_mag_done mag_diag_done mag_spread mag_row_done score_done leaky_done "
             "penalty_done masked_done neg_max_done exp_done e_turned eT_done inv_sum_done "
             "out_summed h_done h_neg_done h_exp_done elu1_done x_done").split()
    s = Shared()
    (s.stats_done, s.meanvar_done, s.var_eps_done, s.rstd_done, s.xln_done, s.xln_kept, s.x_turned,
     s.xT_done, s.xp_summed, s.xpT_done, s.A_summed, s.sumsq_done, s.inv_mag_done, s.mag_diag_done, s.mag_spread,
     s.mag_row_done, s.score_done, s.leaky_done, s.penalty_done, s.masked_done, s.neg_max_done,
     s.exp_done, s.e_turned, s.eT_done, s.inv_sum_done, s.out_summed, s.h_done, s.h_neg_done, s.h_exp_done,
     s.elu1_done, s.x_done) = [sem("c_" + name) for name in names]

    adj_rows = adj_dram.rearrange("b (h p) m -> b p h m", p=P)

    with nc.Block() as block:

        @block.sync
        def _(sp):
            sp.dma_start(W_a[:], w["L1_gnn_W_a"]).then_inc(w_in[0], 16)
            sp.dma_start(bias[:], w["L1_gnn_bias"].partition_broadcast(P)
                         .rearrange("p a d -> p (a d)")).then_inc(w_in[1], 16)

            def step(i, u):
                a = Item(i, u, 3, U, B)
                if a.alive:
                    if a.after(2):
                        sp.wait_ge(s.penalty_done, a.n - 1)
                    sp.dma_start(adj[:, a.pair].rearrange("p (h m) -> p h m", h=2),
                                 adj_rows[bass.ds(a.n, 1)].rearrange("a p h m -> (a p) h m")
                                 ).then_inc(adj_in[a.pair], 16)
                if a.known and a.n == 1:
                    gate.sync_begin(sp)
                gate.sync(sp, i, u)
            steps(sp, B, 8, U, step)
            gate.sync_end(sp)

        @block.gpsimd
        def _(pool):
            combine.pool_begin(pool)

            def step(i, u):
                combine.pool(pool, i, u)
                b = Item(i, u, 2, U, B)
                if b.alive:
                    pool.wait_ge(s.meanvar_done, b.n + 1)
                    pool.tensor_tensor(var_eps[:, b.pair], meanvar[:, b.pair, :, 1], c.ln_eps[:], ALU.add
                                       ).then_inc(s.var_eps_done, 1)
                    if b.after(2):
                        pool.wait_ge(s.xln_done, b.n - 1)
                    pool.wait_ge(s.var_eps_done, b.n + 1)
                    pool.tensor_tensor(rstd[:, b.pair], var_eps[:, b.pair], c.neg_half[:, 0:2], ALU.pow
                                       ).then_inc(s.rstd_done, 1)
                a = Item(i, u, 3, U, B)
                if a.alive:
                    if a.after(2):
                        pool.wait_ge(s.score_done, a.n - 1)
                        pool.wait_ge(s.mag_diag_done, a.n - 1)
                    pool.wait_ge(s.sumsq_done, a.n + 1)
                    pool.tensor_tensor(inv_mag[:, a.pair], sumsq[:, a.pair], c.neg_half[:, 0:2], ALU.pow
                                       ).then_inc(s.inv_mag_done, 1)
                gate.pool(pool, i, u)
            steps(pool, B, 7, U, step)

        @block.tensor
        def _(pe):
            pe.wait_ge(w_in[0], 16)
            gate.tensor_begin(pe)

            def step(i, u):
                gate.tensor_scores(pe, i, u)
                y = Item(i, u, 4, U, B)
                if y.alive:
                    pe.wait_ge(s.mag_diag_done, y.n + 1)
                    if y.after(1):
                        pe.wait_ge(s.mag_row_done, y.n)
                    pe.matmul(mag_ps[:, 0:256], c.ones[:], mag_diag[:, y.pair], start=True, stop=True
                              ).then_inc(s.mag_spread, 1)
                a = Item(i, u, 3, U, B)
                if a.alive:
                    pe.wait_ge(s.xT_done, a.n + 1)
                    if a.after(1):
                        pe.wait_ge(s.xpT_done, a.n)
                    pe.matmul(xpT_ps[:, 0:256], W_a[:], xT[:, a.pair], start=True, stop=True).then_inc(s.xp_summed, 1)
                z = Item(i, u, 5, U, B)
                if z.alive:
                    pe.wait_ge(s.exp_done, 2 * z.n + 2)
                    if z.after(1):
                        pe.wait_ge(s.eT_done, z.n)
                    for m in range(2):
                        for k in range(2):
                            mm = pe.transpose(eT_ps[:, 256 * m + P * k:256 * m + P * k + P],
                                              e[:, z.pair, 256 * k + P * m:256 * k + P * m + P], c.ident[:])
                    mm.then_inc(s.e_turned, 1)
                if a.alive:
                    pe.wait_ge(s.xpT_done, a.n + 1)
                    if a.after(2):
                        pe.wait_ge(s.score_done, a.n - 1)
                    for k in range(2):
                        mm = pe.matmul(A_ps[a.pair][:, 256 * k:256 * k + 256], xpT[:, a.pair, P * k:P * k + P],
                                       xpT[:, a.pair], start=True, stop=True)
                    mm.then_inc(s.A_summed, 1)
                b = Item(i, u, 2, U, B)
                if b.alive:
                    pe.wait_ge(s.xln_done, b.n + 1)
                    if b.after(1):
                        pe.wait_ge(s.xT_done, b.n)
                    for k in range(2):
                        mm = pe.transpose(xT_ps[:, P * k:P * k + P], xln[:, b.pair, k], c.ident[:])
                    mm.then_inc(s.x_turned, 1)
                if z.alive:
                    pe.wait_ge(s.eT_done, z.n + 1)
                    pe.wait_ge(s.xln_kept, z.n + 1)
                    if z.after(1):
                        pe.wait_ge(s.h_done, z.n)
                    for k in range(2):
                        for m in range(2):
                            mm = pe.matmul(out_ps[:, P * k:P * k + P], eT[:, z.pair, 256 * m + P * k:256 * m + P * k + P],
                                           tiles(xln_all, z.n, 2)[:, m], start=(m == 0), stop=(m == 1))
                    mm.then_inc(s.out_summed, 1)
                gate.tensor_turn(pe, i, u)
            steps(pe, B, 9, U, step)

        @block.scalar
        def _(act):
            def step(i, u):
                y = Item(i, u, 4, U, B)
                if y.alive:
                    act.wait_ge(s.inv_mag_done, y.n + 1)
                    if y.after(2):
                        act.wait_ge(s.mag_spread, y.n - 1)
                    for k in range(2):
                        op = act.activation(mag_diag[:, y.pair, P * k:P * k + P], c.ident[:], ACT.Copy,
                                            scale=inv_mag[:, y.pair, k:k + 1])
                    op.then_inc(s.mag_diag_done, 1)
                    act.wait_ge(s.mag_spread, y.n + 1)
                    if y.after(2):
                        act.wait_ge(s.score_done, y.n - 1)
                    act.copy(mag_row[:, y.pair], mag_ps[:, 0:256]).then_inc(s.mag_row_done, 1)
                a = Item(i, u, 3, U, B)
                if a.alive:
                    act.wait_ge(s.xp_summed, a.n + 1)
                    if a.after(2):
                        act.wait_ge(s.A_summed, a.n - 1)
                    act.copy(xpT[:, a.pair], xpT_ps[:, 0:256]).then_inc(s.xpT_done, 1)
                z = Item(i, u, 5, U, B)
                if z.alive:
                    act.wait_ge(s.e_turned, z.n + 1)
                    if z.after(2):
                        act.wait_ge(s.out_summed, z.n - 1)
                    act.copy(eT[:, z.pair], eT_ps[:]).then_inc(s.eT_done, 1)
                gate.scalar_norm(act, i, u)
                v = Item(i, u, 6, U, B)
                if v.alive:
                    act.wait_ge(s.h_neg_done, v.n + 1)
                    if v.after(2):
                        act.wait_ge(s.elu1_done, v.n - 1)
                    act.activation(h_exp[:, v.pair], h_neg[:, v.pair], ACT.Exp).then_inc(s.h_exp_done, 1)
                if a.alive:
                    act.wait_ge(s.A_summed, a.n + 1)
                    if a.after(2):
                        act.wait_ge(s.inv_mag_done, a.n - 1)
                    for k in range(2):
                        op = act.activation(squares[:, a.pair, 256 * k:256 * k + 256], A_ps[a.pair][:, 256 * k:256 * k + 256], ACT.Square,
                                            accum_out=sumsq[:, a.pair, k:k + 1])
                    op.then_inc(s.sumsq_done, 1)
                b = Item(i, u, 2, U, B)
                if b.alive:
                    act.wait_ge(s.x_turned, b.n + 1)
                    if b.after(2):
                        act.wait_ge(s.xp_summed, b.n - 1)
                    act.copy(xT[:, b.pair], xT_ps[:, 0:256]).then_inc(s.xT_done, 1)
                    act.copy(tiles(xln_all, b.n, 2), xln[:, b.pair]).then_inc(s.xln_kept, 1)
                if y.alive:
                    act.wait_ge(s.neg_max_done, y.n + 1)
                    if y.after(2):
                        act.wait_ge(s.e_turned, y.n - 1)
                        act.wait_ge(s.inv_sum_done, y.n - 1)
                    for k in range(2):
                        act.activation(e[:, y.pair, 256 * k:256 * k + 256], masked[:, y.pair, 256 * k:256 * k + 256],
                                       ACT.Exp, bias=neg_max[:, y.pair, k:k + 1],
                                       accum_out=e_sum[:, y.pair, k:k + 1]).then_inc(s.exp_done, 1)
                gate.scalar_copy(act, i, u)
            steps(act, B, 8, U, step)

        @block.vector
        def _(dve):
            dve.wait_ge(w_in[1], 16)
            gate.vector_begin(dve)

            def step(i, u):
                v = Item(i, u, 6, U, B)
                z = Item(i, u, 5, U, B)
                y = Item(i, u, 4, U, B)
                q = Item(i, u, 7, U, B)
                b = Item(i, u, 2, U, B)
                f = Item(i, u, 1, U, B)
                gate.vector_wait(dve, i, u, s.x_done)
                gate.vector_neg_mean(dve, i, u)
                if y.alive:
                    dve.wait_ge(s.mag_row_done, y.n + 1)
                    if y.after(2):
                        dve.wait_ge(s.leaky_done, y.n - 1)
                    for k in range(2):
                        op = dve.scalar_tensor_tensor(score[:, y.pair, 256 * k:256 * k + 256],
                                                      A_ps[y.pair][:, 256 * k:256 * k + 256],
                                                      inv_mag[:, y.pair, k:k + 1], mag_row[:, y.pair],
                                                      ALU.mult, ALU.mult)
                    op.then_inc(s.score_done, 1)
                if y.alive:
                    dve.wait_ge(s.score_done, y.n + 1)
                    dve.scalar_tensor_tensor(leaky[:, y.pair], score[:, y.pair], NEG_SLOPE, score[:, y.pair],
                                             ALU.mult, ALU.max).then_inc(s.leaky_done, 1)
                if v.alive:
                    dve.wait_ge(s.out_summed, v.n + 1)
                    if v.after(2):
                        dve.wait_ge(s.elu1_done, v.n - 1)
                    for k in range(2):
                        op = dve.scalar_tensor_tensor(h[:, v.pair, P * k:P * k + P], out_ps[:, P * k:P * k + P],
                                                      inv_sum[:, v.pair, k:k + 1], bias[:], ALU.mult, ALU.add)
                    op.then_inc(s.h_done, 1)
                if y.alive:
                    dve.wait_ge(s.leaky_done, y.n + 1)
                    dve.wait_ge(s.penalty_done, y.n + 1)
                    if y.after(2):
                        dve.wait_ge(s.exp_done, 2 * y.n - 2)
                if v.alive:
                    dve.wait_ge(s.h_done, v.n + 1)
                    if v.after(2):
                        dve.wait_ge(s.h_exp_done, v.n - 1)
                    dve.tensor_scalar(h_neg[:, v.pair], h[:, v.pair], 0.0, None, ALU.min).then_inc(s.h_neg_done, 1)
                if y.alive:
                    for k in range(2):
                        op = dve.tensor_tensor_reduce(out=masked[:, y.pair, 256 * k:256 * k + 256],
                                                      in0=leaky[:, y.pair, 256 * k:256 * k + 256],
                                                      in1=penalty[:, y.pair, 256 * k:256 * k + 256], scale=1.0,
                                                      scalar=-BIG, op0=ALU.add, op1=ALU.max,
                                                      accum_out=rowmax[:, y.pair, k:k + 1])
                    op.then_inc(s.masked_done, 1)
                if y.alive:
                    dve.wait_ge(s.masked_done, y.n + 1)
                    dve.tensor_scalar(neg_max[:, y.pair], rowmax[:, y.pair], -1.0, None, ALU.mult
                                      ).then_inc(s.neg_max_done, 1)
                a = Item(i, u, 3, U, B)
                if a.alive:
                    dve.wait_ge(adj_in[a.pair], (a.round + 1) * 16)
                    dve.tensor_scalar(penalty[:, a.pair], adj[:, a.pair], 0.0, MASKED, ALU.is_le, ALU.mult
                                      ).then_inc(s.penalty_done, 1)
                if b.alive:
                    dve.wait_ge(s.rstd_done, b.n + 1)
                    if b.after(2):
                        dve.wait_ge(s.x_turned, b.n - 1)
                        dve.wait_ge(s.xln_kept, b.n - 1)
                    for k in range(2):
                        op = dve.tensor_scalar(xln[:, b.pair, k], tiles(xs, b.n, 2)[:, k], meanvar[:, b.pair, k, 0:1],
                                               rstd[:, b.pair, k:k + 1], ALU.subtract, ALU.mult)
                    op.then_inc(s.xln_done, 1)
                if f.alive:
                    combine.vector(dve, f, tiles(xs, f.n, 2), tiles(xs, f.n, 2))
                    dve.wait_ge(combine.x_done, f.n + 1)
                if v.alive:
                    dve.wait_ge(s.h_exp_done, v.n + 1)
                    dve.scalar_tensor_tensor(h_elu1[:, v.pair], h[:, v.pair], 0.0, h_exp[:, v.pair], ALU.max, ALU.add
                                             ).then_inc(s.elu1_done, 1)
                if f.alive:
                    for k in range(2):
                        op = dve.bn_stats(stats[:, f.pair, k], tiles(xs, f.n, 2)[:, k])
                    op.then_inc(s.stats_done, 1)
                    dve.wait_ge(s.stats_done, f.n + 1)
                if y.alive:
                    dve.wait_ge(s.exp_done, 2 * y.n + 2)
                    dve.reciprocal(inv_sum[:, y.pair], e_sum[:, y.pair]).then_inc(s.inv_sum_done, 1)
                if f.alive:
                    for k in range(2):
                        op = dve.bn_aggr(meanvar[:, f.pair, k], stats[:, f.pair, k])
                    op.then_inc(s.meanvar_done, 1)
                gate.vector_stats(dve, i, u)
                if v.alive:
                    dve.wait_ge(s.elu1_done, v.n + 1)
                    dve.scalar_tensor_tensor(tiles(xs, v.n, 2), h_elu1[:, v.pair].rearrange("p (k d) -> p k d", k=2),
                                             -1.0, tiles(xs, v.n, 2), ALU.add, ALU.add).then_inc(s.x_done, 1)
            steps(dve, B, 9, U, step)
            gate.vector_end(dve)


def last_norm(nc, sem, sb, c, w, xs, xln_dram, combine, out_dram, B):
    U = 2
    xln = sb("l_xln", [P, U, 2, D])
    moe = sb("l_moe", [P, U, 2, D])
    stats = sb("l_stats", [P, U, 2, 6])
    meanvar = sb("l_meanvar", [P, U, 2, 2])
    var_eps = sb("l_var_eps", [P, U, 2])
    rstd = sb("l_rstd", [P, U, 2])
    normed = sb("l_normed", [P, U, 2, D])
    scaled = sb("l_scaled", [P, U, 2, D])
    x_beta = sb("l_x_beta", [P, U, 2, D])
    result = sb("l_result", [P, U, 2, D])
    gamma = sb("l_gamma", [P, 2, D])
    beta = sb("l_beta", [P, 2, D])
    w_in = [sem(f"l_w_in{k}") for k in range(4)]
    xln_in = [sem(f"l_xln_in{k}") for k in range(U)]
    out_stored = [sem(f"l_out_stored{k}") for k in range(U)]
    stats_done = sem("l_stats_done")
    meanvar_done = sem("l_meanvar_done")
    var_eps_done = sem("l_var_eps_done")
    rstd_done = sem("l_rstd_done")
    normed_done = sem("l_normed_done")
    scaled_done = sem("l_scaled_done")
    x_beta_done = sem("l_x_beta_done")
    result_done = sem("l_result_done")

    with nc.Block() as block:

        @block.sync
        def _(sp):
            for k in range(2):
                sp.dma_start(gamma[:, k], w["L1_ffn_gamma"].partition_broadcast(P)).then_inc(w_in[k], 16)
                sp.dma_start(beta[:, k], w["L1_ffn_beta"].partition_broadcast(P)).then_inc(w_in[2 + k], 16)

            def step(i, u):
                g = Item(i, u, 0, U, B)
                if g.alive:
                    if g.after(2):
                        sp.wait_ge(combine.x_done, g.n - 1)
                    sp.dma_start(xln[:, g.pair], rows(xln_dram, g.n, 2)).then_inc(xln_in[g.pair], 16)
                o = Item(i, u, 3, U, B)
                if o.alive:
                    sp.wait_ge(result_done, o.n + 1)
                    sp.dma_start(rows(out_dram, o.n, 2), result[:, o.pair]).then_inc(out_stored[o.pair], 16)
            steps(sp, B, 3, U, step)
            for k in range(U):
                sp.wait_ge(out_stored[k], B // U * 16)

        @block.gpsimd
        def _(pool):
            combine.pool_begin(pool)

            def step(i, u):
                combine.pool(pool, i, u)
                f = Item(i, u, 1, U, B)
                if f.alive:
                    pool.wait_ge(meanvar_done, f.n + 1)
                    pool.tensor_tensor(var_eps[:, f.pair], meanvar[:, f.pair, :, 1], c.ln_eps[:], ALU.add
                                       ).then_inc(var_eps_done, 1)
                    if f.after(2):
                        pool.wait_ge(normed_done, f.n - 1)
                    pool.wait_ge(var_eps_done, f.n + 1)
                    pool.tensor_tensor(rstd[:, f.pair], var_eps[:, f.pair], c.neg_half[:, 0:2], ALU.pow
                                       ).then_inc(rstd_done, 1)
            steps(pool, B, 1, U, step)

        @block.vector
        def _(dve):
            for k in range(4):
                dve.wait_ge(w_in[k], 16)

            def step(i, u):
                f = Item(i, u, 1, U, B)
                if f.alive:
                    dve.wait_ge(xln_in[f.pair], (f.round + 1) * 16)
                    if f.after(2):
                        dve.wait_ge(normed_done, f.n - 1)
                    combine.vector(dve, f, xln[:, f.pair], moe[:, f.pair])
                    dve.wait_ge(combine.x_done, f.n + 1)
                    for k in range(2):
                        op = dve.bn_stats(stats[:, f.pair, k], moe[:, f.pair, k])
                    op.then_inc(stats_done, 1)
                    dve.wait_ge(stats_done, f.n + 1)
                o = Item(i, u, 3, U, B)
                if o.alive:
                    dve.wait_ge(normed_done, o.n + 1)
                    if o.after(2):
                        dve.wait_ge(out_stored[o.pair], o.round * 16)
                    dve.tensor_tensor(scaled[:, o.pair], normed[:, o.pair], gamma[:], ALU.mult).then_inc(scaled_done, 1)
                    dve.tensor_tensor(x_beta[:, o.pair], tiles(xs, o.n, 2), beta[:], ALU.add).then_inc(x_beta_done, 1)
                if f.alive:
                    for k in range(2):
                        op = dve.bn_aggr(meanvar[:, f.pair, k], stats[:, f.pair, k])
                    op.then_inc(meanvar_done, 1)
                b = Item(i, u, 2, U, B)
                if b.alive:
                    dve.wait_ge(rstd_done, b.n + 1)
                    if b.after(2):
                        dve.wait_ge(scaled_done, b.n - 1)
                    for k in range(2):
                        op = dve.tensor_scalar(normed[:, b.pair, k], moe[:, b.pair, k], meanvar[:, b.pair, k, 0:1],
                                               rstd[:, b.pair, k:k + 1], ALU.subtract, ALU.mult)
                    op.then_inc(normed_done, 1)
                if o.alive:
                    dve.wait_ge(scaled_done, o.n + 1)
                    dve.wait_ge(x_beta_done, o.n + 1)
                    dve.tensor_tensor(result[:, o.pair], scaled[:, o.pair], x_beta[:, o.pair], ALU.add
                                      ).then_inc(result_done, 1)
            steps(dve, B, 3, U, step)


@contextmanager
def phase(nc):
    with ExitStack() as own:
        sems = []

        def sem(name):
            sems.append(nc.alloc_semaphore(name=name))
            return sems[-1]

        def sb(name, shape, dt=F32):
            return own.enter_context(nc.sbuf_tensor(name, shape, dt))

        def psum(name):
            return own.enter_context(nc.psum_tensor(name, [P, 512], F32))

        yield sem, sb, psum
    nc.clear_and_free_semaphores(sems)
    nc.all_engine_barrier()


class Shared:
    pass


def program(nc, w, out, scratch):
    B, N, _ = w["x"].shape
    x_dram = w["x"].rearrange("b n d -> (b n) d")
    out_dram = out.rearrange("b n d -> (b n) d")
    T = B * N // P
    c = Shared()
    with ExitStack() as ctx:
        def keep(name, shape, dt=F32):
            return ctx.enter_context(nc.sbuf_tensor(name, shape, dt))

        xs = keep("xs", [P, T, D])
        c.W1 = keep("experts_W1", [P, 4096])
        c.W2 = keep("experts_W2", [P, 4096])
        c.b1 = keep("experts_b1", [P, 4096])
        c.b2 = keep("experts_b2", [P, 2048])
        with phase(nc) as (sem, sb, psum):
            constants(nc, sem, keep, sb, psum, c, w)

        logits = keep("logits", [P, T, 16])
        xln_dram = scratch["xln"]

        def gate_and_experts(names):
            E = w[names[0]].shape[1]
            return E, w[names[2]].shape[2], logits[:].rearrange("p t e -> p (t e)")[:, 0:T * E].rearrange(
                "p (t e) -> p t e", e=E)

        def routed(pre, E, F, logits, gelu):
            NT = expert_tiles(T, E)
            r = Shared()
            r.weight = keep(pre + "weight", [P, T, 2])
            r.slot = keep(pre + "slot", [P, T + 2, 2], I32)
            r.expert = keep(pre + "expert", [P, NT + 16], I32)
            r.token = keep(pre + "token", [P, NT + 1], I32)
            with phase(nc) as (sem, sb, psum):
                route(nc, sem, sb, psum, c, pre + "r_", logits, r, T, E)
            with phase(nc) as (sem, sb, psum):
                run_experts(nc, sem, sb, psum, c, pre + "e_", xln_dram, scratch[pre + "y"], r, T, E, F, gelu)
            return r

        names = ["L0_ffn_Wg", "L0_ffn_bg", "L0_ffn_W1", "L0_ffn_b1", "L0_ffn_W2", "L0_ffn_b2"]
        E, F, scores = gate_and_experts(names)
        with phase(nc) as (sem, sb, psum):
            gate = GateScores(sem, sb, psum, c, w, "ag_", 5, xs, xln_dram, scores, names, B, E, F)
            gnn_mlp_layer(nc, sem, sb, psum, c, x_dram, w["adj"], xs, B, gate)
        r = routed("b_", E, F, scores, True)

        names = ["L1_ffn_gate_w", "L1_ffn_gate_b", "L1_ffn_w1", "L1_ffn_b1", "L1_ffn_w2", "L1_ffn_b2"]
        E, F, scores = gate_and_experts(names)
        with phase(nc) as (sem, sb, psum):
            combine = Combine(sem, sb, c, "cc_", r, scratch["b_y"], B)
            gate = GateScores(sem, sb, psum, c, w, "cg_", 7, xs, xln_dram, scores, names, B, E, F)
            graph_attention_layer(nc, sem, sb, psum, c, w, w["adj"], xs, B, combine, gate)
        r = routed("d_", E, F, scores, False)
        with phase(nc) as (sem, sb, psum):
            combine = Combine(sem, sb, c, "lc_", r, scratch["d_y"], B)
            last_norm(nc, sem, sb, c, w, xs, xln_dram, combine, out_dram, B)


_INS = ["x", "adj", "L0_gnn_epsilon", "L0_gnn_W1", "L0_gnn_b1", "L0_gnn_rms_weight", "L0_gnn_W2", "L0_gnn_b2",
        "L0_ffn_Wg", "L0_ffn_bg", "L0_ffn_W1", "L0_ffn_b1", "L0_ffn_W2", "L0_ffn_b2", "L1_gnn_W_a", "L1_gnn_bias",
        "L1_ffn_gate_w", "L1_ffn_gate_b", "L1_ffn_w1", "L1_ffn_b1", "L1_ffn_w2", "L1_ffn_b2", "L1_ffn_gamma",
        "L1_ffn_beta"]


def kernel(**inputs):
    import numpy as _np
    import concourse.bacc as _bacc
    from concourse.bass_utils import run_bass_kernel_spmd as _run

    nc = _bacc.Bacc("TRN2", target_bir_lowering=False, num_devices=1)
    arrays, args = {}, {}
    for name in _INS:
        a = _np.ascontiguousarray(inputs[name])
        if name == "L0_gnn_epsilon":
            a = a.reshape(1)
        arrays[f"in_{name}"] = a
        args[name] = nc.dram_tensor(f"in_{name}", a.shape, mybir.dt.from_np(a.dtype), kind="ExternalInput").ap()
    out = nc.dram_tensor("out_x", inputs["x"].shape, F32, kind="ExternalOutput").ap()
    tokens = inputs["x"].shape[0] * inputs["x"].shape[1]
    scratch = {"xln": nc.dram_tensor("xln_rows", [tokens, D], F32).ap()}
    for layer, gate in (("b_", "L0_ffn_Wg"), ("d_", "L1_ffn_gate_w")):
        slots = expert_tiles(tokens // P, inputs[gate].shape[1]) * P
        scratch[layer + "y"] = nc.dram_tensor(layer + "y_rows", [slots, D], F32).ap()
    program(nc, args, out, scratch)
    r = _run(nc, [arrays], core_ids=[0])
    return r.results[0]["out_x"]
```

```python
from contextlib import ExitStack, contextmanager

import concourse.bass as bass
from concourse import mybir
from concourse.alu_op_type import AluOpType as ALU

ACT = mybir.ActivationFunctionType
F32 = mybir.dt.float32
BF16 = mybir.dt.bfloat16
I32 = mybir.dt.int32
AX_X = mybir.AxisListType.X

P = 128
D = 128
LN_EPS = 1e-5
RMS_EPS = 1e-6
MASKED = -9000000000000000.0
BIG = 3.0e38


def steps(eng, count, depth, unroll, step):
    head = -(-(depth + unroll) // unroll) * unroll
    full = count // unroll * unroll
    assert head < full
    for s in range(head):
        step(s // unroll, s % unroll)
    with eng.Fori(head // unroll, full // unroll) as i:
        for u in range(unroll):
            step(i, u)
    for s in range(full, count + depth):
        step(s // unroll, s % unroll)


class Item:

    def __init__(self, i, u, lag, unroll, count):
        self.n = i * unroll + (u - lag)
        self.round = i + (u - lag) // unroll
        self.slot = (u - lag) % unroll
        self.pair = self.slot % 2
        self.known = isinstance(i, int)
        self.alive = not self.known or 0 <= self.n < count

    def after(self, k):
        return not self.known or self.n >= k


def rows(dram, n, k):
    v = dram.rearrange("(n k p) d -> n p k d", p=P, k=k)
    return v[bass.ds(n, 1)].rearrange("a p k d -> (a p) k d")


def tiles(buf, n, k):
    return buf[:, bass.ds(n * k, k), :]


def constants(nc, sem, keep, sb, psum, c, w):
    H = 512
    HC = H // P
    c.ident = keep("ident", [P, P])
    c.ones = keep("ones", [P, P])
    c.neg_half = keep("neg_half", [P, 256])
    c.zero_i = keep("zero_i", [P, 1], I32)
    c.iota_row = keep("iota_row", [P, 256])
    c.iota_row_bf = keep("iota_row_bf", [P, 256], BF16)
    c.part_no = keep("part_no", [P, 1])
    c.before = keep("before", [P, P], BF16)
    c.ones_bf = keep("ones_bf", [P, P], BF16)
    c.a_W1w = keep("a_W1w", [P, H])
    c.a_W2 = keep("a_W2", [P, HC, D])
    c.a_b1w = keep("a_b1w", [P, HC])
    c.a_gram = keep("a_gram", [P, P])
    c.a_cross = keep("a_cross", [P, 1])
    c.a_b1sq = keep("a_b1sq", [P, 1])
    c.a_eps_ident = keep("a_eps_ident", [P, 512])
    c.a_b2 = keep("a_b2", [P, 2, D])
    W1 = sb("s_W1", [P, H])
    W1T = sb("s_W1T", [P, H])
    w_bc = sb("s_w_bc", [P, H])
    b1_bc = sb("s_b1_bc", [P, H])
    b1_col = sb("s_b1_col", [P, HC])
    w_col = sb("s_w_col", [P, HC])
    eps_bc = sb("s_eps_bc", [P, 1])
    junk = sb("s_junk", [P, H])
    cross = sb("s_cross", [P, 2])
    iota_i = sb("s_iota_i", [P, 256], I32)
    part_i = sb("s_part_i", [P, 1], I32)
    turn_ps = psum("s_turn_ps")
    gram_ps = psum("s_gram_ps")

    loaded = [sem(f"s_loaded{n}") for n in range(9)]
    pool_filled = sem("s_pool_filled")
    pool_made = sem("s_pool_made")
    turned = sem("s_turned")
    w1T_done = sem("s_w1T_done")
    gram_summed = sem("s_gram_summed")
    made = sem("s_made")

    loads = [
        (W1[:], w["L0_gnn_W1"]),
        (w_bc[:], w["L0_gnn_rms_weight"].partition_broadcast(P)),
        (b1_bc[:], w["L0_gnn_b1"].partition_broadcast(P)),
        (b1_col[:], w["L0_gnn_b1"].rearrange("(c p) -> p c", p=P)),
        (w_col[:], w["L0_gnn_rms_weight"].rearrange("(c p) -> p c", p=P)),
        (c.a_W2[:], w["L0_gnn_W2"].rearrange("(c p) d -> p c d", p=P)),
        (c.a_b2[:, 0], w["L0_gnn_b2"].partition_broadcast(P)),
        (c.a_b2[:, 1], w["L0_gnn_b2"].partition_broadcast(P)),
        (eps_bc[:], w["L0_gnn_epsilon"].partition_broadcast(P)),
    ]

    with nc.Block() as block:

        @block.sync
        def _(sp):
            for n, (dst, src) in enumerate(loads):
                sp.dma_start(dst, src, allow_slow_non_contiguous=True).then_inc(loaded[n], 16)
            for n in range(len(loads)):
                sp.wait_ge(loaded[n], 16)

        @block.gpsimd
        def _(pool):
            pool.memset(c.ident[:], 0.0)
            pool.memset(c.before[:], 1.0)
            pool.memset(c.ones[:], 1.0)
            pool.memset(c.ones_bf[:], 1.0)
            pool.memset(c.neg_half[:], -0.5)
            pool.memset(c.zero_i[:], 0)
            pool.memset(c.a_eps_ident[:], 0.0)
            pool.iota(iota_i[:], [[1, 256]], base=0, channel_multiplier=0)
            pool.iota(part_i[:], [[0, 1]], base=0, channel_multiplier=1).then_inc(pool_filled, 1)
            pool.wait_ge(pool_filled, 1)
            pool.affine_select(out=c.ident[:], in_=c.ident[:], compare_op=ALU.not_equal, fill=1.0, base=0,
                               pattern=[[-1, P]], channel_multiplier=1)
            pool.affine_select(out=c.before[:], in_=c.before[:], compare_op=ALU.is_gt, fill=0.0, base=0,
                               pattern=[[1, P]], channel_multiplier=-1)
            pool.tensor_copy(c.iota_row[:], iota_i[:])
            pool.tensor_copy(c.iota_row_bf[:], iota_i[:])
            pool.tensor_copy(c.part_no[:], part_i[:]).then_inc(pool_made, 1)

        @block.tensor
        def _(pe):
            pe.wait_ge(pool_made, 1)
            pe.wait_ge(loaded[0], 16)
            for j in range(HC):
                mm = pe.transpose(turn_ps[:, P * j:P * j + P], W1[:, P * j:P * j + P], c.ident[:])
            mm.then_inc(turned, 1)
            pe.wait_ge(w1T_done, 1)
            for j in range(HC):
                mm = pe.matmul(gram_ps[:, 0:P], W1T[:, P * j:P * j + P], W1T[:, P * j:P * j + P],
                               start=(j == 0), stop=(j == HC - 1))
            mm.then_inc(gram_summed, 1)

        @block.vector
        def _(dve):
            for n in range(len(loads)):
                dve.wait_ge(loaded[n], 16)
            dve.wait_ge(pool_made, 1)
            dve.tensor_tensor(c.a_W1w[:], W1[:], w_bc[:], ALU.mult)
            dve.tensor_tensor(c.a_b1w[:], b1_col[:], w_col[:], ALU.mult)
            dve.tensor_tensor_reduce(out=junk[:], in0=W1[:], in1=b1_bc[:], scale=1.0, scalar=0.0, op0=ALU.mult,
                                     op1=ALU.add, accum_out=cross[:, 0:1]).then_inc(made, 1)
            dve.wait_ge(made, 1)
            dve.tensor_scalar(c.a_cross[:], cross[:, 0:1], 2.0, None, ALU.mult)
            dve.tensor_tensor_reduce(out=junk[:], in0=b1_bc[:], in1=b1_bc[:], scale=1.0, scalar=0.0, op0=ALU.mult,
                                     op1=ALU.add, accum_out=cross[:, 1:2]).then_inc(made, 1)
            dve.wait_ge(made, 2)
            dve.tensor_scalar(c.a_b1sq[:], cross[:, 1:2], H * RMS_EPS, None, ALU.add)
            for m in range(2):
                dve.tensor_scalar(c.a_eps_ident[:, 384 * m:384 * m + P], c.ident[:], eps_bc[:, 0:1], None, ALU.mult)
            dve.wait_ge(turned, 1)
            dve.tensor_copy(W1T[:], turn_ps[:]).then_inc(w1T_done, 1)
            dve.wait_ge(gram_summed, 1)
            dve.tensor_copy(c.a_gram[:], gram_ps[:, 0:P]).then_inc(made, 1)
            dve.wait_ge(made, 3)


def gnn_mlp_layer(nc, sem, sb, psum, c, x_dram, adj_dram, xs, B, gate):
    H = 512
    HC = H // P
    U = 2

    adj = sb("a_adj", [P, U, 2, 256])
    stats = sb("a_stats", [P, U, 2, 6])
    meanvar = sb("a_meanvar", [P, U, 2, 2])
    var_eps = sb("a_var_eps", [P, U, 2])
    rstd = sb("a_rstd", [P, U, 2])
    xln = sb("a_xln", [P, U, 2, D])
    adjT = sb("a_adjT", [P, U, 512])
    aggT = sb("a_aggT", [P, U, 256])
    prod = sb("a_prod", [P, U, 256])
    sumsq = sb("a_sumsq", [P, U, 2])
    rms_col = sb("a_rms_col", [P, U, 2])
    rms_diag = sb("a_rms_diag", [P, U, 256])
    rms = sb("a_rms", [P, U, 256])
    hid = sb("a_hid", [P, U, HC * 256])
    act_hid = sb("a_act_hid", [P, U, HC * 256])
    x_b2 = sb("a_x_b2", [P, U, 2, D])

    adjT_ps = psum("a_adjT_ps")
    agg_ps = psum("a_agg_ps")
    ss_ps = psum("a_ss_ps")
    rms_ps = psum("a_rms_ps")
    out_ps = psum("a_out_ps")
    hid_ps = [psum(f"a_hid_ps{j}") for j in range(2)]

    x_in = [sem(f"a_x_in{i}") for i in range(U)]
    adj_in = [sem(f"a_adj_in{i}") for i in range(U)]
    stats_done = sem("a_stats_done")
    meanvar_done = sem("a_meanvar_done")
    var_eps_done = sem("a_var_eps_done")
    rstd_done = sem("a_rstd_done")
    xln_done = sem("a_xln_done")
    adj_turned = sem("a_adj_turned")
    adjT_done = sem("a_adjT_done")
    agg_summed = sem("a_agg_summed")
    aggT_done = sem("a_aggT_done")
    quad_summed = sem("a_quad_summed")
    prod_done = sem("a_prod_done")
    ss_summed = sem("a_ss_summed")
    sumsq_done = sem("a_sumsq_done")
    rms_col_done = sem("a_rms_col_done")
    rms_diag_done = sem("a_rms_diag_done")
    rms_spread = sem("a_rms_spread")
    rms_done = sem("a_rms_done")
    hid_summed = sem("a_hid_summed")
    hid_done = sem("a_hid_done")
    silu_done = sem("a_silu_done")
    out_summed = sem("a_out_summed")
    x_b2_done = sem("a_x_b2_done")
    x_done = sem("a_x_done")

    adj_rows = adj_dram.rearrange("b (h p) m -> b p h m", p=P)

    lag = dict(stats=2, meanvar=2, rstd=3, xln=3, adj_turn=2, adjT=3, agg=4, aggT=4, quad=4, prod=4, ss=5, sumsq=5,
               rms_col=5, rms_diag=5, rms_spread=6, rms=6, hid_ps=5, hid=6, silu=6, x_b2=6, out=7, x=7,
               gate_stats=9, gate_rstd=10, neg_mean=10, gate_xln=11, gate_turn=13, gate_xT=13, gate_sum=13,
               logits=14)
    DEPTH = max(lag.values())

    def at(i, u, part):
        return Item(i, u, lag[part], U, B)

    with nc.Block() as block:

        @block.sync
        def _(sp):
            def step(i, u):
                b = Item(i, u, 0, U, B)
                if b.alive:
                    if b.after(2):
                        sp.wait_ge(adj_turned, b.n - 1)
                        sp.wait_ge(xln_done, b.n - 1)
                    sp.dma_start(tiles(xs, b.n, 2), rows(x_dram, b.n, 2)).then_inc(x_in[b.pair], 16)
                    sp.dma_start(adj[:, b.pair], adj_rows[bass.ds(b.n, 1)].rearrange("a p h m -> (a p) h m")
                                 ).then_inc(adj_in[b.pair], 16)
                if b.known:
                    gate.sync_weights(sp, b.n)
                gate.sync(sp, at(i, u, "gate_xln"))
            steps(sp, B, lag["gate_xln"], U, step)
            gate.sync_end(sp)

        @block.gpsimd
        def _(pool):
            def step(i, u):
                b = at(i, u, "rstd")
                if b.alive:
                    if b.after(2):
                        pool.wait_ge(xln_done, b.n - 1)
                    pool.wait_ge(var_eps_done, b.n + 1)
                    pool.tensor_tensor(rstd[:, b.pair], var_eps[:, b.pair], c.neg_half[:, 0:2], ALU.pow
                                       ).then_inc(rstd_done, 1)
                gate.pool_rstd(pool, at(i, u, "gate_rstd"))
                b = at(i, u, "x_b2")
                if b.alive:
                    if b.after(2):
                        pool.wait_ge(x_done, b.n - 1)
                    pool.tensor_tensor(x_b2[:, b.pair], tiles(xs, b.n, 2), c.a_b2[:], ALU.add
                                       ).then_inc(x_b2_done, 1)
                b = at(i, u, "rms_col")
                if b.alive:
                    if b.after(2):
                        pool.wait_ge(rms_diag_done, b.n - 1)
                    pool.wait_ge(sumsq_done, b.n + 1)
                    pool.tensor_tensor(rms_col[:, b.pair], sumsq[:, b.pair], c.neg_half[:, 0:2], ALU.pow
                                       ).then_inc(rms_col_done, 1)
            steps(pool, B, lag["gate_rstd"], U, step)

        @block.tensor
        def _(pe):
            def hidden(b, k):
                if b.alive:
                    if b.after(1):
                        pe.wait_ge(hid_done, 2 * b.n - 1 + k)
                    for j in range(2 * k, 2 * k + 2):
                        mm = pe.matmul(hid_ps[k][:, 256 * (j % 2):256 * (j % 2) + 256],
                                       c.a_W1w[:, P * j:P * j + P], aggT[:, b.pair], start=True, stop=True)
                    mm.then_inc(hid_summed, 1)

            def step(i, u):
                b = at(i, u, "rms_spread")
                if b.alive:
                    pe.wait_ge(rms_diag_done, b.n + 1)
                    if b.after(1):
                        pe.wait_ge(rms_done, b.n)
                    pe.matmul(rms_ps[:, 0:256], c.ones[:], rms_diag[:, b.pair], start=True, stop=True
                              ).then_inc(rms_spread, 1)
                b = at(i, u, "agg")
                if b.alive:
                    pe.wait_ge(adjT_done, b.n + 1)
                    pe.wait_ge(xln_done, b.n + 1)
                    if b.after(1):
                        pe.wait_ge(prod_done, b.n)
                    for m in range(2):
                        mm = pe.matmul(agg_ps[:, 0:256], xln[:, b.pair, m], adjT[:, b.pair, 256 * m:256 * m + 256],
                                       start=(m == 0), stop=(m == 1))
                    mm.then_inc(agg_summed, 1)
                b = at(i, u, "ss")
                if b.alive:
                    pe.wait_ge(prod_done, b.n + 1)
                    if b.after(1):
                        pe.wait_ge(sumsq_done, b.n)
                    for h in range(2):
                        mm = pe.matmul(ss_ps[:, h:h + 1], prod[:, b.pair, P * h:P * h + P], c.ones[:, 0:1],
                                       start=True, stop=True)
                    mm.then_inc(ss_summed, 1)
                gate.tensor_turn(pe, at(i, u, "gate_turn"))
                b = at(i, u, "out")
                if b.alive:
                    pe.wait_ge(silu_done, 2 * b.n + 2)
                    if b.after(1):
                        pe.wait_ge(x_done, b.n)
                    for h in range(2):
                        for j in range(HC):
                            mm = pe.matmul(out_ps[:, P * h:P * h + P],
                                           act_hid[:, b.pair, 256 * j + P * h:256 * j + P * h + P],
                                           c.a_W2[:, j], start=(j == 0), stop=(j == HC - 1))
                    mm.then_inc(out_summed, 1)
                hidden(at(i, u, "hid_ps"), 0)
                b = at(i, u, "quad")
                if b.alive:
                    pe.wait_ge(aggT_done, b.n + 1)
                    pe.matmul(agg_ps[:, 256:512], c.a_gram[:], aggT[:, b.pair], start=True, stop=True
                              ).then_inc(quad_summed, 1)
                gate.tensor_scores(pe, at(i, u, "gate_sum"))
                b = at(i, u, "adj_turn")
                if b.alive:
                    pe.wait_ge(adj_in[b.pair], (b.round + 1) * 16)
                    if b.after(1):
                        pe.wait_ge(adjT_done, b.n)
                    for m in range(2):
                        for h in range(2):
                            mm = pe.transpose(adjT_ps[:, 256 * m + P * h:256 * m + P * h + P],
                                              adj[:, b.pair, h, P * m:P * m + P], c.ident[:])
                    mm.then_inc(adj_turned, 1)
                hidden(at(i, u, "hid_ps"), 1)
            steps(pe, B, DEPTH, U, step)

        @block.scalar
        def _(act):
            def silu(b, k):
                if b.alive:
                    act.wait_ge(hid_done, 2 * b.n + 1 + k)
                    if b.after(2):
                        act.wait_ge(out_summed, b.n - 1)
                    act.activation(act_hid[:, b.pair, 512 * k:512 * k + 512], hid[:, b.pair, 512 * k:512 * k + 512],
                                   ACT.Silu).then_inc(silu_done, 1)

            def step(i, u):
                b = at(i, u, "rms")
                if b.alive:
                    act.wait_ge(rms_spread, b.n + 1)
                    if b.after(2):
                        act.wait_ge(hid_done, 2 * b.n - 2)
                    act.copy(rms[:, b.pair], rms_ps[:, 0:256]).then_inc(rms_done, 1)
                gate.scalar_copy(act, at(i, u, "gate_xT"))
                b = at(i, u, "aggT")
                if b.alive:
                    act.wait_ge(agg_summed, b.n + 1)
                    if b.after(2):
                        act.wait_ge(hid_summed, 2 * b.n - 2)
                        act.wait_ge(prod_done, b.n - 1)
                    act.copy(aggT[:, b.pair], agg_ps[:, 0:256]).then_inc(aggT_done, 1)
                silu(at(i, u, "silu"), 0)
                b = at(i, u, "rms_diag")
                if b.alive:
                    act.wait_ge(rms_col_done, b.n + 1)
                    if b.after(2):
                        act.wait_ge(rms_spread, b.n - 1)
                    for h in range(2):
                        op = act.activation(rms_diag[:, b.pair, P * h:P * h + P], c.ident[:], ACT.Copy,
                                            scale=rms_col[:, b.pair, h:h + 1])
                    op.then_inc(rms_diag_done, 1)
                silu(at(i, u, "silu"), 1)
                gate.scalar_norm(act, at(i, u, "gate_xln"))
            steps(act, B, lag["gate_xT"], U, step)

        @block.vector
        def _(dve):
            def hidden(b, k):
                if b.alive:
                    if k == 0:
                        dve.wait_ge(rms_done, b.n + 1)
                    dve.wait_ge(hid_summed, 2 * b.n + 1 + k)
                    if b.after(2):
                        dve.wait_ge(silu_done, 2 * b.n - 3 + k)
                    for j in range(2 * k, 2 * k + 2):
                        op = dve.scalar_tensor_tensor(hid[:, b.pair, 256 * j:256 * j + 256],
                                                      hid_ps[k][:, 256 * (j % 2):256 * (j % 2) + 256],
                                                      c.a_b1w[:, j:j + 1], rms[:, b.pair], ALU.add, ALU.mult)
                    op.then_inc(hid_done, 1)

            def step(i, u):
                gate_stats = at(i, u, "gate_stats")
                gate.vector_wait(dve, gate_stats, x_done)
                gate.vector_add(dve, at(i, u, "logits"))
                gate.vector_stats(dve, gate_stats)
                b = at(i, u, "adjT")
                if b.alive:
                    if b.after(2):
                        dve.wait_ge(agg_summed, b.n - 1)
                    dve.wait_ge(adj_turned, b.n + 1)
                    dve.tensor_tensor(adjT[:, b.pair], adjT_ps[:], c.a_eps_ident[:], ALU.add
                                      ).then_inc(adjT_done, 1)
                gate.vector_aggregate(dve, gate_stats)
                hidden(at(i, u, "hid"), 0)
                gate.vector_var_eps(dve, gate_stats)
                b = at(i, u, "sumsq")
                if b.alive:
                    dve.wait_ge(ss_summed, b.n + 1)
                    if b.after(2):
                        dve.wait_ge(rms_col_done, b.n - 1)
                    dve.tensor_scalar(sumsq[:, b.pair], ss_ps[:, 0:2], c.a_b1sq[:, 0:1], 1.0 / H, ALU.add, ALU.mult
                                      ).then_inc(sumsq_done, 1)
                b = at(i, u, "xln")
                if b.alive:
                    dve.wait_ge(rstd_done, b.n + 1)
                    for h in range(2):
                        op = dve.tensor_scalar(xln[:, b.pair, h], tiles(xs, b.n, 2)[:, h], meanvar[:, b.pair, h, 0:1],
                                               rstd[:, b.pair, h:h + 1], ALU.subtract, ALU.mult)
                    op.then_inc(xln_done, 1)
                hidden(at(i, u, "hid"), 1)
                b = at(i, u, "prod")
                if b.alive:
                    dve.wait_ge(quad_summed, b.n + 1)
                    if b.after(2):
                        dve.wait_ge(ss_summed, b.n - 1)
                    dve.scalar_tensor_tensor(prod[:, b.pair], agg_ps[:, 256:512], c.a_cross[:, 0:1], aggT[:, b.pair],
                                             ALU.add, ALU.mult).then_inc(prod_done, 1)
                f = at(i, u, "stats")
                if f.alive:
                    dve.wait_ge(x_in[f.pair], (f.round + 1) * 16)
                    for h in range(2):
                        op = dve.bn_stats(stats[:, f.pair, h], tiles(xs, f.n, 2)[:, h])
                    op.then_inc(stats_done, 1)
                    dve.wait_ge(stats_done, f.n + 1)
                gate.vector_neg_mean(dve, at(i, u, "neg_mean"))
                b = at(i, u, "x")
                if b.alive:
                    dve.wait_ge(out_summed, b.n + 1)
                    dve.wait_ge(x_b2_done, b.n + 1)
                    dve.tensor_tensor(tiles(xs, b.n, 2), out_ps[:, 0:256].rearrange("p (h d) -> p h d", h=2),
                                      x_b2[:, b.pair], ALU.add).then_inc(x_done, 1)
                if f.alive:
                    for h in range(2):
                        op = dve.bn_aggr(meanvar[:, f.pair, h], stats[:, f.pair, h])
                    op.then_inc(meanvar_done, 1)
                    dve.wait_ge(meanvar_done, f.n + 1)
                    if f.after(2):
                        dve.wait_ge(rstd_done, f.n - 1)
                    dve.tensor_scalar(var_eps[:, f.pair], meanvar[:, f.pair, :, 1], LN_EPS, None, ALU.add
                                      ).then_inc(var_eps_done, 1)
            steps(dve, B, DEPTH, U, step)
            gate.vector_end(dve)


EXPERT_PAD = 4


def expert_tiles(T, E):
    return -(-(2 * T + E) // 8) * 8


LOAD_PARTS = 8


def load_experts(eng, loaded, c, w, names, E, F, part):
    W1, b1, W2, b2 = (w[name] for name in names)
    n = E // LOAD_PARTS
    own = slice(part * n, part * n + n)
    K = F // P
    eng.dma_start(c.W1[:, part * n * F:(part + 1) * n * F].rearrange("p (e f) -> p e f", e=n),
                  W1[own].rearrange("e d f -> d e f")).then_inc(loaded[0], 16)
    eng.dma_start(c.W2[:, part * n * K * D:(part + 1) * n * K * D].rearrange("p (n d) -> p n d", d=D),
                  W2[own].rearrange("e (k p) d -> p (e k) d", p=P)).then_inc(loaded[1], 16)
    if part == LOAD_PARTS - 1:
        eng.dma_start(c.b1[:, 0:E * F // P], b1.rearrange("e (k p) -> p (e k)", p=P), allow_slow_non_contiguous=True
                      ).then_inc(loaded[2], 16)
        eng.dma_start(c.b2[:, 0:E * D], b2.rearrange("e d -> (e d)").partition_broadcast(P)).then_inc(loaded[3], 16)


class GateScores:

    def __init__(self, sem, sb, psum, c, w, pre, xs, xln_dram, logits, names, B, E, F):
        self.c, self.w, self.B, self.E, self.F = c, w, B, E, F
        self.xs, self.xln_dram, self.logits, self.names = xs, xln_dram, logits, names
        self.stats = sb(pre + "stats", [P, 2, 2, 6])
        self.meanvar = sb(pre + "meanvar", [P, 2, 2, 2])
        self.var_eps = sb(pre + "var_eps", [P, 2, 2])
        self.rstd = sb(pre + "rstd", [P, 2, 2])
        self.neg_mean = sb(pre + "neg_mean", [P, 2, 2])
        self.xln = sb(pre + "xln", [P, 2, 2, D])
        self.xT = sb(pre + "xT", [P, 2, 256])
        self.Wg = sb(pre + "Wg", [P, E])
        self.bg = sb(pre + "bg", [P, 2, E])
        self.ps = psum(pre + "ps")
        self.experts_in = [sem(f"{pre}experts_in{i}") for i in range(4)]
        self.gate_in = [sem(f"{pre}gate_in{i}") for i in range(3)]
        self.xln_out = [sem(f"{pre}xln_out{i}") for i in range(2)]
        self.stats_done = sem(pre + "stats_done")
        self.meanvar_done = sem(pre + "meanvar_done")
        self.var_eps_done = sem(pre + "var_eps_done")
        self.rstd_done = sem(pre + "rstd_done")
        self.neg_mean_done = sem(pre + "neg_mean_done")
        self.xln_done = sem(pre + "xln_done")
        self.x_turned = sem(pre + "x_turned")
        self.xT_done = sem(pre + "xT_done")
        self.gate_summed = sem(pre + "gate_summed")
        self.gate_done = sem(pre + "gate_done")

    def sync_weights(self, sp, n):
        gate_w, gate_b, *expert_names = self.names
        if n == 1:
            sp.dma_start(self.Wg[:], self.w[gate_w]).then_inc(self.gate_in[0], 16)
            for k in range(2):
                sp.dma_start(self.bg[:, k], self.w[gate_b].partition_broadcast(P)).then_inc(self.gate_in[1 + k], 16)
        if 0 <= n - 2 < LOAD_PARTS:
            load_experts(sp, self.experts_in, self.c, self.w, expert_names, self.E, self.F, n - 2)

    def sync(self, sp, b):
        if b.alive:
            sp.wait_ge(self.xln_done, b.n + 1)
            sp.dma_start(rows(self.xln_dram, b.n, 2), self.xln[:, b.pair]).then_inc(self.xln_out[b.pair], 16)

    def sync_end(self, sp):
        for k in range(2):
            sp.wait_ge(self.xln_out[k], self.B // 2 * 16)
        for k in range(4):
            sp.wait_ge(self.experts_in[k], 16 * (LOAD_PARTS if k < 2 else 1))

    def pool_rstd(self, pool, f):
        if f.alive:
            if f.after(2):
                pool.wait_ge(self.xln_done, f.n - 1)
            pool.wait_ge(self.var_eps_done, f.n + 1)
            pool.tensor_tensor(self.rstd[:, f.pair], self.var_eps[:, f.pair], self.c.neg_half[:, 0:2], ALU.pow
                               ).then_inc(self.rstd_done, 1)

    def tensor_scores(self, pe, a):
        if a.alive:
            if a.known and a.n == 0:
                pe.wait_ge(self.gate_in[0], 16)
            pe.wait_ge(self.xT_done, a.n + 1)
            for k in range(2):
                mm = pe.matmul(self.ps[:, 256 + self.E * k:256 + self.E * k + self.E],
                               self.xT[:, a.pair, P * k:P * k + P], self.Wg[:], start=True, stop=True)
            mm.then_inc(self.gate_summed, 1)

    def tensor_turn(self, pe, b):
        if b.alive:
            pe.wait_ge(self.xln_done, b.n + 1)
            if b.after(1):
                pe.wait_ge(self.gate_done, b.n)
            for k in range(2):
                mm = pe.transpose(self.ps[:, P * k:P * k + P], self.xln[:, b.pair, k], self.c.ident[:])
            mm.then_inc(self.x_turned, 1)

    def scalar_norm(self, act, b):
        if b.alive:
            act.wait_ge(self.neg_mean_done, b.n + 1)
            if b.after(2):
                act.wait_ge(self.x_turned, b.n - 1)
                act.wait_ge(self.xln_out[b.pair], b.round * 16)
            for k in range(2):
                op = act.activation(self.xln[:, b.pair, k], tiles(self.xs, b.n, 2)[:, k], ACT.Identity,
                                    bias=self.neg_mean[:, b.pair, k:k + 1], scale=self.rstd[:, b.pair, k:k + 1])
            op.then_inc(self.xln_done, 1)

    def scalar_copy(self, act, b):
        if b.alive:
            act.wait_ge(self.x_turned, b.n + 1)
            if b.after(2):
                act.wait_ge(self.gate_summed, b.n - 1)
            act.copy(self.xT[:, b.pair], self.ps[:, 0:256]).then_inc(self.xT_done, 1)

    def vector_wait(self, dve, f, x_done):
        if f.alive:
            if f.after(2):
                dve.wait_ge(self.meanvar_done, f.n - 1)
            dve.wait_ge(x_done, f.n + 1)

    def vector_stats(self, dve, f):
        if f.alive:
            for k in range(2):
                op = dve.bn_stats(self.stats[:, f.pair, k], tiles(self.xs, f.n, 2)[:, k])
            op.then_inc(self.stats_done, 1)
            dve.wait_ge(self.stats_done, f.n + 1)

    def vector_aggregate(self, dve, f):
        if f.alive:
            for k in range(2):
                op = dve.bn_aggr(self.meanvar[:, f.pair, k], self.stats[:, f.pair, k])
            op.then_inc(self.meanvar_done, 1)

    def vector_var_eps(self, dve, f):
        if f.alive:
            dve.wait_ge(self.meanvar_done, f.n + 1)
            if f.after(2):
                dve.wait_ge(self.rstd_done, f.n - 1)
            dve.tensor_scalar(self.var_eps[:, f.pair], self.meanvar[:, f.pair, :, 1], LN_EPS, None, ALU.add
                              ).then_inc(self.var_eps_done, 1)

    def vector_add(self, dve, a):
        if a.alive:
            if a.known and a.n == 0:
                for k in range(2):
                    dve.wait_ge(self.gate_in[1 + k], 16)
            dve.wait_ge(self.gate_summed, a.n + 1)
            dve.tensor_tensor(tiles(self.logits, a.n, 2),
                              self.ps[:, 256:256 + 2 * self.E].rearrange("p (k e) -> p k e", k=2),
                              self.bg[:], ALU.add).then_inc(self.gate_done, 1)

    def vector_neg_mean(self, dve, b):
        if b.alive:
            dve.wait_ge(self.rstd_done, b.n + 1)
            if b.after(2):
                dve.wait_ge(self.xln_done, b.n - 1)
            dve.scalar_tensor_tensor(self.neg_mean[:, b.pair], self.meanvar[:, b.pair, :, 0], -1.0,
                                     self.rstd[:, b.pair], ALU.mult, ALU.mult).then_inc(self.neg_mean_done, 1)

    def vector_end(self, dve):
        dve.wait_ge(self.gate_done, self.B)


def route(nc, sem, sb, psum, c, pre, logits, r, T, E):
    NT = expert_tiles(T, E)
    TE = T * E
    G = 4
    R = 4
    NB = -(-TE // 512)
    TB = T // NB

    def work(name, shape, dt=F32):
        return sb(pre + name, shape, dt)

    best = work("best", [P, 2, T])
    hit = work("hit", [P, T, E])
    rank = work("rank", [P, T, E])
    top_rank = work("top_rank", [P, T])
    chosen = [work(f"chosen{k}", [P, T, E]) for k in range(2)]
    rest = work("rest", [P, T, E])
    order = work("order", [P, E])
    gap = work("gap", [P, T])
    gap_exp = work("gap_exp", [P, T])
    denom = work("denom", [P, T])
    taken = work("taken", [P, TE], BF16)
    count = work("count", [P, E, T])
    zeros = work("zeros", [P, TE])
    running = work("running", [P, E, T])
    start = work("start", [P, E + 1])
    total = work("total", [P, E])
    tiles_i = work("tiles_i", [P, 2, E], I32)
    n_tiles = work("n_tiles", [P, E])
    tile_end = work("tile_end", [P, E])
    shift = work("shift", [P, E])
    offset = work("offset", [P, E, T])
    place = work("place", [P, T, E])
    slot_f = work("slot_f", [P, T, 2])
    row_i = work("row_i", [P, T, 2], I32)
    tile_i = work("tile_i", [P, T, 2], I32)
    row_f = work("row_f", [P, 2 * T])
    tile_f = work("tile_f", [P, 2 * T])
    ended = work("ended", [P, NT, E])
    expert_f = work("expert_f", [P, NT])
    is_row = work("is_row", [P, R, G, P], BF16)
    row_part = work("row_part", [P, R, G, P], BF16)
    row_tile = work("row_tile", [P, R, G, P], BF16)
    is_tile = work("is_tile", [P, R, G, NT], BF16)
    part_f = work("part_f", [P, NT])
    token_f = work("token_f", [P, NT])

    before_ps = [psum(f"{pre}before_ps{k}") for k in range(NB)]
    count_ps = [psum(f"{pre}count_ps{k}") for k in range(NB)]
    tile_ps = psum(pre + "tile_ps")
    part_ps = psum(pre + "part_ps")

    chain = sem(pre + "chain")
    gap_done = sem(pre + "gap_done")
    exp_done = sem(pre + "exp_done")
    taken_done = sem(pre + "taken_done")
    counted = sem(pre + "counted")
    hot_done = sem(pre + "hot_done")
    scaled_done = sem(pre + "scaled_done")
    hot_used = sem(pre + "hot_used")

    with nc.Block() as block:

        @block.scalar
        def _(act):
            act.wait_ge(gap_done, 1)
            act.activation(gap_exp[:], gap[:], ACT.Exp).then_inc(exp_done, 1)

            def step(i, u):
                a = Item(i, u, 0, R, 2 * T // G)
                if a.alive:
                    act.wait_ge(hot_done, a.n + 1)
                    if a.after(R):
                        act.wait_ge(hot_used, a.n - R + 1)
                    act.activation(row_part[:, a.slot], is_row[:, a.slot], ACT.Copy, scale=c.part_no[:, 0:1])
                    for g in range(0, G, 2):
                        op = act.activation(row_tile[:, a.slot, g:g + 2], is_row[:, a.slot, g:g + 2], ACT.Copy,
                                            scale=c.iota_row[:, bass.ds(a.n * (G // 2) + g // 2, 1)])
                    op.then_inc(scaled_done, 1)
            steps(act, 2 * T // G, 0, R, step)

        @block.tensor
        def _(pe):
            pe.wait_ge(taken_done, 1)
            for k in range(NB):
                pe.matmul(before_ps[k][:, 0:TB * E], c.before[:], taken[:, TB * E * k:TB * E * (k + 1)],
                          start=True, stop=True)
                mm = pe.matmul(count_ps[k][:, 0:TB * E], c.ones_bf[:], taken[:, TB * E * k:TB * E * (k + 1)],
                               start=True, stop=True)
            mm.then_inc(counted, 1)

            def step(i, u):
                a = Item(i, u, 1, R, 2 * T // G)
                if a.alive:
                    pe.wait_ge(scaled_done, a.n + 1)
                    for g in range(G):
                        first = a.known and a.n == 0 and g == 0
                        last = a.known and a.n == 2 * T // G - 1 and g == G - 1
                        pe.matmul(tile_ps[:, 0:NT], row_tile[:, a.slot, g], is_tile[:, a.slot, g], start=first, stop=last)
                        mm = pe.matmul(part_ps[:, 0:NT], row_part[:, a.slot, g], is_tile[:, a.slot, g],
                                       start=first, stop=last)
                    mm.then_inc(hot_used, 1)
            steps(pe, 2 * T // G, 1, R, step)

        @block.vector
        def _(dve):
            made = [0]

            def link(op):
                made[0] += 1
                op.then_inc(chain, 1)
                dve.wait_ge(chain, made[0])

            def over_e(v):
                return v.unsqueeze(2).to_broadcast([P, v.shape[1], E])

            def over_t(v, n):
                return v.unsqueeze(1).to_broadcast([P, n, v.shape[1]])

            dve.memset(zeros[:], 0.0)
            dve.memset(r.expert[:, 0:EXPERT_PAD], 0)
            dve.memset(r.expert[:, NT + EXPERT_PAD:NT + 16], 0)
            dve.memset(start[:, 0:1], 0.0)
            link(dve.tensor_scalar(order[:], c.iota_row[:, 0:E], -1.0, float(E), ALU.mult, ALU.add))
            left = logits
            for k in range(2):
                link(dve.tensor_reduce(best[:, k], left[:], AX_X, ALU.max))
                link(dve.tensor_tensor(hit[:], left[:], over_e(best[:, k]), ALU.is_equal))
                link(dve.tensor_tensor(rank[:], hit[:], over_t(order[:], T), ALU.mult))
                link(dve.tensor_reduce(top_rank[:], rank[:], AX_X, ALU.max))
                link(dve.tensor_tensor(chosen[k][:], rank[:], over_e(top_rank[:]), ALU.is_equal))
                if k == 0:
                    link(dve.scalar_tensor_tensor(rest[:], chosen[0][:], -BIG, logits[:], ALU.mult, ALU.add))
                    left = rest
            dve.tensor_tensor(gap[:], best[:, 1], best[:, 0], ALU.subtract).then_inc(gap_done, 1)
            dve.tensor_tensor(taken[:].rearrange("p (t e) -> p t e", e=E), chosen[0][:], chosen[1][:], ALU.add
                              ).then_inc(taken_done, 1)
            dve.wait_ge(exp_done, 1)
            link(dve.tensor_scalar(denom[:], gap_exp[:], 1.0, None, ALU.add))
            link(dve.reciprocal(r.weight[:, :, 0], denom[:]))
            dve.tensor_tensor(r.weight[:, :, 1], gap_exp[:], r.weight[:, :, 0], ALU.mult)
            dve.wait_ge(counted, 1)
            for k in range(NB):
                op = dve.tensor_copy(count[:, :, TB * k:TB * k + TB],
                                     count_ps[k][:, 0:TB * E].rearrange("p (t e) -> p e t", e=E))
            link(op)
            link(dve.tensor_tensor_scan(running[:].rearrange("p e t -> p (e t)"),
                                        count[:].rearrange("p e t -> p (e t)"), zeros[:], 0.0, ALU.add, ALU.add))
            link(dve.tensor_copy(start[:, 1:E + 1], running[:, :, T - 1]))
            link(dve.tensor_tensor(total[:], start[:, 1:E + 1], start[:, 0:E], ALU.subtract))
            link(dve.tensor_scalar(tiles_i[:, 0], total[:], float(P - 1), None, ALU.add))
            link(dve.tensor_scalar(tiles_i[:, 1], tiles_i[:, 0], 7, None, ALU.arith_shift_right))
            link(dve.tensor_copy(n_tiles[:], tiles_i[:, 1]))
            link(dve.tensor_tensor_scan(tile_end[:], n_tiles[:], zeros[:, 0:E], 0.0, ALU.add, ALU.add))
            link(dve.tensor_tensor(total[:], tile_end[:], n_tiles[:], ALU.subtract))
            link(dve.scalar_tensor_tensor(shift[:], total[:], float(P), start[:, 0:E], ALU.mult, ALU.subtract))
            link(dve.tensor_tensor(offset[:], running[:], count[:], ALU.subtract))
            link(dve.tensor_tensor(offset[:], offset[:], shift[:].unsqueeze(2).to_broadcast([P, E, T]), ALU.add))
            for k in range(NB):
                op = dve.tensor_tensor(place[:, TB * k:TB * k + TB],
                                       before_ps[k][:, 0:TB * E].rearrange("p (t e) -> p t e", e=E),
                                       offset[:, :, TB * k:TB * k + TB].rearrange("p e t -> p t e"), ALU.add)
            link(op)
            for k in range(2):
                link(dve.tensor_tensor(rank[:], place[:], chosen[k][:], ALU.mult))
                link(dve.tensor_reduce(slot_f[:, :, k], rank[:], AX_X, ALU.add))
            link(dve.tensor_copy(r.slot[:], slot_f[:]))
            dve.tensor_scalar(row_i[:], r.slot[:], P - 1, None, ALU.bitwise_and)
            link(dve.tensor_scalar(tile_i[:], r.slot[:], 7, None, ALU.arith_shift_right))
            dve.tensor_copy(row_f[:], row_i[:].rearrange("p t k -> p (t k)"))
            dve.tensor_copy(tile_f[:], tile_i[:].rearrange("p t k -> p (t k)"))
            dve.memset(r.token[:, NT:NT + 1], 0)
            link(dve.tensor_tensor(ended[:], over_t(tile_end[:], NT), over_e(c.iota_row[:, 0:NT]), ALU.is_le))
            link(dve.tensor_reduce(expert_f[:], ended[:], AX_X, ALU.add))
            link(dve.tensor_scalar(r.expert[:, EXPERT_PAD:NT + EXPERT_PAD], expert_f[:], float(E - 1), None, ALU.min))

            def step(i, u):
                a = Item(i, u, 0, R, 2 * T // G)
                if not a.alive:
                    return
                if a.after(R):
                    dve.wait_ge(hot_used, a.n - R + 1)
                for g in range(G):
                    col = bass.ds(a.n * G + g, 1)
                    dve.tensor_scalar(is_row[:, a.slot, g], c.iota_row_bf[:, 0:P], row_f[:, col], None, ALU.is_equal)
                    op = dve.tensor_scalar(is_tile[:, a.slot, g], c.iota_row_bf[:, 0:NT], tile_f[:, col], None,
                                           ALU.is_equal)
                op.then_inc(hot_done, 1)
            steps(dve, 2 * T // G, 0, R, step)
            dve.wait_ge(hot_used, 2 * T // G)
            link(dve.tensor_copy(part_f[:], part_ps[:, 0:NT]))
            link(dve.scalar_tensor_tensor(token_f[:], tile_ps[:, 0:NT], float(P), part_f[:], ALU.mult, ALU.add))
            link(dve.tensor_copy(r.token[:, 0:NT], token_f[:]))


def run_experts(nc, sem, sb, psum, c, pre, xln_dram, y_dram, r, T, E, F, gelu):
    U = 8
    S = 4
    NT = expert_tiles(T, E)
    K = F // P
    index = sb(pre + "index", [P, U], I32)
    x = sb(pre + "x", [P, U, D])
    xT = sb(pre + "xT", [P, 2, P])
    W1 = sb(pre + "W1", [P, 2, F])
    hidT = sb(pre + "hidT", [P, 2, F])
    y = sb(pre + "y", [P, S, D])
    xT_ps = [psum(f"{pre}xT_ps{i}") for i in range(2)]
    hidT_ps = [psum(f"{pre}hidT_ps{i}") for i in range(2)]
    y_ps = [psum(f"{pre}y_ps{i}") for i in range(2)]
    x_in = [sem(f"{pre}x_in{i}") for i in range(U)]
    y_out = [sem(f"{pre}y_out{i}") for i in range(S)]
    index_done = sem(pre + "index_done")
    x_turned = sem(pre + "x_turned")
    xT_done = sem(pre + "xT_done")
    W1_done = sem(pre + "W1_done")
    hid_summed = sem(pre + "hid_summed")
    hidT_done = sem(pre + "hidT_done")
    y_summed = sem(pre + "y_summed")
    y_done = sem(pre + "y_done")

    def load_window(engine, i, first, count):
        return nc.values_load_multi_w_load_instructions(r.expert[0:1, bass.ds(i * U + first, count)], engines=(engine,),
                                                        min_val=0, max_val=E - 1,
                                                        skip_runtime_bounds_check_because=
                                                        "route clamps every expert to 0 .. E - 1")[1]

    LAG_Y = EXPERT_PAD
    LAG_HID = 2
    LAG_X = 1

    with nc.Block() as block:

        @block.gpsimd
        def _(pool):
            pool.tensor_tensor(index[:, 0:1], r.token[:, 0:1], c.zero_i[:], ALU.add).then_inc(index_done, 1)

            def step(i, u):
                j = Item(i, u, 0, U, NT)
                if not j.alive:
                    return
                if j.after(7):
                    pool.wait_ge(x_turned, j.n - 6)
                pool.wait_ge(index_done, j.n + 1)
                nxt = (u + 1) % U
                pool.tensor_tensor(index[:, nxt:nxt + 1], r.token[:, bass.ds(j.n + 1, 1)], c.zero_i[:], ALU.add
                                   ).then_inc(index_done, 1)
                pool.indirect_dma_start(x[:, j.slot], None, xln_dram,
                                        bass.IndirectOffsetOnAxis(ap=index[:, u:u + 1], axis=0)
                                        ).then_inc(x_in[j.slot], 16)
            steps(pool, NT, 0, U, step)

        @block.tensor
        def _(pe):
            window = []

            def step(i, u):
                t = Item(i, u, LAG_X, U, NT)
                if t.alive:
                    pe.wait_ge(x_in[t.slot], (t.round + 1) * 16)
                    if t.after(2):
                        pe.wait_ge(xT_done, t.n - 1)
                    pe.transpose(xT_ps[t.pair][:, 0:P], x[:, t.slot], c.ident[:]).then_inc(x_turned, 1)
                if u == 0:
                    window[:] = load_window(mybir.EngineType.PE, i, 0, U)
                o = Item(i, u, LAG_Y, U, NT)
                if o.alive:
                    e = window[u]
                    pe.wait_ge(hidT_done, o.n + 1)
                    if o.after(2):
                        pe.wait_ge(y_done, o.n - 1)
                    for k in range(K):
                        mm = pe.matmul(y_ps[o.pair][:, 0:D], hidT[:, o.pair, P * k:P * k + P],
                                       c.W2[:, bass.ds(e * (K * D) + k * D, D)], start=(k == 0), stop=(k == K - 1))
                    mm.then_inc(y_summed, 1)
                h = Item(i, u, LAG_HID, U, NT)
                if h.alive:
                    pe.wait_ge(xT_done, h.n + 1)
                    pe.wait_ge(W1_done, h.n + 1)
                    if h.after(2):
                        pe.wait_ge(hidT_done, h.n - 1)
                    for k in range(K):
                        mm = pe.matmul(hidT_ps[h.pair][:, P * k:P * k + P], W1[:, h.pair, P * k:P * k + P],
                                       xT[:, h.pair], start=True, stop=True)
                    mm.then_inc(hid_summed, 1)
            steps(pe, NT, LAG_Y, U, step)

        @block.scalar
        def _(act):
            window = []

            def step(i, u):
                if u == 0:
                    window[:] = load_window(mybir.EngineType.Activation, i, LAG_Y - LAG_HID, U)
                h = Item(i, u, LAG_HID, U, NT)
                if h.alive:
                    e = window[u]
                    act.wait_ge(hid_summed, h.n + 1)
                    if h.after(2):
                        act.wait_ge(y_summed, h.n - 1)
                    for k in range(K):
                        op = act.activation(hidT[:, h.pair, P * k:P * k + P], hidT_ps[h.pair][:, P * k:P * k + P],
                                            ACT.Gelu if gelu else ACT.Relu, bias=c.b1[:, bass.ds(e * K + k, 1)])
                    op.then_inc(hidT_done, 1)
            steps(act, NT, LAG_HID, U, step)

        @block.vector
        def _(dve):
            window = []

            def step(i, u):
                if u == 0:
                    window[:] = load_window(mybir.EngineType.DVE, i, 0, U + LAG_Y - LAG_X)
                o = Item(i, u, LAG_Y, U, NT)
                if o.alive:
                    e = window[u]
                    dve.wait_ge(y_summed, o.n + 1)
                    if o.after(S):
                        dve.wait_ge(y_out[o.slot % S], (i * (U // S) + (u - LAG_Y) // S) * 16)
                    dve.tensor_tensor(y[:, o.slot % S], y_ps[o.pair][:, 0:D], c.b2[:, bass.ds(e * D, D)], ALU.add
                                      ).then_inc(y_done, 1)
                t = Item(i, u, LAG_X, U, NT)
                if t.alive:
                    e = window[u + LAG_Y - LAG_X]
                    if t.after(2):
                        dve.wait_ge(hid_summed, t.n - 1)
                    dve.tensor_copy(W1[:, t.pair], c.W1[:, bass.ds(e * F, F)]).then_inc(W1_done, 1)
                    dve.wait_ge(x_turned, t.n + 1)
                    dve.tensor_copy(xT[:, t.pair], xT_ps[t.pair][:, 0:P]).then_inc(xT_done, 1)
            steps(dve, NT, LAG_Y, U, step)

        @block.sync
        def _(sp):
            def step(i, u):
                o = Item(i, u, LAG_Y, U, NT)
                if o.alive:
                    sp.wait_ge(y_done, o.n + 1)
                    sp.dma_start(rows(y_dram, o.n, 1), y[:, o.slot % S].unsqueeze(1)).then_inc(y_out[o.slot % S], 16)
            steps(sp, NT, LAG_Y, U, step)
            for k in range(S):
                sp.wait_ge(y_out[k], NT // S * 16)


class Combine:

    def __init__(self, sem, sb, c, pre, r, y_dram, B):
        self.c, self.r, self.y_dram, self.B = c, r, y_dram, B
        self.index = sb(pre + "index", [P, 2, 4], I32)
        self.idle = sb(pre + "idle", [P, 1], I32)
        self.y = sb(pre + "y", [P, 2, 4, D])
        self.y_in = [sem(f"{pre}y_in{i}") for i in range(2)]
        self.index_done = sem(pre + "index_done")
        self.first_done = sem(pre + "first_done")
        self.x_done = sem(pre + "x_done")

    def pool_stage(self, pool, g):
        if g.alive:
            if g.after(2):
                pool.wait_ge(self.y_in[g.pair], g.round * 64)
            pool.tensor_tensor(self.index[:, g.pair].rearrange("p (t k) -> p t k", k=2), tiles(self.r.slot, g.n, 2),
                               self.c.zero_i[:].unsqueeze(2).to_broadcast([P, 2, 2]), ALU.add
                               ).then_inc(self.index_done, 1)

    def pool_wait(self, pool, g, idle):
        if g.alive:
            if g.after(2):
                pool.wait_ge(self.x_done, g.n - 1)
            pool.wait_ge(self.index_done, g.n + 1)
            if idle:
                pool.tensor_tensor(self.idle[:], self.c.zero_i[:], self.c.zero_i[:], ALU.add)

    def pool_gather(self, pool, g):
        if g.alive:
            for n in range(4):
                pool.indirect_dma_start(self.y[:, g.pair, n], None, self.y_dram,
                                        bass.IndirectOffsetOnAxis(ap=self.index[:, g.pair, n:n + 1], axis=0)
                                        ).then_inc(self.y_in[g.pair], 16)

    def vector_first(self, dve, a, base, dst):
        weight = tiles(self.r.weight, a.n, 2)
        dve.wait_ge(self.y_in[a.pair], (a.round + 1) * 64)
        for t in range(2):
            op = dve.scalar_tensor_tensor(dst[:, t], self.y[:, a.pair, 2 * t], weight[:, t, 0:1], base[:, t],
                                          ALU.mult, ALU.add)
        op.then_inc(self.first_done, 1)

    def vector_second(self, dve, a, dst):
        weight = tiles(self.r.weight, a.n, 2)
        dve.wait_ge(self.first_done, a.n + 1)
        for t in range(2):
            op = dve.scalar_tensor_tensor(dst[:, t], self.y[:, a.pair, 2 * t + 1], weight[:, t, 1:2], dst[:, t],
                                          ALU.mult, ALU.add)
        op.then_inc(self.x_done, 1)


def graph_attention_layer(nc, sem, sb, psum, c, w, adj_dram, xs, B, combine, gate):
    U = 2
    NEG_SLOPE = -0.2

    adj = sb("c_adj", [P, U, 512])
    penalty = sb("c_penalty", [P, U, 512])
    stats = sb("c_stats", [P, U, 2, 6])
    meanvar = sb("c_meanvar", [P, U, 2, 2])
    var_eps = sb("c_var_eps", [P, U, 2])
    rstd = sb("c_rstd", [P, U, 2])
    neg_mean = sb("c_neg_mean", [P, U, 2])
    xln = sb("c_xln", [P, U, 2, D])
    xln_all = sb("c_xln_all", [P, 2 * B, D])
    xT = sb("c_xT", [P, U, 256])
    xpT = sb("c_xpT", [P, U, 256])
    squares = sb("c_squares", [P, U, 512])
    sumsq = sb("c_sumsq", [P, U, 2])
    inv_mag = sb("c_inv_mag", [P, U, 2])
    mag_diag = sb("c_mag_diag", [P, U, 256])
    mag_row = sb("c_mag_row", [P, U, 256])
    score = sb("c_score", [P, U, 512])
    leaky = sb("c_leaky", [P, U, 512])
    masked = sb("c_masked", [P, U, 512])
    rowmax = sb("c_rowmax", [P, U, 2])
    neg_max = sb("c_neg_max", [P, U, 2])
    e = sb("c_e", [P, U, 512])
    eT = sb("c_eT", [P, U, 512])
    e_sum = sb("c_e_sum", [P, U, 2])
    inv_sum = sb("c_inv_sum", [P, U, 2])
    h = sb("c_h", [P, U, 256])
    h_neg = sb("c_h_neg", [P, U, 256])
    h_exp = sb("c_h_exp", [P, U, 256])
    h_elu1 = sb("c_h_elu1", [P, U, 256])
    W_a = sb("c_W_a", [P, P])
    bias = sb("c_bias", [P, D])

    xT_ps = psum("c_xT_ps")
    xpT_ps = psum("c_xpT_ps")
    A_ps = [psum(f"c_A_ps{i}") for i in range(U)]
    mag_ps = psum("c_mag_ps")
    eT_ps = psum("c_eT_ps")
    out_ps = psum("c_out_ps")

    adj_in = [sem(f"c_adj_in{i}") for i in range(U)]
    w_in = [sem(f"c_w_in{i}") for i in range(2)]
    names = ("stats_done meanvar_done var_eps_done rstd_done neg_mean_done xln_done xln_kept x_turned xT_done xp_summed "
             "xpT_done A_summed sumsq_done inv_mag_done mag_diag_done mag_spread mag_row_done score_done leaky_done "
             "penalty_done masked_done neg_max_done exp_done e_turned eT_done inv_sum_done "
             "out_summed h_done h_neg_done h_exp_done elu1_done x_done").split()
    s = Shared()
    (s.stats_done, s.meanvar_done, s.var_eps_done, s.rstd_done, s.neg_mean_done, s.xln_done, s.xln_kept, s.x_turned,
     s.xT_done, s.xp_summed, s.xpT_done, s.A_summed, s.sumsq_done, s.inv_mag_done, s.mag_diag_done, s.mag_spread,
     s.mag_row_done, s.score_done, s.leaky_done, s.penalty_done, s.masked_done, s.neg_max_done,
     s.exp_done, s.e_turned, s.eT_done, s.inv_sum_done, s.out_summed, s.h_done, s.h_neg_done, s.h_exp_done,
     s.elu1_done, s.x_done) = [sem("c_" + name) for name in names]

    adj_rows = adj_dram.rearrange("b (h p) m -> b p h m", p=P)

    lag = dict(gather=0, combine=1, stats=1, rstd=2, neg_mean=2, xln=2, x_turn=2, xT=2, xln_kept=3, xp=3, xpT=3,
               A=3, sumsq=3, inv_mag=3, mag_diag=4, mag_spread=4, mag_row=4, score=4, leaky=4, adj_load=3, penalty=5,
               masked=5, neg_max=5, exp=6, e_turn=7, eT=7, inv_sum=7, out=7, h=8, h_neg=8, h_exp=9, elu1=9, x=9,
               gate_stats=11, gate_rstd=12, gate_neg_mean=13, gate_xln=13, gate_turn=14, gate_xT=14, gate_sum=15,
               logits=15)
    DEPTH = max(lag.values())

    def at(i, u, part):
        return Item(i, u, lag[part], U, B)

    with nc.Block() as block:

        @block.sync
        def _(sp):
            sp.dma_start(W_a[:], w["L1_gnn_W_a"]).then_inc(w_in[0], 16)
            sp.dma_start(bias[:], w["L1_gnn_bias"].partition_broadcast(P)
                         .rearrange("p a d -> p (a d)")).then_inc(w_in[1], 16)

            def step(i, u):
                a = at(i, u, "adj_load")
                if a.alive:
                    if a.after(2):
                        sp.wait_ge(s.penalty_done, a.n - 1)
                    sp.dma_start(adj[:, a.pair].rearrange("p (h m) -> p h m", h=2),
                                 adj_rows[bass.ds(a.n, 1)].rearrange("a p h m -> (a p) h m")
                                 ).then_inc(adj_in[a.pair], 16)
                if a.known:
                    gate.sync_weights(sp, a.n)
                gate.sync(sp, at(i, u, "gate_xln"))
            steps(sp, B, lag["gate_xln"], U, step)
            gate.sync_end(sp)

        @block.gpsimd
        def _(pool):
            def step(i, u):
                g = at(i, u, "gather")
                combine.pool_stage(pool, g)
                b = at(i, u, "rstd")
                if b.alive:
                    if b.after(2):
                        pool.wait_ge(s.xln_done, b.n - 1)
                    pool.wait_ge(s.var_eps_done, b.n + 1)
                    pool.tensor_tensor(rstd[:, b.pair], var_eps[:, b.pair], c.neg_half[:, 0:2], ALU.pow
                                       ).then_inc(s.rstd_done, 1)
                gate_rstd = at(i, u, "gate_rstd")
                combine.pool_wait(pool, g, idle=not gate_rstd.alive)
                gate.pool_rstd(pool, gate_rstd)
                combine.pool_gather(pool, g)
                b = at(i, u, "inv_mag")
                if b.alive:
                    if b.after(2):
                        pool.wait_ge(s.score_done, b.n - 1)
                        pool.wait_ge(s.mag_diag_done, b.n - 1)
                    pool.wait_ge(s.sumsq_done, b.n + 1)
                    pool.tensor_tensor(inv_mag[:, b.pair], sumsq[:, b.pair], c.neg_half[:, 0:2], ALU.pow
                                       ).then_inc(s.inv_mag_done, 1)
            steps(pool, B, lag["gate_rstd"], U, step)

        @block.tensor
        def _(pe):
            pe.wait_ge(w_in[0], 16)

            def step(i, u):
                gate.tensor_scores(pe, at(i, u, "gate_sum"))
                b = at(i, u, "e_turn")
                if b.alive:
                    pe.wait_ge(s.exp_done, 2 * b.n + 2)
                    if b.after(1):
                        pe.wait_ge(s.eT_done, b.n)
                    for m in range(2):
                        for k in range(2):
                            mm = pe.transpose(eT_ps[:, 256 * m + P * k:256 * m + P * k + P],
                                              e[:, b.pair, 256 * k + P * m:256 * k + P * m + P], c.ident[:])
                    mm.then_inc(s.e_turned, 1)
                b = at(i, u, "xp")
                if b.alive:
                    pe.wait_ge(s.xT_done, b.n + 1)
                    if b.after(1):
                        pe.wait_ge(s.xpT_done, b.n)
                    pe.matmul(xpT_ps[:, 0:256], W_a[:], xT[:, b.pair], start=True, stop=True).then_inc(s.xp_summed, 1)
                gate.tensor_turn(pe, at(i, u, "gate_turn"))
                b = at(i, u, "mag_spread")
                if b.alive:
                    pe.wait_ge(s.mag_diag_done, b.n + 1)
                    if b.after(1):
                        pe.wait_ge(s.mag_row_done, b.n)
                    pe.matmul(mag_ps[:, 0:256], c.ones[:], mag_diag[:, b.pair], start=True, stop=True
                              ).then_inc(s.mag_spread, 1)
                b = at(i, u, "A")
                if b.alive:
                    pe.wait_ge(s.xpT_done, b.n + 1)
                    if b.after(2):
                        pe.wait_ge(s.score_done, b.n - 1)
                    for k in range(2):
                        mm = pe.matmul(A_ps[b.pair][:, 256 * k:256 * k + 256], xpT[:, b.pair, P * k:P * k + P],
                                       xpT[:, b.pair], start=True, stop=True)
                    mm.then_inc(s.A_summed, 1)
                b = at(i, u, "out")
                if b.alive:
                    pe.wait_ge(s.eT_done, b.n + 1)
                    pe.wait_ge(s.xln_kept, b.n + 1)
                    if b.after(1):
                        pe.wait_ge(s.h_done, b.n)
                    for k in range(2):
                        for m in range(2):
                            mm = pe.matmul(out_ps[:, P * k:P * k + P], eT[:, b.pair, 256 * m + P * k:256 * m + P * k + P],
                                           tiles(xln_all, b.n, 2)[:, m], start=(m == 0), stop=(m == 1))
                    mm.then_inc(s.out_summed, 1)
                b = at(i, u, "x_turn")
                if b.alive:
                    pe.wait_ge(s.xln_done, b.n + 1)
                    if b.after(1):
                        pe.wait_ge(s.xT_done, b.n)
                    for k in range(2):
                        mm = pe.transpose(xT_ps[:, P * k:P * k + P], xln[:, b.pair, k], c.ident[:])
                    mm.then_inc(s.x_turned, 1)
            steps(pe, B, DEPTH, U, step)

        @block.scalar
        def _(act):
            def step(i, u):
                b = at(i, u, "h_exp")
                if b.alive:
                    act.wait_ge(s.h_neg_done, b.n + 1)
                    if b.after(2):
                        act.wait_ge(s.elu1_done, b.n - 1)
                    act.activation(h_exp[:, b.pair], h_neg[:, b.pair], ACT.Exp).then_inc(s.h_exp_done, 1)
                b = at(i, u, "mag_diag")
                if b.alive:
                    act.wait_ge(s.inv_mag_done, b.n + 1)
                    if b.after(2):
                        act.wait_ge(s.mag_spread, b.n - 1)
                    for k in range(2):
                        op = act.activation(mag_diag[:, b.pair, P * k:P * k + P], c.ident[:], ACT.Copy,
                                            scale=inv_mag[:, b.pair, k:k + 1])
                    op.then_inc(s.mag_diag_done, 1)
                b = at(i, u, "xln_kept")
                if b.alive:
                    act.wait_ge(s.xln_done, b.n + 1)
                    act.copy(tiles(xln_all, b.n, 2), xln[:, b.pair]).then_inc(s.xln_kept, 1)
                b = at(i, u, "xpT")
                if b.alive:
                    act.wait_ge(s.xp_summed, b.n + 1)
                    if b.after(2):
                        act.wait_ge(s.A_summed, b.n - 1)
                    act.copy(xpT[:, b.pair], xpT_ps[:, 0:256]).then_inc(s.xpT_done, 1)
                b = at(i, u, "eT")
                if b.alive:
                    act.wait_ge(s.e_turned, b.n + 1)
                    if b.after(2):
                        act.wait_ge(s.out_summed, b.n - 1)
                    act.copy(eT[:, b.pair], eT_ps[:]).then_inc(s.eT_done, 1)
                gate.scalar_copy(act, at(i, u, "gate_xT"))
                b = at(i, u, "exp")
                if b.alive:
                    act.wait_ge(s.neg_max_done, b.n + 1)
                    if b.after(2):
                        act.wait_ge(s.e_turned, b.n - 1)
                        act.wait_ge(s.inv_sum_done, b.n - 1)
                    for k in range(2):
                        act.activation(e[:, b.pair, 256 * k:256 * k + 256], masked[:, b.pair, 256 * k:256 * k + 256],
                                       ACT.Exp, bias=neg_max[:, b.pair, k:k + 1],
                                       accum_out=e_sum[:, b.pair, k:k + 1]).then_inc(s.exp_done, 1)
                b = at(i, u, "mag_row")
                if b.alive:
                    act.wait_ge(s.mag_spread, b.n + 1)
                    if b.after(2):
                        act.wait_ge(s.score_done, b.n - 1)
                    act.copy(mag_row[:, b.pair], mag_ps[:, 0:256]).then_inc(s.mag_row_done, 1)
                b = at(i, u, "xln")
                if b.alive:
                    act.wait_ge(s.neg_mean_done, b.n + 1)
                    if b.after(2):
                        act.wait_ge(s.x_turned, b.n - 1)
                        act.wait_ge(s.xln_kept, b.n - 1)
                    for k in range(2):
                        op = act.activation(xln[:, b.pair, k], tiles(xs, b.n, 2)[:, k], ACT.Identity,
                                            bias=neg_mean[:, b.pair, k:k + 1], scale=rstd[:, b.pair, k:k + 1])
                    op.then_inc(s.xln_done, 1)
                b = at(i, u, "sumsq")
                if b.alive:
                    act.wait_ge(s.A_summed, b.n + 1)
                    if b.after(2):
                        act.wait_ge(s.inv_mag_done, b.n - 1)
                    for k in range(2):
                        op = act.activation(squares[:, b.pair, 256 * k:256 * k + 256],
                                            A_ps[b.pair][:, 256 * k:256 * k + 256], ACT.Square,
                                            accum_out=sumsq[:, b.pair, k:k + 1])
                    op.then_inc(s.sumsq_done, 1)
                gate.scalar_norm(act, at(i, u, "gate_xln"))
                b = at(i, u, "xT")
                if b.alive:
                    act.wait_ge(s.x_turned, b.n + 1)
                    if b.after(2):
                        act.wait_ge(s.xp_summed, b.n - 1)
                    act.copy(xT[:, b.pair], xT_ps[:, 0:256]).then_inc(s.xT_done, 1)
            steps(act, B, lag["gate_xT"], U, step)

        @block.vector
        def _(dve):
            def step(i, u):
                f = at(i, u, "stats")
                gate_stats = at(i, u, "gate_stats")
                gate.vector_add(dve, at(i, u, "logits"))
                gate.vector_wait(dve, gate_stats, s.x_done)
                b = at(i, u, "h")
                if b.alive:
                    if b.known and b.n == 0:
                        dve.wait_ge(w_in[1], 16)
                    dve.wait_ge(s.out_summed, b.n + 1)
                    dve.wait_ge(s.inv_sum_done, b.n + 1)
                    if b.after(2):
                        dve.wait_ge(s.elu1_done, b.n - 1)
                    for k in range(2):
                        op = dve.scalar_tensor_tensor(h[:, b.pair, P * k:P * k + P], out_ps[:, P * k:P * k + P],
                                                      inv_sum[:, b.pair, k:k + 1], bias[:], ALU.mult, ALU.add)
                    op.then_inc(s.h_done, 1)
                gate.vector_stats(dve, gate_stats)
                b = at(i, u, "penalty")
                if b.alive:
                    dve.wait_ge(adj_in[b.pair], (b.round + 1) * 16)
                    dve.tensor_scalar(penalty[:, b.pair], adj[:, b.pair], 0.0, MASKED, ALU.is_le, ALU.mult
                                      ).then_inc(s.penalty_done, 1)
                gate.vector_neg_mean(dve, at(i, u, "gate_neg_mean"))
                b = at(i, u, "masked")
                if b.alive:
                    dve.wait_ge(s.leaky_done, b.n + 1)
                    dve.wait_ge(s.penalty_done, b.n + 1)
                    if b.after(2):
                        dve.wait_ge(s.exp_done, 2 * b.n - 2)
                b = at(i, u, "inv_sum")
                if b.alive:
                    dve.wait_ge(s.exp_done, 2 * b.n + 2)
                    dve.reciprocal(inv_sum[:, b.pair], e_sum[:, b.pair]).then_inc(s.inv_sum_done, 1)
                b = at(i, u, "masked")
                if b.alive:
                    for k in range(2):
                        op = dve.tensor_tensor_reduce(out=masked[:, b.pair, 256 * k:256 * k + 256],
                                                      in0=leaky[:, b.pair, 256 * k:256 * k + 256],
                                                      in1=penalty[:, b.pair, 256 * k:256 * k + 256], scale=1.0,
                                                      scalar=-BIG, op0=ALU.add, op1=ALU.max,
                                                      accum_out=rowmax[:, b.pair, k:k + 1])
                    op.then_inc(s.masked_done, 1)
                if f.alive:
                    combine.vector_first(dve, f, tiles(xs, f.n, 2), tiles(xs, f.n, 2))
                if gate_stats.alive and gate_stats.after(2):
                    dve.wait_ge(gate.neg_mean_done, gate_stats.n - 1)
                b = at(i, u, "neg_mean")
                if b.alive:
                    dve.wait_ge(s.rstd_done, b.n + 1)
                    if b.after(2):
                        dve.wait_ge(s.xln_done, b.n - 1)
                    dve.scalar_tensor_tensor(neg_mean[:, b.pair], meanvar[:, b.pair, :, 0], -1.0, rstd[:, b.pair],
                                             ALU.mult, ALU.mult).then_inc(s.neg_mean_done, 1)
                gate.vector_aggregate(dve, gate_stats)
                b = at(i, u, "h_neg")
                if b.alive:
                    dve.wait_ge(s.h_done, b.n + 1)
                    if b.after(2):
                        dve.wait_ge(s.h_exp_done, b.n - 1)
                    dve.tensor_scalar(h_neg[:, b.pair], h[:, b.pair], 0.0, None, ALU.min).then_inc(s.h_neg_done, 1)
                if f.alive:
                    combine.vector_second(dve, f, tiles(xs, f.n, 2))
                b = at(i, u, "elu1")
                if b.alive:
                    dve.wait_ge(s.h_exp_done, b.n + 1)
                    dve.scalar_tensor_tensor(h_elu1[:, b.pair], h[:, b.pair], 0.0, h_exp[:, b.pair], ALU.max, ALU.add
                                             ).then_inc(s.elu1_done, 1)
                if f.alive:
                    dve.wait_ge(combine.x_done, f.n + 1)
                b = at(i, u, "neg_max")
                if b.alive:
                    dve.wait_ge(s.masked_done, b.n + 1)
                    dve.tensor_scalar(neg_max[:, b.pair], rowmax[:, b.pair], -1.0, None, ALU.mult
                                      ).then_inc(s.neg_max_done, 1)
                if f.alive:
                    for k in range(2):
                        op = dve.bn_stats(stats[:, f.pair, k], tiles(xs, f.n, 2)[:, k])
                    op.then_inc(s.stats_done, 1)
                    dve.wait_ge(s.stats_done, f.n + 1)
                b = at(i, u, "score")
                if b.alive:
                    dve.wait_ge(s.mag_row_done, b.n + 1)
                    if b.after(2):
                        dve.wait_ge(s.leaky_done, b.n - 1)
                    for k in range(2):
                        op = dve.scalar_tensor_tensor(score[:, b.pair, 256 * k:256 * k + 256],
                                                      A_ps[b.pair][:, 256 * k:256 * k + 256],
                                                      inv_mag[:, b.pair, k:k + 1], mag_row[:, b.pair],
                                                      ALU.mult, ALU.mult)
                    op.then_inc(s.score_done, 1)
                if f.alive and f.after(2):
                    dve.wait_ge(s.neg_mean_done, f.n - 1)
                b = at(i, u, "x")
                if b.alive:
                    dve.wait_ge(s.elu1_done, b.n + 1)
                    dve.scalar_tensor_tensor(tiles(xs, b.n, 2), h_elu1[:, b.pair].rearrange("p (k d) -> p k d", k=2),
                                             -1.0, tiles(xs, b.n, 2), ALU.add, ALU.add).then_inc(s.x_done, 1)
                if f.alive:
                    for k in range(2):
                        op = dve.bn_aggr(meanvar[:, f.pair, k], stats[:, f.pair, k])
                    op.then_inc(s.meanvar_done, 1)
                gate.vector_var_eps(dve, gate_stats)
                if f.alive:
                    dve.wait_ge(s.meanvar_done, f.n + 1)
                    if f.after(2):
                        dve.wait_ge(s.rstd_done, f.n - 1)
                    dve.tensor_scalar(var_eps[:, f.pair], meanvar[:, f.pair, :, 1], LN_EPS, None, ALU.add
                                      ).then_inc(s.var_eps_done, 1)
                b = at(i, u, "leaky")
                if b.alive:
                    dve.wait_ge(s.score_done, b.n + 1)
                    dve.scalar_tensor_tensor(leaky[:, b.pair], score[:, b.pair], NEG_SLOPE, score[:, b.pair],
                                             ALU.mult, ALU.max).then_inc(s.leaky_done, 1)
            steps(dve, B, DEPTH, U, step)
            gate.vector_end(dve)


def last_norm(nc, sem, sb, c, w, xs, xln_dram, combine, out_dram, B):
    U = 2
    xln = sb("l_xln", [P, U, 2, D])
    moe = sb("l_moe", [P, U, 2, D])
    stats = sb("l_stats", [P, U, 2, 6])
    meanvar = sb("l_meanvar", [P, U, 2, 2])
    var_eps = sb("l_var_eps", [P, U, 2])
    rstd = sb("l_rstd", [P, U, 2])
    normed = sb("l_normed", [P, U, 2, D])
    scaled = sb("l_scaled", [P, U, 2, D])
    x_beta = sb("l_x_beta", [P, U, 2, D])
    result = sb("l_result", [P, U, 2, D])
    gamma = sb("l_gamma", [P, 2, D])
    beta = sb("l_beta", [P, 2, D])
    w_in = [sem(f"l_w_in{k}") for k in range(4)]
    xln_in = [sem(f"l_xln_in{k}") for k in range(U)]
    out_stored = [sem(f"l_out_stored{k}") for k in range(U)]
    stats_done = sem("l_stats_done")
    meanvar_done = sem("l_meanvar_done")
    var_eps_done = sem("l_var_eps_done")
    rstd_done = sem("l_rstd_done")
    normed_done = sem("l_normed_done")
    scaled_done = sem("l_scaled_done")
    x_beta_done = sem("l_x_beta_done")
    result_done = sem("l_result_done")

    with nc.Block() as block:

        @block.sync
        def _(sp):
            for k in range(2):
                sp.dma_start(gamma[:, k], w["L1_ffn_gamma"].partition_broadcast(P)).then_inc(w_in[k], 16)
                sp.dma_start(beta[:, k], w["L1_ffn_beta"].partition_broadcast(P)).then_inc(w_in[2 + k], 16)

            def step(i, u):
                g = Item(i, u, 0, U, B)
                if g.alive:
                    if g.after(2):
                        sp.wait_ge(combine.x_done, g.n - 1)
                    sp.dma_start(xln[:, g.pair], rows(xln_dram, g.n, 2)).then_inc(xln_in[g.pair], 16)
                o = Item(i, u, 3, U, B)
                if o.alive:
                    sp.wait_ge(result_done, o.n + 1)
                    sp.dma_start(rows(out_dram, o.n, 2), result[:, o.pair]).then_inc(out_stored[o.pair], 16)
            steps(sp, B, 3, U, step)
            for k in range(U):
                sp.wait_ge(out_stored[k], B // U * 16)

        @block.gpsimd
        def _(pool):
            def step(i, u):
                g = Item(i, u, 0, U, B)
                f = Item(i, u, 2, U, B)
                combine.pool_stage(pool, g)
                if f.alive:
                    if f.after(2):
                        pool.wait_ge(normed_done, f.n - 1)
                    pool.wait_ge(var_eps_done, f.n + 1)
                combine.pool_wait(pool, g, idle=not f.alive)
                if f.alive:
                    pool.tensor_tensor(rstd[:, f.pair], var_eps[:, f.pair], c.neg_half[:, 0:2], ALU.pow
                                       ).then_inc(rstd_done, 1)
                combine.pool_gather(pool, g)
            steps(pool, B, 2, U, step)

        @block.vector
        def _(dve):
            for k in range(4):
                dve.wait_ge(w_in[k], 16)

            def step(i, u):
                f = Item(i, u, 1, U, B)
                b = Item(i, u, 2, U, B)
                o = Item(i, u, 3, U, B)
                if o.alive:
                    dve.wait_ge(normed_done, o.n + 1)
                    dve.tensor_tensor(scaled[:, o.pair], normed[:, o.pair], gamma[:], ALU.mult).then_inc(scaled_done, 1)
                if f.alive:
                    dve.wait_ge(xln_in[f.pair], (f.round + 1) * 16)
                    if f.after(2):
                        dve.wait_ge(normed_done, f.n - 1)
                    combine.vector_first(dve, f, xln[:, f.pair], moe[:, f.pair])
                if o.alive:
                    dve.tensor_tensor(x_beta[:, o.pair], tiles(xs, o.n, 2), beta[:], ALU.add).then_inc(x_beta_done, 1)
                if f.alive:
                    combine.vector_second(dve, f, moe[:, f.pair])
                    dve.wait_ge(combine.x_done, f.n + 1)
                if b.alive:
                    dve.wait_ge(rstd_done, b.n + 1)
                    if b.after(2):
                        dve.wait_ge(scaled_done, b.n - 1)
                    for k in range(2):
                        op = dve.tensor_scalar(normed[:, b.pair, k], moe[:, b.pair, k], meanvar[:, b.pair, k, 0:1],
                                               rstd[:, b.pair, k:k + 1], ALU.subtract, ALU.mult)
                    op.then_inc(normed_done, 1)
                if f.alive:
                    for k in range(2):
                        op = dve.bn_stats(stats[:, f.pair, k], moe[:, f.pair, k])
                    op.then_inc(stats_done, 1)
                    dve.wait_ge(stats_done, f.n + 1)
                if o.alive:
                    if o.after(2):
                        dve.wait_ge(out_stored[o.pair], o.round * 16)
                    dve.wait_ge(scaled_done, o.n + 1)
                    dve.wait_ge(x_beta_done, o.n + 1)
                    dve.tensor_tensor(result[:, o.pair], scaled[:, o.pair], x_beta[:, o.pair], ALU.add
                                      ).then_inc(result_done, 1)
                if f.alive:
                    for k in range(2):
                        op = dve.bn_aggr(meanvar[:, f.pair, k], stats[:, f.pair, k])
                    op.then_inc(meanvar_done, 1)
                    dve.wait_ge(meanvar_done, f.n + 1)
                    if f.after(2):
                        dve.wait_ge(rstd_done, f.n - 1)
                    dve.tensor_scalar(var_eps[:, f.pair], meanvar[:, f.pair, :, 1], LN_EPS, None, ALU.add
                                      ).then_inc(var_eps_done, 1)
            steps(dve, B, 3, U, step)


@contextmanager
def phase(nc):
    with ExitStack() as own:
        sems = []

        def sem(name):
            sems.append(nc.alloc_semaphore(name=name))
            return sems[-1]

        def sb(name, shape, dt=F32):
            return own.enter_context(nc.sbuf_tensor(name, shape, dt))

        def psum(name):
            return own.enter_context(nc.psum_tensor(name, [P, 512], F32))

        yield sem, sb, psum
    nc.clear_and_free_semaphores(sems)
    nc.all_engine_barrier()


class Shared:
    pass


def program(nc, w, out, scratch):
    B, N, _ = w["x"].shape
    x_dram = w["x"].rearrange("b n d -> (b n) d")
    out_dram = out.rearrange("b n d -> (b n) d")
    T = B * N // P
    c = Shared()
    with ExitStack() as ctx:
        def keep(name, shape, dt=F32):
            return ctx.enter_context(nc.sbuf_tensor(name, shape, dt))

        xs = keep("xs", [P, T, D])
        c.W1 = keep("experts_W1", [P, 4096])
        c.W2 = keep("experts_W2", [P, 4096])
        c.b1 = keep("experts_b1", [P, 32])
        c.b2 = keep("experts_b2", [P, 2048])
        with phase(nc) as (sem, sb, psum):
            constants(nc, sem, keep, sb, psum, c, w)

        logits = keep("logits", [P, T, 16])
        xln_dram = scratch["xln"]

        def gate_and_experts(names):
            E = w[names[0]].shape[1]
            return E, w[names[2]].shape[2], logits[:].rearrange("p t e -> p (t e)")[:, 0:T * E].rearrange(
                "p (t e) -> p t e", e=E)

        def routed(pre, E, F, logits, gelu):
            NT = expert_tiles(T, E)
            r = Shared()
            r.weight = keep(pre + "weight", [P, T, 2])
            r.slot = keep(pre + "slot", [P, T, 2], I32)
            r.expert = keep(pre + "expert", [P, NT + 16], I32)
            r.token = keep(pre + "token", [P, NT + 1], I32)
            with phase(nc) as (sem, sb, psum):
                route(nc, sem, sb, psum, c, pre + "r_", logits, r, T, E)
            with phase(nc) as (sem, sb, psum):
                run_experts(nc, sem, sb, psum, c, pre + "e_", xln_dram, scratch[pre + "y"], r, T, E, F, gelu)
            return r

        names = ["L0_ffn_Wg", "L0_ffn_bg", "L0_ffn_W1", "L0_ffn_b1", "L0_ffn_W2", "L0_ffn_b2"]
        E, F, scores = gate_and_experts(names)
        with phase(nc) as (sem, sb, psum):
            gate = GateScores(sem, sb, psum, c, w, "ag_", xs, xln_dram, scores, names, B, E, F)
            gnn_mlp_layer(nc, sem, sb, psum, c, x_dram, w["adj"], xs, B, gate)
        r = routed("b_", E, F, scores, True)

        names = ["L1_ffn_gate_w", "L1_ffn_gate_b", "L1_ffn_w1", "L1_ffn_b1", "L1_ffn_w2", "L1_ffn_b2"]
        E, F, scores = gate_and_experts(names)
        with phase(nc) as (sem, sb, psum):
            combine = Combine(sem, sb, c, "cc_", r, scratch["b_y"], B)
            gate = GateScores(sem, sb, psum, c, w, "cg_", xs, xln_dram, scores, names, B, E, F)
            graph_attention_layer(nc, sem, sb, psum, c, w, w["adj"], xs, B, combine, gate)
        r = routed("d_", E, F, scores, False)
        with phase(nc) as (sem, sb, psum):
            combine = Combine(sem, sb, c, "lc_", r, scratch["d_y"], B)
            last_norm(nc, sem, sb, c, w, xs, xln_dram, combine, out_dram, B)


_INS = ["x", "adj", "L0_gnn_epsilon", "L0_gnn_W1", "L0_gnn_b1", "L0_gnn_rms_weight", "L0_gnn_W2", "L0_gnn_b2",
        "L0_ffn_Wg", "L0_ffn_bg", "L0_ffn_W1", "L0_ffn_b1", "L0_ffn_W2", "L0_ffn_b2", "L1_gnn_W_a", "L1_gnn_bias",
        "L1_ffn_gate_w", "L1_ffn_gate_b", "L1_ffn_w1", "L1_ffn_b1", "L1_ffn_w2", "L1_ffn_b2", "L1_ffn_gamma",
        "L1_ffn_beta"]


def kernel(**inputs):
    import numpy as _np
    import concourse.bacc as _bacc
    from concourse.bass_utils import run_bass_kernel_spmd as _run

    nc = _bacc.Bacc("TRN2", target_bir_lowering=False, num_devices=1)
    arrays, args = {}, {}
    for name in _INS:
        a = _np.ascontiguousarray(inputs[name])
        if name == "L0_gnn_epsilon":
            a = a.reshape(1)
        arrays[f"in_{name}"] = a
        args[name] = nc.dram_tensor(f"in_{name}", a.shape, mybir.dt.from_np(a.dtype), kind="ExternalInput").ap()
    out = nc.dram_tensor("out_x", inputs["x"].shape, F32, kind="ExternalOutput").ap()
    tokens = inputs["x"].shape[0] * inputs["x"].shape[1]
    scratch = {"xln": nc.dram_tensor("xln_rows", [tokens, D], F32).ap()}
    for layer, gate in (("b_", "L0_ffn_Wg"), ("d_", "L1_ffn_gate_w")):
        slots = expert_tiles(tokens // P, inputs[gate].shape[1]) * P
        scratch[layer + "y"] = nc.dram_tensor(layer + "y_rows", [slots, D], F32).ap()
    program(nc, args, out, scratch)
    r = _run(nc, [arrays], core_ids=[0])
    return r.results[0]["out_x"]
```
